# Optimizing a Trainium2 kernel written in Bass

```python
import numpy as np
import jax
import jax.numpy as jnp

def _softmax(x, axis=-1):
    return jax.nn.softmax(x, axis=axis)

def _gelu(x):
    return jax.nn.gelu(x, approximate=True)

def _silu(x):
    return jax.nn.silu(x)

def _sigmoid(x):
    return jax.nn.sigmoid(x)

def _layernorm(x, axis=-1, eps=1e-05):
    m = jnp.mean(x, axis=axis, keepdims=True)
    v = jnp.var(x, axis=axis, keepdims=True)
    return (x - m) / jnp.sqrt(v + eps)

def _scatter_add(tgt, idx, src, axis=0):
    return tgt.at[idx].add(src)

def _segment_sum(src, seg, n):
    return jax.ops.segment_sum(src, seg, n)
kernel_name = 'mk_hybrid_d1_jaxref_r8_9d83a1'

def setup_inputs(seed: int=0):
    np.random.seed(seed)
    _w = jnp.asarray

    def _L0_attn_a_setup():
        import jax, jax.numpy as jnp
        import numpy as np
        D_MODEL = 128
        N_HEADS = 16
        HEAD_DIM = D_MODEL // N_HEADS
        D_LATENT = 32
        LAMBDA_DECAY = 0.01
        TIME_STEP = 0.01
        CLAMP = 10000.0

        def _reference_tuple_inner(x, Wq, Wk, Wv, Wo, W_down_kv, W_up_k, W_up_v):
            B, S, _ = x.shape
            q = x @ Wq
            k = x @ Wk
            v = x @ Wv
            latent_kv = (k + v) @ W_down_kv
            k_rec = latent_kv @ W_up_k
            v_rec = latent_kv @ W_up_v

            def heads(t):
                return t.reshape(B, S, N_HEADS, HEAD_DIM).transpose(0, 2, 1, 3)
            qh, kh, vh = (heads(q), heads(k_rec), heads(v_rec))
            scale = 1.0 / (jnp.sqrt(jnp.float32(D_MODEL)) + 1e-08)
            scores = jnp.einsum('bhqd,bhkd->bhqk', qh, kh) * scale
            scores = jnp.clip(jnp.nan_to_num(scores, nan=-1000000000.0), -CLAMP, CLAMP)
            idx = jnp.arange(S, dtype=jnp.float32)
            decay = jnp.exp(-LAMBDA_DECAY * TIME_STEP * jnp.abs(idx[:, None] - idx[None, :]))
            scores = scores * decay[None, None, :, :]
            scores = jnp.clip(jnp.nan_to_num(scores, nan=-1000000000.0), -CLAMP, CLAMP)
            attn = jax.nn.softmax(scores, axis=-1)
            out = jnp.einsum('bhqk,bhkd->bhqd', attn, vh)
            out = out.transpose(0, 2, 1, 3).reshape(B, S, D_MODEL)
            return (out @ Wo, latent_kv)
        key = jax.random.key(seed)
        ks = jax.random.split(key, 8)
        B, S = (2, 256)

        def w(k, i, o):
            return jax.random.normal(k, (i, o), dtype=jnp.float32) * 0.02
        return {'x': jax.random.normal(ks[0], (B, S, D_MODEL), dtype=jnp.float32), 'Wq': w(ks[1], D_MODEL, D_MODEL), 'Wk': w(ks[2], D_MODEL, D_MODEL), 'Wv': w(ks[3], D_MODEL, D_MODEL), 'Wo': w(ks[4], D_MODEL, D_MODEL), 'W_down_kv': w(ks[5], D_MODEL, D_LATENT), 'W_up_k': w(ks[6], D_LATENT, D_MODEL), 'W_up_v': w(ks[7], D_LATENT, D_MODEL)}
    _L0_attn_a_in = _L0_attn_a_setup()

    def _L0_attn_b_setup():
        import jax, jax.numpy as jnp
        import numpy as np
        from jax import lax
        D_MODEL = 128
        D_INNER = 256
        D_STATE = 16
        D_CONV = 4
        DT_RANK = 64
        N_LAYERS = 1
        EPS = 1e-05

        def _selective_scan(u, delta, A, B, C, Dp):

            def step(h, xs):
                d_t, B_t, C_t, u_t = xs
                dA = jnp.exp(d_t[..., None] * A)
                dBu = d_t[..., None] * B_t[:, None, :] * u_t[..., None]
                h = dA * h + dBu
                y_t = jnp.einsum('bdn,bn->bd', h, C_t)
                return (h, y_t)
            b = u.shape[0]
            h0 = jnp.zeros((b, D_INNER, D_STATE), u.dtype)
            xs = (delta.transpose(1, 0, 2), B.transpose(1, 0, 2), C.transpose(1, 0, 2), u.transpose(1, 0, 2))
            _, ys = lax.scan(step, h0, xs)
            y = ys.transpose(1, 0, 2)
            return y + u * Dp

        def _mamba_block(x, in_proj_w, conv_w, conv_b, x_proj_w, dt_proj_w, dt_proj_b, A_log, Dp, out_proj_w):
            b, l, _ = x.shape
            xz = x @ in_proj_w.T
            xm, res = jnp.split(xz, 2, axis=-1)
            xm_bdl = xm.transpose(0, 2, 1)
            conv = lax.conv_general_dilated(xm_bdl, conv_w, window_strides=(1,), padding=[(D_CONV - 1, 0)], feature_group_count=D_INNER, dimension_numbers=('NCH', 'OIH', 'NCH'))
            xm = jax.nn.silu((conv + conv_b[None, :, None]).transpose(0, 2, 1))
            x_dbl = xm @ x_proj_w.T
            dt, Bm, Cm = jnp.split(x_dbl, [DT_RANK, DT_RANK + D_STATE], axis=-1)
            delta = jax.nn.softplus(dt @ dt_proj_w.T + dt_proj_b)
            A = -jnp.exp(A_log)
            y = _selective_scan(xm, delta, A, Bm, Cm, Dp)
            y = y * jax.nn.silu(res)
            return y @ out_proj_w.T
        key = jax.random.key(seed)
        ks = jax.random.split(key, 16)
        s = lambda fan_in: 1.0 / np.sqrt(fan_in)
        inp = {'seq_embeddings': jax.random.normal(ks[0], (8, 128, D_MODEL), jnp.float32), 'in_proj_w': jax.random.normal(ks[1], (2 * D_INNER, D_MODEL), jnp.float32) * s(D_MODEL), 'conv_w': jax.random.normal(ks[2], (D_INNER, 1, D_CONV), jnp.float32) * s(D_CONV), 'conv_b': jax.random.normal(ks[3], (D_INNER,), jnp.float32) * 0.01, 'x_proj_w': jax.random.normal(ks[4], (DT_RANK + 2 * D_STATE, D_INNER), jnp.float32) * s(D_INNER), 'dt_proj_w': jax.random.normal(ks[5], (D_INNER, DT_RANK), jnp.float32) * s(DT_RANK), 'dt_proj_b': jax.random.normal(ks[6], (D_INNER,), jnp.float32) * 0.01, 'A_log': jnp.log(jnp.tile(jnp.arange(1.0, D_STATE + 1.0, dtype=jnp.float32), (D_INNER, 1))), 'D': jnp.ones((D_INNER,), jnp.float32), 'out_proj_w': jax.random.normal(ks[7], (D_MODEL, D_INNER), jnp.float32) * s(D_INNER), 'ffn_w1': jax.random.normal(ks[8], (4 * D_MODEL, D_MODEL), jnp.float32) * s(D_MODEL), 'ffn_b1': jnp.zeros((4 * D_MODEL,), jnp.float32), 'ffn_w2': jax.random.normal(ks[9], (D_MODEL, 4 * D_MODEL), jnp.float32) * s(4 * D_MODEL), 'ffn_b2': jnp.zeros((D_MODEL,), jnp.float32)}
        return inp
    _L0_attn_b_in = _L0_attn_b_setup()

    def _L0_ffn_setup():
        import jax, jax.numpy as jnp
        import numpy as np
        B, S, D, H, E = (4, 256, 128, 512, 8)
        key = jax.random.key(seed)
        ks = jax.random.split(key, 8)
        s_d = 1.0 / np.sqrt(D)
        s_h = 1.0 / np.sqrt(H)
        return {'x': jax.random.normal(ks[0], (B, S, D), dtype=jnp.float32), 'gate_w': jax.random.uniform(ks[1], (E, D), jnp.float32, -s_d, s_d), 'gate_b': jax.random.uniform(ks[2], (E,), jnp.float32, -s_d, s_d), 'w1': jax.random.uniform(ks[3], (E, H, D), jnp.float32, -s_d, s_d), 'b1': jax.random.uniform(ks[4], (E, H), jnp.float32, -s_d, s_d), 'w2': jax.random.uniform(ks[5], (E, D, H), jnp.float32, -s_h, s_h), 'b2': jax.random.uniform(ks[6], (E, D), jnp.float32, -s_h, s_h)}
    _L0_ffn_in = _L0_ffn_setup()
    _d = {'L0_attn_a_x': _L0_attn_a_in['x'], 'L0_attn_a_Wq': _L0_attn_a_in['Wq'], 'L0_attn_a_Wk': _L0_attn_a_in['Wk'], 'L0_attn_a_Wv': _L0_attn_a_in['Wv'], 'L0_attn_a_Wo': _L0_attn_a_in['Wo'], 'L0_attn_a_W_down_kv': _L0_attn_a_in['W_down_kv'], 'L0_attn_a_W_up_k': _L0_attn_a_in['W_up_k'], 'L0_attn_a_W_up_v': _L0_attn_a_in['W_up_v'], 'L0_attn_b_in_proj_w': _L0_attn_b_in['in_proj_w'], 'L0_attn_b_conv_w': _L0_attn_b_in['conv_w'], 'L0_attn_b_conv_b': _L0_attn_b_in['conv_b'], 'L0_attn_b_x_proj_w': _L0_attn_b_in['x_proj_w'], 'L0_attn_b_dt_proj_w': _L0_attn_b_in['dt_proj_w'], 'L0_attn_b_dt_proj_b': _L0_attn_b_in['dt_proj_b'], 'L0_attn_b_A_log': _L0_attn_b_in['A_log'], 'L0_attn_b_D': _L0_attn_b_in['D'], 'L0_attn_b_out_proj_w': _L0_attn_b_in['out_proj_w'], 'L0_attn_b_ffn_w1': _L0_attn_b_in['ffn_w1'], 'L0_attn_b_ffn_b1': _L0_attn_b_in['ffn_b1'], 'L0_attn_b_ffn_w2': _L0_attn_b_in['ffn_w2'], 'L0_attn_b_ffn_b2': _L0_attn_b_in['ffn_b2'], 'L0_ffn_gate_w': _L0_ffn_in['gate_w'], 'L0_ffn_gate_b': _L0_ffn_in['gate_b'], 'L0_ffn_w1': _L0_ffn_in['w1'], 'L0_ffn_b1': _L0_ffn_in['b1'], 'L0_ffn_w2': _L0_ffn_in['w2'], 'L0_ffn_b2': _L0_ffn_in['b2']}
    _x0 = _d['L0_attn_a_x']
    _d['L0_attn_a_x'] = jax.random.normal(jax.random.fold_in(jax.random.key(seed), 1), (8, 256, 128), dtype=_x0.dtype)
    del _x0
    return _d

def reference(L0_attn_a_x, L0_attn_a_Wq, L0_attn_a_Wk, L0_attn_a_Wv, L0_attn_a_Wo, L0_attn_a_W_down_kv, L0_attn_a_W_up_k, L0_attn_a_W_up_v, L0_attn_b_in_proj_w, L0_attn_b_conv_w, L0_attn_b_conv_b, L0_attn_b_x_proj_w, L0_attn_b_dt_proj_w, L0_attn_b_dt_proj_b, L0_attn_b_A_log, L0_attn_b_D, L0_attn_b_out_proj_w, L0_attn_b_ffn_w1, L0_attn_b_ffn_b1, L0_attn_b_ffn_w2, L0_attn_b_ffn_b2, L0_ffn_gate_w, L0_ffn_gate_b, L0_ffn_w1, L0_ffn_b1, L0_ffn_w2, L0_ffn_b2):

    def _L0_attn_a_ref(x, Wq, Wk, Wv, Wo, W_down_kv, W_up_k, W_up_v):
        import jax, jax.numpy as jnp
        import numpy as np
        D_MODEL = 128
        N_HEADS = 16
        HEAD_DIM = D_MODEL // N_HEADS
        D_LATENT = 32
        LAMBDA_DECAY = 0.01
        TIME_STEP = 0.01
        CLAMP = 10000.0

        def _reference_tuple_inner(x, Wq, Wk, Wv, Wo, W_down_kv, W_up_k, W_up_v):
            B, S, _ = x.shape
            q = x @ Wq
            k = x @ Wk
            v = x @ Wv
            latent_kv = (k + v) @ W_down_kv
            k_rec = latent_kv @ W_up_k
            v_rec = latent_kv @ W_up_v

            def heads(t):
                return t.reshape(B, S, N_HEADS, HEAD_DIM).transpose(0, 2, 1, 3)
            qh, kh, vh = (heads(q), heads(k_rec), heads(v_rec))
            scale = 1.0 / (jnp.sqrt(jnp.float32(D_MODEL)) + 1e-08)
            scores = jnp.einsum('bhqd,bhkd->bhqk', qh, kh) * scale
            scores = jnp.clip(jnp.nan_to_num(scores, nan=-1000000000.0), -CLAMP, CLAMP)
            idx = jnp.arange(S, dtype=jnp.float32)
            decay = jnp.exp(-LAMBDA_DECAY * TIME_STEP * jnp.abs(idx[:, None] - idx[None, :]))
            scores = scores * decay[None, None, :, :]
            scores = jnp.clip(jnp.nan_to_num(scores, nan=-1000000000.0), -CLAMP, CLAMP)
            attn = jax.nn.softmax(scores, axis=-1)
            out = jnp.einsum('bhqk,bhkd->bhqd', attn, vh)
            out = out.transpose(0, 2, 1, 3).reshape(B, S, D_MODEL)
            return (out @ Wo, latent_kv)
        return _reference_tuple_inner(x, Wq, Wk, Wv, Wo, W_down_kv, W_up_k, W_up_v)[0]

    def _L0_attn_b_ref(seq_embeddings, in_proj_w, conv_w, conv_b, x_proj_w, dt_proj_w, dt_proj_b, A_log, D, out_proj_w, ffn_w1, ffn_b1, ffn_w2, ffn_b2):
        import jax, jax.numpy as jnp
        import numpy as np
        from jax import lax
        D_MODEL = 128
        D_INNER = 256
        D_STATE = 16
        D_CONV = 4
        DT_RANK = 64
        N_LAYERS = 1
        EPS = 1e-05

        def _selective_scan(u, delta, A, B, C, Dp):

            def step(h, xs):
                d_t, B_t, C_t, u_t = xs
                dA = jnp.exp(d_t[..., None] * A)
                dBu = d_t[..., None] * B_t[:, None, :] * u_t[..., None]
                h = dA * h + dBu
                y_t = jnp.einsum('bdn,bn->bd', h, C_t)
                return (h, y_t)
            b = u.shape[0]
            h0 = jnp.zeros((b, D_INNER, D_STATE), u.dtype)
            xs = (delta.transpose(1, 0, 2), B.transpose(1, 0, 2), C.transpose(1, 0, 2), u.transpose(1, 0, 2))
            _, ys = lax.scan(step, h0, xs)
            y = ys.transpose(1, 0, 2)
            return y + u * Dp

        def _mamba_block(x, in_proj_w, conv_w, conv_b, x_proj_w, dt_proj_w, dt_proj_b, A_log, Dp, out_proj_w):
            b, l, _ = x.shape
            xz = x @ in_proj_w.T
            xm, res = jnp.split(xz, 2, axis=-1)
            xm_bdl = xm.transpose(0, 2, 1)
            conv = lax.conv_general_dilated(xm_bdl, conv_w, window_strides=(1,), padding=[(D_CONV - 1, 0)], feature_group_count=D_INNER, dimension_numbers=('NCH', 'OIH', 'NCH'))
            xm = jax.nn.silu((conv + conv_b[None, :, None]).transpose(0, 2, 1))
            x_dbl = xm @ x_proj_w.T
            dt, Bm, Cm = jnp.split(x_dbl, [DT_RANK, DT_RANK + D_STATE], axis=-1)
            delta = jax.nn.softplus(dt @ dt_proj_w.T + dt_proj_b)
            A = -jnp.exp(A_log)
            y = _selective_scan(xm, delta, A, Bm, Cm, Dp)
            y = y * jax.nn.silu(res)
            return y @ out_proj_w.T
        x = seq_embeddings
        for _ in range(N_LAYERS):
            m = _mamba_block(x, in_proj_w, conv_w, conv_b, x_proj_w, dt_proj_w, dt_proj_b, A_log, D, out_proj_w)
            f = jax.nn.gelu(m @ ffn_w1.T + ffn_b1, approximate=False) @ ffn_w2.T + ffn_b2
            c = m + f
            mu = jnp.mean(c, axis=(1, 2), keepdims=True)
            var = jnp.var(c, axis=(1, 2), keepdims=True)
            x = (c - mu) / jnp.sqrt(var + EPS)
        return x

    def _L0_ffn_ref(x, gate_w, gate_b, w1, b1, w2, b2):
        import jax, jax.numpy as jnp
        import numpy as np
        B, S, D, H, E = (4, 256, 128, 512, 8)
        b, s, d = x.shape
        xf = x.reshape(-1, d)
        logits = xf @ gate_w.T + gate_b
        top1 = jnp.argmax(logits, axis=-1)
        out = jnp.zeros_like(xf)
        n_experts = w1.shape[0]
        for e in range(n_experts):
            h = jax.nn.relu(xf @ w1[e].T + b1[e])
            y = h @ w2[e].T + b2[e]
            out = out + jnp.where((top1 == e)[:, None], y, jnp.zeros((), y.dtype))
        return out.reshape(b, s, d)
    x = L0_attn_a_x
    x = x + _L0_attn_a_ref(_layernorm(x, axis=-1), L0_attn_a_Wq, L0_attn_a_Wk, L0_attn_a_Wv, L0_attn_a_Wo, L0_attn_a_W_down_kv, L0_attn_a_W_up_k, L0_attn_a_W_up_v)
    x = x + _L0_ffn_ref(_layernorm(x, axis=-1), L0_ffn_gate_w, L0_ffn_gate_b, L0_ffn_w1, L0_ffn_b1, L0_ffn_w2, L0_ffn_b2)
    x = x + _L0_attn_b_ref(_layernorm(x, axis=-1), L0_attn_b_in_proj_w, L0_attn_b_conv_w, L0_attn_b_conv_b, L0_attn_b_x_proj_w, L0_attn_b_dt_proj_w, L0_attn_b_dt_proj_b, L0_attn_b_A_log, L0_attn_b_D, L0_attn_b_out_proj_w, L0_attn_b_ffn_w1, L0_attn_b_ffn_b1, L0_attn_b_ffn_w2, L0_attn_b_ffn_b2)
    x = x + _L0_ffn_ref(_layernorm(x, axis=-1), L0_ffn_gate_w, L0_ffn_gate_b, L0_ffn_w1, L0_ffn_b1, L0_ffn_w2, L0_ffn_b2)
    return x

_drawn_inputs = setup_inputs


def setup_inputs(seed=0):
    import zlib

    import numpy as np

    out = dict(_drawn_inputs(seed))
    spreads = {'L0_attn_b_D': (1.0, 0.2),
     'L0_attn_b_ffn_b1': (0.0, 0.307),
     'L0_attn_b_ffn_b2': (0.0, 0.1)}
    factors = {'L0_attn_a_Wq': 8.0,
     'L0_attn_a_Wk': 8.0,
     'L0_attn_a_Wv': 8.0,
     'L0_attn_a_Wo': 8.0,
     'L0_attn_a_W_down_kv': 8.0,
     'L0_attn_a_W_up_k': 8.0,
     'L0_attn_a_W_up_v': 8.0,
     'L0_attn_b_conv_b': 12.771,
     'L0_attn_b_dt_proj_b': 24.221,
     'L0_ffn_b1': 4.605,
     'L0_ffn_b2': 3.641}
    for name, (base, spread) in spreads.items():
        noise = np.random.default_rng([zlib.crc32(name.encode()), seed]).standard_normal(out[name].shape)
        drawn = base * np.exp(spread * noise) if base else spread * noise
        out[name] = jnp.asarray(drawn.astype(out[name].dtype))
    for name, factor in factors.items():
        out[name] = (out[name] * factor).astype(out[name].dtype)
    return out
```

```python
from contextlib import ExitStack

import concourse.bass as bass
from concourse import mybir

F32 = mybir.dt.float32
BF16 = mybir.dt.bfloat16
U32 = mybir.dt.uint32
BF16_ONE = 0x3F80
ALU = mybir.AluOpType
ACT = mybir.ActivationFunctionType
AX = mybir.AxisListType

P = 128
B, S = 8, 256
NTOK = B * S
NT = NTOK // P
QT = S // P
HEADS, HD = 16, 8
GROUPS, GH = 4, 4
CLAMP = 10000.0
EPS = 1e-5
BANK = 512
E_N, HID = 8, 512
HC = HID // P
SLOT_TILES = 24
DI, NS, DTR = 256, 16, 64
DC = DI // P


class Program:

    def __init__(self, nc):
        self.nc, self.held = nc, []

    def phase(self, build, *args):
        build(self, *args)
        self.nc.clear_and_free_semaphores(self.held)
        self.nc.all_engine_barrier()
        self.held = []

    def sem(self, name):
        self.held.append(self.nc.alloc_semaphore(name))
        return self.held[-1]

    def semaphores(self, prefix, names):
        return [self.sem(f"{prefix}_{n}") for n in names.split()]


def buffers(nc, stack, prefix):
    def sb(name, shape, dtype=F32):
        return stack.enter_context(nc.sbuf_tensor(f"{prefix}_{name}", shape, dtype))

    def bank(name, dtype=F32):
        return stack.enter_context(nc.psum_tensor(f"{prefix}_{name}", [P, BANK], dtype))

    return sb, bank


def load_phase(prog, d):
    nc = prog.nc
    (loaded, zeroed, scratch_cleared) = prog.semaphores("ld", "loaded zeroed scratch_cleared")
    with nc.Block() as block:

        @block.sync
        def _(sp):
            for q in range(4):
                tiles = slice(q * 4, q * 4 + 4)
                sp.dma_start(prog.x[:, tiles, :], d["x"].rearrange("(t p) c -> p t c", p=P)[:, tiles, :]).then_inc(loaded, 16)
            sp.dma_start(prog.ident[:, :], d["c_ident"]).then_inc(loaded, 16)
            sp.dma_start(prog.route_consts[:, :], d["c_route"]).then_inc(loaded, 16)
            sp.dma_start(prog.tri[:, :], d["c_tri"].bitcast(BF16)).then_inc(loaded, 16)
            sp.wait_ge(loaded, 16 * 7)

        @block.gpsimd
        def _(pool):
            pool.memset(prog.zeros[:, :], 0.0).then_inc(zeroed, 1)
            pool.memset(prog.ones_b[:, :], 1.0).then_inc(zeroed, 1)
            pool.memset(prog.inv_p[:, :], 1.0 / P).then_inc(zeroed, 1)

        @block.scalar
        def _(act):
            act.wait_ge(zeroed, 3)
            for q in range(0, SLOT_TILES, 4):
                act.dma_start(d["sorted_x"].rearrange("(j p) c -> p j c", p=P)[:, q:q + 4, :],
                              prog.zeros[:, :].rearrange("p (j c) -> p j c", j=4)).then_inc(scratch_cleared, 16)
            act.wait_ge(scratch_cleared, 16 * (SLOT_TILES // 4))


def norm_phase(prog, tag):
    nc = prog.nc
    x, xn, xnT = prog.x, prog.xn, prog.xnT
    (stats_done, moments_done, std_done, rstd_step, normed, transposed, evac_a, evac_v) = prog.semaphores(
        tag, "stats_done moments_done std_done rstd_step normed transposed evac_a evac_v")
    with ExitStack() as stack:
        sb, bank = buffers(nc, stack, tag)
        stats = sb("stats", [P, NT, 6])
        mom = sb("mom", [P, NT, 2])
        var = sb("var", [P, NT])
        std = sb("std", [P, NT])
        r = sb("r", [P, NT])
        r2 = sb("r2", [P, NT])
        r3 = sb("r3", [P, NT])
        tb = [bank(f"tb{i}") for i in range(4)]
        block = stack.enter_context(nc.Block())

        @block.vector
        def _(dve):
            for t in range(NT):
                dve.bn_stats(stats[:, t, :], x[:, t, :]).then_inc(stats_done, 1)
            for t in range(NT):
                dve.wait_ge(stats_done, t + 1)
                dve.bn_aggr(mom[:, t, :], stats[:, t, :]).then_inc(moments_done, 1)
            dve.wait_ge(moments_done, NT)
            dve.tensor_scalar(var[:, :], mom[:, :, 1], EPS, None, ALU.add).then_inc(moments_done, 1)
            dve.wait_ge(std_done, 1)
            dve.reciprocal(r[:, :], std[:, :]).then_inc(rstd_step, 1)
            dve.wait_ge(rstd_step, 1)
            dve.tensor_tensor(r2[:, :], r[:, :], r[:, :], ALU.mult).then_inc(rstd_step, 1)
            dve.wait_ge(rstd_step, 2)
            dve.tensor_tensor(r3[:, :], r2[:, :], var[:, :], ALU.mult).then_inc(rstd_step, 1)
            dve.wait_ge(rstd_step, 3)
            dve.tensor_scalar(r2[:, :], r3[:, :], -0.5, 1.5, ALU.mult, ALU.add).then_inc(rstd_step, 1)
            dve.wait_ge(rstd_step, 4)
            dve.tensor_tensor(r3[:, :], r2[:, :], r[:, :], ALU.mult).then_inc(rstd_step, 1)
            dve.wait_ge(rstd_step, 5)
            for t in range(NT):
                dve.tensor_scalar(xn[:, t, :], x[:, t, :], mom[:, t, 0:1], r3[:, t:t + 1],
                                  ALU.subtract, ALU.mult).then_inc(normed, 1)
            for q in (1, 3):
                dve.wait_ge(transposed, 4 * (q + 1))
                dve.tensor_copy(xnT[:, q * BANK:(q + 1) * BANK], tb[q][:, :]).then_inc(evac_v, 1)

        @block.tensor
        def _(pe):
            for t in range(NT):
                pe.wait_ge(normed, t + 1)
                pe.transpose(tb[t // 4][:, (t % 4) * P:(t % 4 + 1) * P], xn[:, t, :], prog.ident[:, :]).then_inc(transposed, 1)

        @block.scalar
        def _(act):
            act.wait_ge(moments_done, NT + 1)
            act.activation(std[:, :], var[:, :], ACT.Sqrt).then_inc(std_done, 1)
            for q in (0, 2):
                act.wait_ge(transposed, 4 * (q + 1))
                act.activation(xnT[:, q * BANK:(q + 1) * BANK], tb[q][:, :], ACT.Copy).then_inc(evac_a, 1)


def wait(engine, semaphore, value):
    if not isinstance(value, int) or value > 0:
        engine.wait_ge(semaphore, value)


def attention_phase(prog, d):
    nc = prog.nc
    x, xnT, ident = prog.x, prog.xnT, prog.ident
    SCALE = 1.0 / (128.0 ** 0.5 + 1e-08)
    H = HEADS
    with ExitStack() as stack:
        sb, bank = buffers(nc, stack, "at")
        wq = sb("wq", [P, P])
        wkvT = sb("wkvT", [P, P])
        wvT = sb("wvT", [P, P])
        wdown = sb("wdown", [P, 32])
        wup = sb("wup", [32, 2, P])
        wo = sb("wo", [P, P])
        decay = sb("decay", [P, QT, S])
        headmask = sb("headmask", [P, HEADS])
        downT = sb("downT", [32, P])
        wkv_eff = sb("wkv_eff", [P, 2, P])
        qT = sb("qT", [P, NTOK])
        kT = sb("kT", [P, NTOK])
        v = sb("v", [P, NT, P])
        q_cur = sb("q_cur", [P, S])
        qm = sb("qm", [P, HEADS, S])
        vaug = sb("vaug", [P, QT, HEADS, 32])
        sc = [sb(f"sc{i}", [P, BANK]) for i in range(2)]
        sd = [sb(f"sd{i}", [P, BANK]) for i in range(4)]
        rowmax = sb("rowmax", [P, HEADS, QT])
        negmax = sb("negmax", [P, HEADS, QT])
        pr = [sb(f"pr{i}", [P, BANK]) for i in range(4)]
        prT = [sb(f"prT{i}", [P, BANK]) for i in range(8)]
        oT = sb("oT", [P, S])
        rden = sb("rden", [P, QT, GH])
        on = sb("on", [P, QT, P])
        onT = sb("onT", [P, S])
        score_b = [bank(f"score{i}") for i in range(2)]
        trans_b = [bank(f"trans{i}") for i in range(2)]
        out_b = [bank(f"out{i}") for i in range(2)]
        quad_b = bank("quad")
        misc_b = bank("misc")
        proj_b = [*score_b, *trans_b]

        (wloaded, wsum, eff_step, eff_evac, vones, projected_in, evac_a, evac_v) = prog.semaphores(
            "atw", "wloaded wsum eff_step eff_evac vones projected_in evac_a evac_v")
        with nc.Block() as block:
            FILLS = 2 * NTOK // BANK + NT // 4

            @block.sync
            def _(sp):
                for dst, src in ((wkvT[:, :], d["WkT"]), (wvT[:, :], d["WvT"]), (wdown[:, :], d["W_down"]),
                                 (wup[:, 0, :], d["W_up_k"]), (wup[:, 1, :], d["W_up_v"]), (wq[:, :], d["Wq"]), (wo[:, :], d["Wo"]),
                                 (headmask[:, :], d["c_headmask"]), (decay[:, :, :], d["c_decay"])):
                    sp.dma_start(dst, src).then_inc(wloaded, 16)

            @block.gpsimd
            def _(pool):
                pool.memset(vaug[:, :, :, :], 0.0).then_inc(vones, 1)
                pool.wait_ge(vones, 1)
                pool.memset(vaug[:, :, :, HD:HD + 1], 1.0).then_inc(vones, 1)

            @block.vector
            def _(dve):
                dve.wait_ge(wloaded, 16 * 9)
                dve.tensor_tensor(wkvT[:, :], wkvT[:, :], wvT[:, :], ALU.add).then_inc(wsum, 1)
                dve.wait_ge(eff_step, 1)
                dve.tensor_copy(downT[:, :], misc_b[0:32, 0:P]).then_inc(eff_evac, 1)
                dve.wait_ge(eff_step, 2)
                dve.tensor_copy(wkv_eff[:, :, :], quad_b[:, 0:2 * P].rearrange("p (a c) -> p a c", a=2)).then_inc(eff_evac, 1)
                for f in range(1, FILLS, 2):
                    dve.wait_ge(projected_in, f + 1)
                    if f < 8:
                        dst = kT[:, (f // 2) * BANK:(f // 2 + 1) * BANK]
                    else:
                        dst = v[:, (f - 8) * 4:(f - 7) * 4, :].rearrange("p t c -> p (t c)")
                    dve.tensor_copy(dst, proj_b[f % 4][:, :]).then_inc(evac_v, 1)

            @block.tensor
            def _(pe):
                pe.wait_ge(wsum, 1)
                pe.matmul(misc_b[0:32, 0:P], wdown[:, :], wkvT[:, :], start=True, stop=True).then_inc(eff_step, 1)
                pe.wait_ge(eff_evac, 1)
                pe.matmul(quad_b[:, 0:2 * P], downT[:, :], wup[:, :, :].rearrange("p a c -> p (a c)"),
                          start=True, stop=True).then_inc(eff_step, 1)
                pe.wait_ge(eff_evac, 2)
                for f in range(FILLS):
                    if f >= 4:
                        pe.wait_ge(evac_v if f % 2 else evac_a, (f - 4) // 2 + 1)
                    if f < 8:
                        w = wkv_eff[:, 0, :] if f % 2 else wq[:, :]
                        pe.matmul(proj_b[f % 4][:, :], w, xnT[:, (f // 2) * BANK:(f // 2 + 1) * BANK],
                                  start=True, stop=True).then_inc(projected_in, 1)
                    else:
                        for t in range(4):
                            tok = ((f - 8) * 4 + t) * P
                            last = pe.matmul(proj_b[f % 4][:, t * P:(t + 1) * P], xnT[:, tok:tok + P], wkv_eff[:, 1, :],
                                             start=True, stop=True)
                        last.then_inc(projected_in, 1)

            @block.scalar
            def _(act):
                for f in range(0, FILLS, 2):
                    act.wait_ge(projected_in, f + 1)
                    if f < 8:
                        act.activation(qT[:, (f // 2) * BANK:(f // 2 + 1) * BANK], proj_b[f % 4][:, :], ACT.Copy,
                                       scale=SCALE).then_inc(evac_a, 1)
                    else:
                        act.activation(v[:, (f - 8) * 4:(f - 7) * 4, :].rearrange("p t c -> p (t c)"), proj_b[f % 4][:, :],
                                       ACT.Copy).then_inc(evac_a, 1)

        (q_copied, qm_ready, vaug_ready, scored, clipped, decayed, negated, exped, ptrans, pt_ready, attended, ot_ready,
         ot_trans, rden_ready, normed, on_trans, ont_ready, projected, added) = prog.semaphores(
            "at", "q_copied qm_ready vaug_ready scored clipped decayed negated exped ptrans pt_ready attended ot_ready "
                  "ot_trans rden_ready normed on_trans ont_ready projected added")
        block = stack.enter_context(nc.Block())
        LAST_STEP = 12

        def sequences(engine, steps):
            steps(0, range(H), lambda n: n >= 0)
            with engine.Fori(1, B) as b:
                steps(b, range(H), lambda n: True)
            steps(B, range(LAST_STEP), lambda n: n < 0)

        @block.tensor
        def _(pe):
            def steps(b, numbers, live):
                for s in numbers:
                    if live(s):
                        wait(pe, qm_ready, b * H + s + 1)
                        wait(pe, clipped, b * H + s - 1)
                        for q in range(QT):
                            last = pe.matmul(score_b[s % 2][:, q * S:(q + 1) * S], qm[:, s, q * P:(q + 1) * P],
                                             kT[:, bass.ds(b * S, S)], start=True, stop=True)
                        last.then_inc(scored, 1)
                    n = s - 3
                    if live(n):
                        wait(pe, exped, (b * H + n + 1) * QT)
                        wait(pe, pt_ready, b * H + n - 1)
                        for k in range(QT):
                            for q in range(QT):
                                last = pe.transpose(trans_b[n % 2][:, k * S + q * P:k * S + (q + 1) * P],
                                                    pr[n % 4][:, q * S + k * P:q * S + (k + 1) * P], ident[:, :])
                        last.then_inc(ptrans, 1)
                    g, at = (s - 7) // GH, (s - 7) % GH == 0
                    if at and live(g):
                        wait(pe, pt_ready, b * H + (g + 1) * GH)
                        wait(pe, vaug_ready, b * GROUPS + g + 1)
                        wait(pe, ot_ready, b * GROUPS + g - 1)
                        for k in range(QT):
                            for j in range(GH):
                                h = (g * GH + j) % H
                                last = pe.matmul(out_b[g % 2][32 * j:32 * j + 32, 0:S], vaug[:, k, h, :],
                                                 prT[h % 8][:, k * S:(k + 1) * S], start=(k == 0), stop=(k == QT - 1))
                        last.then_inc(attended, 1)
                    g, at = (s - 9) // GH, (s - 9) % GH == 0
                    if at and live(g):
                        wait(pe, ot_ready, b * GROUPS + g + 1)
                        wait(pe, normed, b * GROUPS + g)
                        for q in range(QT):
                            last = pe.transpose(quad_b[:, q * P:(q + 1) * P], oT[:, q * P:(q + 1) * P], ident[:, :])
                        last.then_inc(ot_trans, 1)
                    if s == 8 and live(-1):
                        wait(pe, normed, b * GROUPS)
                        for q in range(QT):
                            last = pe.transpose(misc_b[:, q * P:(q + 1) * P], on[:, q, :], ident[:, :])
                        last.then_inc(on_trans, 1)
                    if s == 10 and live(-1):
                        wait(pe, ont_ready, b)
                        for q in range(QT):
                            last = pe.matmul(misc_b[:, q * P:(q + 1) * P], onT[:, q * P:(q + 1) * P], wo[:, :],
                                             start=True, stop=True)
                        last.then_inc(projected, 1)

            sequences(pe, steps)

        @block.vector
        def _(dve):
            def steps(b, numbers, live):
                for s in numbers:
                    if live(s):
                        wait(dve, scored, b * H + s + 1)
                        dve.tensor_scalar(sc[s % 2][:, :], score_b[s % 2][:, :], -CLAMP, CLAMP, ALU.max, ALU.min).then_inc(clipped, 1)
                    n = s - 1
                    if live(n) or live(s):
                        if live(s):
                            wait(dve, clipped, b * H + s + 1)
                            wait(dve, exped, (b * H + s - 3) * QT)
                        if live(n):
                            wait(dve, decayed, (b * H + n + 1) * QT)
                            dve.tensor_scalar(negmax[:, n % H, :], rowmax[:, n % H, :], -1.0, None, ALU.mult).then_inc(negated, 1)
                    if live(s):
                        for q in range(QT):
                            dve.tensor_tensor_reduce(
                                out=sd[s % 4][:, q * S:(q + 1) * S], in0=sc[s % 2][:, q * S:(q + 1) * S], in1=decay[:, q, :],
                                scale=1.0, scalar=-3.0e38, op0=ALU.mult, op1=ALU.max,
                                accum_out=rowmax[:, s, q:q + 1]).then_inc(decayed, 1)
                    g, at = (s - 11) // GH, (s - 11) % GH == 0
                    if at and live(g):
                        wait(dve, ot_trans, b * GROUPS + g + 1)
                        if g >= 0:
                            wait(dve, on_trans, b)
                        heads = quad_b[:, 0:QT * P].rearrange("p (q j c) -> p q j c", q=QT, j=GH)
                        dve.reciprocal(rden[:, :, :], heads[:, :, :, HD]).then_inc(rden_ready, 1)
                        wait(dve, rden_ready, b * GROUPS + g + 1)
                        for q in range(QT):
                            last = dve.tensor_tensor(on[:, q, (g % GROUPS) * 32:(g % GROUPS + 1) * 32].rearrange("p (j c) -> p j c", j=GH),
                                                     heads[:, q, :, 0:HD],
                                                     rden[:, q, :].unsqueeze(2).to_broadcast([P, GH, HD]), ALU.mult)
                        last.then_inc(normed, 1)
                    if s == 11 and live(-1):
                        wait(dve, projected, b)
                        xs = x[:, bass.ds(b * QT - QT, QT), :]
                        dve.tensor_tensor(xs, misc_b[:, 0:QT * P].rearrange("p (q c) -> p q c", q=QT), xs, ALU.add).then_inc(added, 1)

            sequences(dve, steps)

        @block.gpsimd
        def _(pool):
            def sequence(b, first):
                pool.wait_ge(qm_ready, b * H) if not first else None
                pool.wait_ge(wloaded, 16 * 9)
                pool.tensor_copy(q_cur[:, :], qT[:, bass.ds(b * S, S)]).then_inc(q_copied, 1)
                for g in range(GROUPS):
                    for h in range(g * GH, (g + 1) * GH):
                        pool.wait_ge(q_copied, b + 1)
                        if not first:
                            pool.wait_ge(scored, b * H - H + h + 1)
                        pool.tensor_tensor(qm[:, h, :], q_cur[:, :], headmask[:, h:h + 1].to_broadcast([P, S]),
                                           ALU.mult).then_inc(qm_ready, 1)
                    if not first:
                        pool.wait_ge(attended, b * GROUPS - GROUPS + g + 1)
                    pool.wait_ge(wloaded, 16 * 9)
                    pool.tensor_copy(vaug[:, :, g * GH:(g + 1) * GH, 0:HD],
                                     v[:, bass.ds(b * QT, QT), g * 32:(g + 1) * 32].rearrange("p q (j c) -> p q j c", j=GH),
                                     ).then_inc(vaug_ready, 1)

            sequence(0, True)
            with pool.Fori(1, B) as b:
                sequence(b, False)

        @block.scalar
        def _(act):
            def steps(b, numbers, live):
                for s in numbers:
                    if live(s):
                        wait(act, ptrans, b * H + s - 3)
                        wait(act, negated, b * H + s + 1)
                        for q in range(QT):
                            act.activation(pr[s % 4][:, q * S:(q + 1) * S], sd[s % 4][:, q * S:(q + 1) * S], ACT.Exp,
                                           bias=negmax[:, s, q:q + 1]).then_inc(exped, 1)
                    n = s - 2
                    if live(n):
                        wait(act, ptrans, b * H + n + 1)
                        wait(act, attended, b * GROUPS + n // GH - 1)
                        act.activation(prT[n % 8][:, :], trans_b[n % 2][:, :], ACT.Copy).then_inc(pt_ready, 1)
                    g, at = (s - 7) // GH, (s - 7) % GH == 0
                    if at and live(g):
                        wait(act, attended, b * GROUPS + g + 1)
                        wait(act, ot_trans, b * GROUPS + g)
                        act.activation(oT[:, :], out_b[g % 2][:, 0:S], ACT.Copy).then_inc(ot_ready, 1)
                    if s == 9 and live(-1):
                        wait(act, on_trans, b)
                        act.activation(onT[:, :], misc_b[:, 0:S], ACT.Copy).then_inc(ont_ready, 1)

            sequences(act, steps)


R_LESS, R_THRESH, R_TILE, R_PART, R_ONES = 0, 8, 24, 48, 56


def experts_phase(prog, d, tag):
    nc = prog.nc
    x, xn, xnT, ident, rc = prog.x, prog.xn, prog.xnT, prog.ident, prog.route_consts
    U = 4
    WC = HID + HC * P + HC + 1
    with ExitStack() as stack:
        sb, bank = buffers(nc, stack, tag)
        gw = sb("gw", [P, E_N])
        gb = sb("gb", [P, E_N])
        logits = sb("logits", [P, NT, E_N])
        best = sb("best", [P, NT])
        work = sb("work", [P, NT, E_N])
        first = sb("first", [P, NT])
        onehot = sb("onehot", [P, NT, E_N], BF16)
        upto = sb("upto", [P, E_N, NT])
        over = sb("over", [P, E_N, NT])
        tiles = sb("tiles", [P, E_N])
        tile_end = sb("tile_end", [P, E_N])
        tile_start = sb("tile_start", [P, E_N])
        slot_f = sb("slot_f", [P, NT])
        slot = sb("slot", [P, NT], U32)
        before = sb("before", [P, SLOT_TILES, E_N])
        owner_f = sb("owner_f", [P, SLOT_TILES])
        owner = sb("owner", [P, SLOT_TILES], U32)
        sorted_sb = sb("sorted_sb", [P, SLOT_TILES, P])
        sortedT = sb("sortedT", [P, SLOT_TILES * P])
        yT = sb("yT", [P, SLOT_TILES * P])
        y_tok = sb("y_tok", [P, NT, P])
        W = [sb(f"W{u}", [P, WC]) for u in range(U)]
        hT = [sb(f"hT{u}", [P, HC, P]) for u in range(U)]
        banks = [bank(f"b{i}") for i in range(8)]
        logit_b, rank_b = banks[4], banks[5]

        (loaded, logits_done, onehot_done, counted, slots_done, owners_done, chain, scattered, sorted_loaded, transposed,
         evac_a, evac_v) = prog.semaphores(
            tag, "loaded logits_done onehot_done counted slots_done owners_done chain scattered sorted_loaded transposed evac_a evac_v")
        GROUPS_T = SLOT_TILES // 4
        with nc.Block() as block:

            @block.sync
            def _(sp):
                sp.dma_start(gw[:, :], d["gate_wT"]).then_inc(loaded, 16)
                sp.dma_start(gb[:, :], d["gate_b"].to_broadcast([P, E_N])).then_inc(loaded, 16)
                sp.wait_ge(scattered, 16 * NT)
                for q in range(GROUPS_T):
                    sp.dma_start(sorted_sb[:, q * 4:q * 4 + 4, :],
                                 d["sorted_x"].rearrange("(j p) c -> p j c", p=P)[:, q * 4:q * 4 + 4, :]).then_inc(sorted_loaded, 16)

            @block.tensor
            def _(pe):
                pe.wait_ge(loaded, 32)
                for t in range(NT):
                    last = pe.matmul(logit_b[:, t * E_N:(t + 1) * E_N], xnT[:, t * P:(t + 1) * P], gw[:, :], start=True, stop=True)
                last.then_inc(logits_done, 1)
                pe.wait_ge(onehot_done, 1)
                oh = onehot[:, :, :].rearrange("p t e -> p (t e)")
                pe.matmul(rank_b[:, 0:NT * E_N], prog.tri[:, :], oh, start=True, stop=True)
                pe.matmul(rank_b[:, NT * E_N:2 * NT * E_N], prog.ones_b[:, :], oh, start=True, stop=True).then_inc(counted, 1)
                pe.wait_ge(sorted_loaded, 16 * GROUPS_T)
                for q in range(GROUPS_T):
                    if q >= 4:
                        pe.wait_ge(evac_v if q % 2 else evac_a, (q - 4) // 2 + 1)
                    for t in range(4):
                        last = pe.transpose(banks[q % 4][:, t * P:(t + 1) * P], sorted_sb[:, q * 4 + t, :], ident[:, :])
                    last.then_inc(transposed, 1)

            @block.vector
            def _(dve):
                links = [0]

                def link(instruction):
                    links[0] += 1
                    instruction.then_inc(chain, 1)
                    dve.wait_ge(chain, links[0])

                def over_e(a):
                    return a.unsqueeze(2).to_broadcast([P, a.shape[1], E_N])

                def over_t(a, n=NT):
                    return a.unsqueeze(1).to_broadcast([P, n, E_N])

                less = over_t(rc[:, R_LESS:R_LESS + E_N])
                dve.wait_ge(loaded, 32)
                dve.wait_ge(logits_done, 1)
                link(dve.tensor_tensor(logits[:, :, :], logit_b[:, 0:NT * E_N].rearrange("p (t e) -> p t e", e=E_N),
                                       over_t(gb[:, :]), ALU.add))
                link(dve.tensor_reduce(best[:, :], logits[:, :, :], AX.X, ALU.max))
                link(dve.tensor_tensor(work[:, :, :], logits[:, :, :], over_e(best[:, :]), ALU.is_equal))
                link(dve.tensor_tensor(work[:, :, :], work[:, :, :], less, ALU.mult))
                link(dve.tensor_reduce(first[:, :], work[:, :, :], AX.X, ALU.min))
                dve.tensor_tensor(onehot[:, :, :], less, over_e(first[:, :]), ALU.is_equal).then_inc(onehot_done, 1)
                dve.wait_ge(onehot_done, 1)
                dve.wait_ge(counted, 1)
                lower = rank_b[:, 0:NT * E_N].rearrange("p (t e) -> p t e", e=E_N)
                total = rank_b[:, NT * E_N:2 * NT * E_N].rearrange("p (t e) -> p t e", e=E_N)
                for e in range(E_N):
                    last = dve.tensor_tensor_scan(upto[:, e, :], rc[:, R_ONES:R_ONES + NT], total[:, :, e], 0.0, ALU.mult, ALU.add)
                link(last)
                link(dve.tensor_tensor(over[:, :, :], upto[:, :, NT - 1:NT].to_broadcast([P, E_N, NT]),
                                       rc[:, R_THRESH:R_THRESH + NT].unsqueeze(1).to_broadcast([P, E_N, NT]), ALU.is_gt))
                link(dve.tensor_reduce(tiles[:, :], over[:, :, :], AX.X, ALU.add))
                link(dve.tensor_tensor_scan(tile_end[:, :], rc[:, R_ONES:R_ONES + E_N], tiles[:, :], 0.0, ALU.mult, ALU.add))
                link(dve.tensor_tensor(tile_start[:, :], tile_end[:, :], tiles[:, :], ALU.subtract))
                link(dve.tensor_tensor(work[:, :, :], upto[:, :, :].rearrange("p e t -> p t e"), total, ALU.subtract))
                link(dve.scalar_tensor_tensor(work[:, :, :], over_t(tile_start[:, :]), float(P), work[:, :, :], ALU.mult, ALU.add))
                link(dve.tensor_tensor(work[:, :, :], work[:, :, :], lower, ALU.add))
                link(dve.tensor_tensor(work[:, :, :], work[:, :, :], onehot[:, :, :], ALU.mult))
                link(dve.tensor_reduce(slot_f[:, :], work[:, :, :], AX.X, ALU.add))
                dve.tensor_copy(slot[:, :], slot_f[:, :]).then_inc(slots_done, 1)
                link(dve.tensor_tensor(before[:, :, :], over_t(tile_end[:, :], SLOT_TILES),
                                       over_e(rc[:, R_TILE:R_TILE + SLOT_TILES]), ALU.is_le))
                link(dve.tensor_reduce(owner_f[:, :], before[:, :, :], AX.X, ALU.add))
                dve.tensor_scalar(owner[:, :], owner_f[:, :], E_N - 1.0, None, ALU.min).then_inc(owners_done, 1)
                for q in range(1, GROUPS_T, 2):
                    dve.wait_ge(transposed, q + 1)
                    dve.tensor_copy(sortedT[:, q * BANK:(q + 1) * BANK], banks[q % 4][:, :]).then_inc(evac_v, 1)

            @block.gpsimd
            def _(pool):
                pool.wait_ge(slots_done, 1)
                for t in range(NT):
                    pool.indirect_dma_start(out=d["sorted_x"], out_offset=bass.IndirectOffsetOnAxis(ap=slot[:, t:t + 1], axis=0),
                                            in_=xn[:, t, :], in_offset=None).then_inc(scattered, 16)

            @block.scalar
            def _(act):
                for q in range(0, GROUPS_T, 2):
                    act.wait_ge(transposed, q + 1)
                    act.activation(sortedT[:, q * BANK:(q + 1) * BANK], banks[q % 4][:, :], ACT.Copy).then_inc(evac_a, 1)

        (hidden_done, relu_a, relu_v, out_done, out_evac, back_transposed, back_a, back_v, y_stored,
         y_fetched, added) = prog.semaphores(
            tag + "e", "hidden_done relu_a relu_v out_done out_evac back_transposed back_a back_v y_stored y_fetched added")
        fetched = [prog.sem(f"{tag}e_fetched{u}") for u in range(U)]
        PASSES = SLOT_TILES // U
        with nc.Block() as block:

            def passes(engine, steps):
                steps(0, range(U), lambda n: n >= 0)
                with engine.Fori(1, PASSES) as i:
                    steps(i, range(U), lambda n: True)
                steps(PASSES, range(1), lambda n: n < 0)

            @block.sync
            def _(sp):
                def fetch(i, u, first):
                    if not first:
                        sp.wait_ge(out_evac, i * U + (u - U + 1))
                    e = sp.value_load(owner[0:1, bass.ds(i * U + u, 1)], min_val=0, max_val=E_N - 1)
                    sp.dma_start(W[u][:, :], d["experts"][bass.ds(e * P, P), :]).then_inc(fetched[u], 16)

                sp.wait_ge(owners_done, 1)
                for u in range(U):
                    fetch(0, u, True)
                with sp.Fori(1, PASSES) as i:
                    for u in range(U):
                        fetch(i, u, False)

            @block.tensor
            def _(pe):
                def steps(i, numbers, live):
                    for s in numbers:
                        if live(s):
                            pe.wait_ge(fetched[s], (i + 1) * 16)
                            wait(pe, relu_a, i * U + s - 1)
                            wait(pe, relu_v, i * U + s - 1)
                            for c in range(HC):
                                last = pe.matmul(banks[(s % 2) * 2 + c // 2][:, (c % 2) * P:(c % 2 + 1) * P],
                                                 W[s][:, c * P:(c + 1) * P], sortedT[:, bass.ds((i * U + s) * P, P)],
                                                 start=True, stop=True)
                            last.then_inc(hidden_done, 1)
                        n = s - 1
                        if live(n):
                            u = n % U
                            wait(pe, relu_a, i * U + n + 1)
                            wait(pe, relu_v, i * U + n + 1)
                            wait(pe, out_evac, i * U + n - 1)
                            for c in range(HC):
                                last = pe.matmul(banks[4 + u % 2][:, 0:P], W[u][:, HID + c * P:HID + (c + 1) * P], hT[u][:, c, :],
                                                 start=(c == 0), stop=(c == HC - 1))
                            last.then_inc(out_done, 1)

                passes(pe, steps)

            @block.scalar
            def _(act):
                def steps(i, numbers, live):
                    for s in numbers:
                        if live(s):
                            wait(act, out_done, i * U + s - U + 1)
                            wait(act, hidden_done, i * U + s + 1)
                            for c in (0, 1):
                                last = act.activation(hT[s][:, c, :], banks[(s % 2) * 2][:, c * P:(c + 1) * P], ACT.Relu,
                                                      bias=W[s][:, 2 * HID + c:2 * HID + c + 1])
                            last.then_inc(relu_a, 1)
                        n = s - 1
                        if live(n):
                            wait(act, out_done, i * U + n + 1)
                            act.activation(yT[:, bass.ds((i * U + n) * P, P)], banks[4 + n % 2][:, 0:P], ACT.Identity,
                                           bias=W[n % U][:, WC - 1:WC]).then_inc(out_evac, 1)

                passes(act, steps)

            @block.vector
            def _(dve):
                def steps(i, numbers, live):
                    for s in numbers:
                        if live(s):
                            wait(dve, out_done, i * U + s - U + 1)
                            wait(dve, hidden_done, i * U + s + 1)
                            for c in (2, 3):
                                last = dve.tensor_scalar(hT[s][:, c, :], banks[(s % 2) * 2 + 1][:, (c - 2) * P:(c - 1) * P],
                                                         W[s][:, 2 * HID + c:2 * HID + c + 1], 0.0, ALU.add, ALU.max)
                            last.then_inc(relu_v, 1)

                passes(dve, steps)

        with nc.Block() as block:
            y_sorted = sorted_sb

            @block.tensor
            def _(pe):
                for q in range(GROUPS_T):
                    for t in range(4):
                        last = pe.transpose(banks[q][:, t * P:(t + 1) * P], yT[:, (q * 4 + t) * P:(q * 4 + t + 1) * P], ident[:, :])
                    last.then_inc(back_transposed, 1)

            @block.scalar
            def _(act):
                for q in range(0, GROUPS_T, 2):
                    act.wait_ge(back_transposed, q + 1)
                    act.activation(y_sorted[:, q * 4:q * 4 + 4, :].rearrange("p j c -> p (j c)"), banks[q][:, :], ACT.Copy).then_inc(back_a, 1)

            @block.vector
            def _(dve):
                for q in range(1, GROUPS_T, 2):
                    dve.wait_ge(back_transposed, q + 1)
                    dve.tensor_copy(y_sorted[:, q * 4:q * 4 + 4, :].rearrange("p j c -> p (j c)"), banks[q][:, :]).then_inc(back_v, 1)
                dve.wait_ge(y_fetched, 16 * NT)
                dve.tensor_tensor(x[:, :, :], x[:, :, :], y_tok[:, :, :], ALU.add).then_inc(added, 1)

            @block.sync
            def _(sp):
                for q in range(GROUPS_T):
                    sp.wait_ge(back_v if q % 2 else back_a, q // 2 + 1)
                    sp.dma_start(d["sorted_y"].rearrange("(j p) c -> p j c", p=P)[:, q * 4:q * 4 + 4, :],
                                 y_sorted[:, q * 4:q * 4 + 4, :]).then_inc(y_stored, 16)

            @block.gpsimd
            def _(pool):
                pool.wait_ge(y_stored, 16 * GROUPS_T)
                for t in range(NT):
                    pool.indirect_dma_start(out=y_tok[:, t, :], out_offset=None, in_=d["sorted_y"],
                                            in_offset=bass.IndirectOffsetOnAxis(ap=slot[:, t:t + 1], axis=0)).then_inc(y_fetched, 16)


def mamba_phase(prog, d):
    nc = prog.nc
    x, xnT, ident = prog.x, prog.xnT, prog.ident
    G = NTOK // BANK
    GS = BANK // S
    with ExitStack() as stack:
        sb, _ = buffers(nc, stack, "m")
        w_in = sb("w_in", [P, 2 * DI])
        conv_w = sb("conv_w", [P, DC, 4])
        conv_b = sb("conv_b", [P, DC])
        w_x = sb("w_x", [P, DC, DTR + 2 * NS])
        w_dt = sb("w_dt", [DTR, DI])
        b_dt = sb("b_dt", [P, DC])
        a_log = sb("a_log", [P, DC, NS])
        a_exp = sb("a_exp", [P, DC, NS])
        a_neg = sb("a_neg", [P, DC, NS])
        skip = sb("skip", [P, DC])
        w_out = sb("w_out", [P, DC, P])
        f_w1 = sb("f_w1", [P, HID])
        f_b1 = sb("f_b1", [P, HC])
        f_w2 = sb("f_w2", [P, HC, P])
        f_b2 = sb("f_b2", [P, 1])
        pick = sb("pick", [96, 2 * NS, P], BF16)
        u = sb("u", [P, DC, NTOK])
        sres = sb("sres", [P, DC, NTOK])
        delta = sb("delta", [P, DC, NTOK])
        yz = sb("yz", [P, DC, NTOK])
        bc3 = sb("bc3", [96, NTOK], BF16)

        (loaded, xz_done, conv_first, conv_step, conv_done, res_done, u_done) = prog.semaphores(
            "ma", "loaded xz_done conv_first conv_step conv_done res_done u_done")
        with ExitStack() as inner:
            sbi, bank = buffers(nc, inner, "ma")
            xz_b = [[bank(f"xz{i}{c}") for c in range(4)] for i in range(2)]
            acc = [[sbi(f"acc{i}{c}", [P, GS, S]) for c in range(DC)] for i in range(2)]
            block = inner.enter_context(nc.Block())

            @block.sync
            def _(sp):
                for dst, src in ((w_in[:, :], d["in_projT"]), (conv_w[:, :, :], d["conv_w"]), (conv_b[:, :], d["conv_b"]),
                                 (w_x[:, :, :], d["x_projT"]), (w_dt[:, :], d["dt_projT"]), (b_dt[:, :], d["dt_b"]),
                                 (a_log[:, :, :], d["A_log"]), (skip[:, :], d["D"]), (w_out[:, :, :], d["out_projT"]),
                                 (f_w1[:, :], d["ffn_w1T"]), (f_b1[:, :], d["ffn_b1"]), (f_w2[:, :, :], d["ffn_w2T"]),
                                 (f_b2[:, :], d["ffn_b2"]), (pick[:, :, :], d["c_pick"].bitcast(BF16))):
                    sp.dma_start(dst, src).then_inc(loaded, 16)

            @block.tensor
            def _(pe):
                pe.wait_ge(loaded, 16 * 14)
                for g in range(G):
                    for c in range(4):
                        if g >= 2:
                            if c < DC:
                                pe.wait_ge(conv_done, (g - 2) * DC + c + 1)
                            else:
                                pe.wait_ge(res_done, (g - 2) * DC + c - DC + 1)
                        pe.matmul(xz_b[g % 2][c][:, :], w_in[:, c * P:(c + 1) * P], xnT[:, g * BANK:(g + 1) * BANK],
                                  start=True, stop=True).then_inc(xz_done, 1)

            @block.scalar
            def _(act):
                act.wait_ge(loaded, 16 * 14)
                for g in range(G):
                    for c in range(DC):
                        act.wait_ge(xz_done, g * 4 + c + 1)
                        wait(act, u_done, (g - 2) * DC + c + 1)
                        act.activation(acc[g % 2][c][:, :, :].rearrange("p a s -> p (a s)"), xz_b[g % 2][c][:, :], ACT.Identity,
                                       bias=conv_b[:, c:c + 1], scale=conv_w[:, c, 3:4]).then_inc(conv_first, 1)
                    for c in range(DC):
                        act.wait_ge(xz_done, g * 4 + DC + c + 1)
                        act.activation(sres[:, c, g * BANK:(g + 1) * BANK], xz_b[g % 2][DC + c][:, :], ACT.Silu).then_inc(res_done, 1)
                    for c in range(DC):
                        act.wait_ge(conv_done, g * DC + c + 1)
                        act.activation(u[:, c, g * BANK:(g + 1) * BANK], acc[g % 2][c][:, :, :].rearrange("p a s -> p (a s)"),
                                       ACT.Silu).then_inc(u_done, 1)

            @block.vector
            def _(dve):
                for g in range(G):
                    for k in (2, 1, 0):
                        back = 3 - k
                        for c in range(DC):
                            if k == 2:
                                dve.wait_ge(conv_first, g * DC + c + 1)
                            else:
                                dve.wait_ge(conv_step, (g * 2 + 1 - k) * DC + c + 1)
                            src = xz_b[g % 2][c][:, :].rearrange("p (a s) -> p a s", a=GS)[:, :, 0:S - back]
                            to = acc[g % 2][c][:, :, back:S]
                            step = dve.scalar_tensor_tensor(to, src, conv_w[:, c, k:k + 1], to, ALU.mult, ALU.add)
                            if k == 0:
                                step.then_inc(conv_done, 1)
                            else:
                                step.then_inc(conv_step, 1)

        (xdbl_done, dt_copied, bc_copied, split_step, z_done, zb_done, abs_done, exp_done, log_done, sum_done, ones_done,
         rest_done, delta_done, a_done, a_negated) = prog.semaphores(
            "mb", "xdbl_done dt_copied bc_copied split_step z_done zb_done abs_done exp_done log_done sum_done ones_done "
                  "rest_done delta_done a_done a_negated")
        with ExitStack() as inner:
            sbi, bank = buffers(nc, inner, "mb")
            xd_b = [bank(f"xd{i}") for i in range(2)]
            z_b = [bank(f"z{i}") for i in range(4)]
            dtT = [sbi(f"dtT{i}", [DTR, BANK]) for i in range(2)]
            bc = sbi("bc", [32, BANK])
            rest1 = sbi("rest1", [32, BANK])
            rest2 = sbi("rest2", [32, BANK])
            middle = sbi("middle", [32, BANK], BF16)
            zb = [sbi(f"zb{i}", [P, BANK]) for i in range(4)]
            za = [sbi(f"za{i}", [P, BANK]) for i in range(4)]
            ze = [sbi(f"ze{i}", [P, BANK]) for i in range(4)]
            zl = [sbi(f"zl{i}", [P, BANK]) for i in range(4)]
            z1 = [sbi(f"z1{i}", [P, BANK]) for i in range(4)]
            block = inner.enter_context(nc.Block())
            NU = G * DC

            @block.tensor
            def _(pe):
                def delta_in(g):
                    for c in range(DC):
                        k = g * DC + c
                        pe.wait_ge(dt_copied, g + 1)
                        wait(pe, zb_done, k - 3)
                        pe.matmul(z_b[k % 4][:, :], w_dt[:, c * P:(c + 1) * P], dtT[g % 2][:, :], start=True, stop=True).then_inc(z_done, 1)

                for g in range(G):
                    wait(pe, dt_copied, g - 1)
                    wait(pe, bc_copied, g - 1)
                    for c in range(DC):
                        last = pe.matmul(xd_b[g % 2][0:DTR + 2 * NS, :], w_x[:, c, :], u[:, c, g * BANK:(g + 1) * BANK],
                                         start=(c == 0), stop=(c == DC - 1))
                    last.then_inc(xdbl_done, 1)
                    if g:
                        delta_in(g - 1)
                delta_in(G - 1)

            @block.scalar
            def _(act):
                act.activation(a_exp[:, :, :], a_log[:, :, :], ACT.Exp).then_inc(a_done, 1)
                for g in range(G + 1):
                    if g < G:
                        act.wait_ge(xdbl_done, g + 1)
                        wait(act, z_done, (g - 1) * DC)
                        act.activation(dtT[g % 2][:, :], xd_b[g % 2][0:DTR, :], ACT.Copy).then_inc(dt_copied, 1)
                    if g == 0:
                        continue
                    for k in range((g - 1) * DC, g * DC):
                        act.wait_ge(zb_done, k + 1)
                        wait(act, exp_done, k - 3)
                        act.activation(za[k % 4][:, :], zb[k % 4][:, :], ACT.Abs).then_inc(abs_done, 1)
                    for k in range((g - 1) * DC, g * DC):
                        act.wait_ge(abs_done, k + 1)
                        wait(act, rest_done, k - 3)
                        act.activation(ze[k % 4][:, :], za[k % 4][:, :], ACT.Exp, scale=-1.0).then_inc(exp_done, 1)
                    for k in range((g - 1) * DC, g * DC):
                        act.wait_ge(exp_done, k + 1)
                        wait(act, sum_done, k - 3)
                        act.activation(zl[k % 4][:, :], ze[k % 4][:, :], ACT.Ln, bias=1.0).then_inc(log_done, 1)

            @block.vector
            def _(dve):
                dve.wait_ge(a_done, 1)
                dve.tensor_scalar(a_neg[:, :, :], a_exp[:, :, :], -1.0, None, ALU.mult).then_inc(a_negated, 1)
                steps = [0]

                def split(instruction):
                    steps[0] += 1
                    instruction.then_inc(split_step, 1)
                    dve.wait_ge(split_step, steps[0])

                for g in range(G + 1):
                    if g < G:
                        cols = slice(g * BANK, (g + 1) * BANK)
                        dve.wait_ge(xdbl_done, g + 1)
                        dve.tensor_copy(bc[:, :], xd_b[g % 2][DTR:DTR + 2 * NS, :]).then_inc(bc_copied, 1)
                        dve.wait_ge(bc_copied, g + 1)
                        split(dve.tensor_copy(bc3[0:32, cols], bc[:, :]))
                        split(dve.tensor_tensor(rest1[:, :], bc[:, :], bc3[0:32, cols], ALU.subtract))
                        split(dve.tensor_copy(middle[:, :], rest1[:, :]))
                        split(dve.tensor_copy(bc3[32:64, cols], middle[:, :]))
                        split(dve.tensor_tensor(rest2[:, :], rest1[:, :], middle[:, :], ALU.subtract))
                        split(dve.tensor_copy(bc3[64:96, cols], rest2[:, :]))
                    if g == 0:
                        continue
                    mine = range((g - 1) * DC, g * DC)
                    for k in mine:
                        dve.wait_ge(z_done, k + 1)
                        wait(dve, abs_done, k - 3)
                        dve.tensor_scalar(zb[k % 4][:, :], z_b[k % 4][:, :], b_dt[:, k % DC:k % DC + 1], None, ALU.add).then_inc(zb_done, 1)
                    for k in mine:
                        dve.wait_ge(exp_done, k + 1)
                        dve.tensor_scalar(z1[k % 4][:, :], ze[k % 4][:, :], 1.0, -1.0, ALU.add, ALU.add).then_inc(ones_done, 1)
                    for k in mine:
                        dve.wait_ge(ones_done, k + 1)
                        wait(dve, delta_done, k - 3)
                        dve.tensor_tensor(z1[k % 4][:, :], ze[k % 4][:, :], z1[k % 4][:, :], ALU.subtract).then_inc(rest_done, 1)
                    for k in mine:
                        dve.wait_ge(log_done, k + 1)
                        dve.scalar_tensor_tensor(zl[k % 4][:, :], zb[k % 4][:, :], 0.0, zl[k % 4][:, :], ALU.max, ALU.add).then_inc(sum_done, 1)
                    for k in mine:
                        dve.wait_ge(sum_done, k + 1)
                        dve.wait_ge(rest_done, k + 1)
                        c, q = k % DC, k // DC
                        dve.tensor_tensor(delta[:, c, q * BANK:(q + 1) * BANK], zl[k % 4][:, :], z1[k % 4][:, :], ALU.add).then_inc(delta_done, 1)

        (dA_zeroed, b_done, c_done, b_copied, dA_done, du_done, dBu_done, h_done, hc_done, y_done, y_skip, y_evac) = prog.semaphores(
            "mc", "dA_zeroed b_done c_done b_copied dA_done du_done dBu_done h_done hc_done y_done y_skip y_evac")
        with ExitStack() as inner:
            sbi, bank = buffers(nc, inner, "mc")
            y_b = [bank(f"y{c}") for c in range(DC)]
            b_b = [bank(f"b{i}") for i in range(2)]
            c_b = [bank(f"c{i}") for i in range(2)]
            dA_b = [bank(f"dA{i}") for i in range(2)]
            du = [sbi(f"du{c}", [P, BANK]) for c in range(DC)]
            b_s = [sbi(f"bs{i}", [P, BANK]) for i in range(4)]
            dBu = [sbi(f"dBu{i}", [P, BANK]) for i in range(4)]
            h = [sbi(f"h{i}", [P, BANK]) for i in range(4)]
            hc = [sbi(f"hc{i}", [P, BANK]) for i in range(8)]
            ysum = [sbi(f"ysum{c}", [P, BANK]) for c in range(DC)]
            NUNITS = DC * NS
            LAG = 6
            delta_cur = [sbi(f"delta_cur{c}", [P, GS, S]) for c in range(DC)]
            delta_loaded = [prog.sem(f"mc_delta_loaded{c}") for c in range(DC)]
            block = inner.enter_context(nc.Block())

            def cols(g):
                return bass.ds(g * BANK, BANK)

            def passes(engine, steps):
                steps(0, range(NUNITS), lambda n: n >= 0)
                with engine.Fori(1, G) as g:
                    steps(g, range(NUNITS), lambda n: True)
                steps(G, range(LAG + 2), lambda n: n < 0)

            @block.tensor
            def _(pe):
                def steps(g, numbers, live):
                    for s in numbers:
                        n, c = s // DC, s % DC
                        if live(s) and c == 0:
                            wait(pe, b_copied, g * NS + n - 1)
                            pe.matmul(b_b[n % 2][:, :], pick[:, n, :], bc3[:, cols(g)], start=True, stop=True).then_inc(b_done, 1)
                            wait(pe, hc_done, (g * NS + n - 1) * DC)
                            pe.matmul(c_b[n % 2][:, :], pick[:, NS + n, :], bc3[:, cols(g)], start=True, stop=True).then_inc(c_done, 1)
                        k = s - LAG
                        if live(k):
                            n, c = (k % NUNITS) // DC, k % DC
                            wait(pe, hc_done, g * NUNITS + k + 1)
                            if n == 0:
                                wait(pe, y_evac, g * DC)
                            last = pe.matmul(y_b[c][:, :], ident[:, :], hc[k % 8][:, :], start=(n == 0), stop=(n == NS - 1))
                            last.then_inc(y_done, 1)

                passes(pe, steps)

            @block.scalar
            def _(act):
                act.wait_ge(dA_zeroed, 2)

                def steps(g, numbers, live):
                    for s in numbers:
                        n, c = s // DC, s % DC
                        if not live(s):
                            continue
                        if c == 0:
                            wait(act, b_done, g * NS + n + 1)
                            wait(act, dBu_done, (g * NS + n - 3) * DC)
                            act.activation(b_s[n % 4][:, :], b_b[n % 2][:, :], ACT.Copy).then_inc(b_copied, 1)
                        wait(act, h_done, g * NUNITS + s - 1)
                        wait(act, delta_loaded[c], (g + 1) * 16)
                        act.activation(dA_b[s % 2][:, :].rearrange("p (a s) -> p a s", a=GS)[:, :, 1:S],
                                       delta_cur[c][:, :, 1:S], ACT.Exp,
                                       scale=a_neg[:, c, n:n + 1]).then_inc(dA_done, 1)

                passes(act, steps)

            @block.sync
            def _(sp):
                def one_pass(g):
                    for c in range(DC):
                        wait(sp, dA_done, g * NUNITS - (DC - 1 - c))
                        sp.dma_start(delta_cur[c][:, :, :].rearrange("p a s -> p (a s)"), delta[:, c, cols(g)]).then_inc(delta_loaded[c], 16)

                one_pass(0)
                with sp.Fori(1, G) as g:
                    one_pass(g)

            @block.gpsimd
            def _(pool):
                def one_pass(g):
                    wait(pool, dBu_done, g * NUNITS)
                    for c in range(DC):
                        pool.tensor_tensor(du[c][:, :], delta[:, c, cols(g)], u[:, c, cols(g)], ALU.mult).then_inc(du_done, 1)
                    for s in range(NUNITS):
                        n, c = s // DC, s % DC
                        wait(pool, du_done, (g + 1) * DC)
                        wait(pool, h_done, g * NUNITS + s - 3)
                        wait(pool, b_copied, g * NS + n + 1)
                        pool.tensor_tensor(dBu[s % 4][:, :], du[c][:, :], b_s[n % 4][:, :], ALU.mult).then_inc(dBu_done, 1)

                one_pass(0)
                with pool.Fori(1, G) as g:
                    one_pass(g)

            @block.vector
            def _(dve):
                for i in range(2):
                    dve.memset(dA_b[i][:, :], 0.0).then_inc(dA_zeroed, 1)

                def steps(g, numbers, live):
                    for s in numbers:
                        if live(s):
                            wait(dve, dA_done, g * NUNITS + s + 1)
                            wait(dve, dBu_done, g * NUNITS + s + 1)
                            wait(dve, hc_done, g * NUNITS + s - 3)
                            dve.tensor_tensor_scan(h[s % 4][:, :], dA_b[s % 2][:, :], dBu[s % 4][:, :], 0.0, ALU.mult, ALU.add).then_inc(h_done, 1)
                        k = s - 1
                        if live(k):
                            n = (k % NUNITS) // DC
                            wait(dve, h_done, g * NUNITS + k + 1)
                            wait(dve, c_done, g * NS + k // DC + 1)
                            wait(dve, y_done, g * NUNITS + k - 7)
                            dve.tensor_tensor(hc[k % 8][:, :], h[k % 4][:, :], c_b[n % 2][:, :], ALU.mult).then_inc(hc_done, 1)
                        if s == LAG + 1 and live(-1):
                            for c in range(DC):
                                wait(dve, y_done, g * NUNITS - DC + c + 1)
                                dve.scalar_tensor_tensor(ysum[c][:, :], u[:, c, cols(g - 1)], skip[:, c:c + 1], y_b[c][:, :],
                                                         ALU.mult, ALU.add).then_inc(y_evac, 1)
                            for c in range(DC):
                                wait(dve, y_evac, (g - 1) * DC + c + 1)
                                dve.tensor_tensor(yz[:, c, cols(g - 1)], ysum[c][:, :], sres[:, c, cols(g - 1)], ALU.mult).then_inc(y_skip, 1)

                passes(dve, steps)

        (m_done, m_copied, f1_done, gelu_done, f2_done, c_summed, stat_done, moments, mean_done, mean_copied, dev_step, var_done,
         var_copied, std_done, rstd_done, c_normed, c_trans, added) = prog.semaphores(
            "md", "m_done m_copied f1_done gelu_done f2_done c_summed stat_done moments mean_done mean_copied dev_step var_done "
                  "var_copied std_done rstd_done c_normed c_trans added")
        with ExitStack() as inner:
            sbi, bank = buffers(nc, inner, "md")
            m_b = [bank(f"m{i}") for i in range(2)]
            f_b = [bank(f"f{i}") for i in range(4)]
            o_b = bank("o")
            s_b = bank("s")
            mT = [sbi(f"mT{i}", [P, BANK]) for i in range(2)]
            gl = [[sbi(f"gl{i}{c}", [P, BANK]) for c in range(HC)] for i in range(2)]
            cT = sbi("cT", [P, B, S])
            cn = sbi("cn", [P, NT, P])
            stats = sbi("stats", [P, B, 6])
            mom = sbi("mom", [P, B, 2])
            mean = sbi("mean", [P, B])
            dev = sbi("dev", [P, B])
            dev2 = sbi("dev2", [P, B])
            part_var = sbi("part_var", [P, B])
            var = sbi("var", [P, B])
            std = sbi("std", [P, B])
            rstd = sbi("rstd", [P, B])
            block = inner.enter_context(nc.Block())

            @block.tensor
            def _(pe):
                def out_proj(g):
                    wait(pe, m_copied, g - 1)
                    for c in range(DC):
                        last = pe.matmul(m_b[g % 2][:, :], w_out[:, c, :], yz[:, c, g * BANK:(g + 1) * BANK],
                                         start=(c == 0), stop=(c == DC - 1))
                    last.then_inc(m_done, 1)

                out_proj(0)
                for g in range(G):
                    pe.wait_ge(m_copied, g + 1)
                    for c in range(HC):
                        wait(pe, gelu_done, (g - 1) * HC + c + 1)
                        pe.matmul(f_b[c][:, :], f_w1[:, c * P:(c + 1) * P], mT[g % 2][:, :], start=True, stop=True).then_inc(f1_done, 1)
                    if g + 1 < G:
                        out_proj(g + 1)
                    wait(pe, c_summed, g)
                    for c in range(HC):
                        pe.wait_ge(gelu_done, g * HC + c + 1)
                        last = pe.matmul(o_b[:, :], f_w2[:, c, :], gl[g % 2][c][:, :], start=(c == 0), stop=(c == HC - 1))
                    last.then_inc(f2_done, 1)
                pe.wait_ge(moments, B)
                pe.matmul(s_b[:, 0:B], prog.inv_p[:, :], mom[:, :, 0], start=True, stop=True).then_inc(mean_done, 1)
                pe.wait_ge(dev_step, 3)
                pe.wait_ge(mean_copied, 1)
                pe.matmul(s_b[:, B:2 * B], prog.inv_p[:, :], part_var[:, :], start=True, stop=True).then_inc(var_done, 1)
                for t in range(NT):
                    pe.wait_ge(c_normed, t // QT + 1)
                    pe.transpose(f_b[t // 4][:, (t % 4) * P:(t % 4 + 1) * P], cn[:, t, :], ident[:, :]).then_inc(c_trans, 1)

            @block.scalar
            def _(act):
                for g in range(G):
                    act.wait_ge(m_done, g + 1)
                    wait(act, f1_done, (g - 1) * HC)
                    wait(act, c_summed, g - 1)
                    act.activation(mT[g % 2][:, :], m_b[g % 2][:, :], ACT.Copy).then_inc(m_copied, 1)
                    for c in range(HC):
                        act.wait_ge(f1_done, g * HC + c + 1)
                        wait(act, f2_done, g - 1)
                        act.activation(gl[g % 2][c][:, :], f_b[c][:, :], ACT.Gelu, bias=f_b1[:, c:c + 1]).then_inc(gelu_done, 1)
                act.wait_ge(var_copied, 1)
                act.activation(std[:, :], var[:, :], ACT.Sqrt).then_inc(std_done, 1)

            @block.vector
            def _(dve):
                for g in range(G):
                    dve.wait_ge(f2_done, g + 1)
                    dve.wait_ge(m_copied, g + 1)
                    dve.scalar_tensor_tensor(cT[:, g * GS:(g + 1) * GS, :].rearrange("p a s -> p (a s)"), o_b[:, :], f_b2[:, 0:1],
                                             mT[g % 2][:, :], ALU.add, ALU.add).then_inc(c_summed, 1)
                    dve.wait_ge(c_summed, g + 1)
                    for b in range(g * GS, (g + 1) * GS):
                        dve.bn_stats(stats[:, b, :], cT[:, b, :]).then_inc(stat_done, 1)
                    for b in range(g * GS, (g + 1) * GS):
                        dve.wait_ge(stat_done, b + 1)
                        dve.bn_aggr(mom[:, b, :], stats[:, b, :]).then_inc(moments, 1)
                dve.wait_ge(mean_done, 1)
                dve.tensor_copy(mean[:, :], s_b[:, 0:B]).then_inc(mean_copied, 1)
                dve.wait_ge(mean_copied, 1)
                dve.tensor_tensor(dev[:, :], mom[:, :, 0], mean[:, :], ALU.subtract).then_inc(dev_step, 1)
                dve.wait_ge(dev_step, 1)
                dve.tensor_tensor(dev2[:, :], dev[:, :], dev[:, :], ALU.mult).then_inc(dev_step, 1)
                dve.wait_ge(dev_step, 2)
                dve.tensor_tensor(part_var[:, :], dev2[:, :], mom[:, :, 1], ALU.add).then_inc(dev_step, 1)
                dve.wait_ge(var_done, 1)
                dve.tensor_scalar(var[:, :], s_b[:, B:2 * B], EPS, None, ALU.add).then_inc(var_copied, 1)
                dve.wait_ge(std_done, 1)
                dve.reciprocal(rstd[:, :], std[:, :]).then_inc(rstd_done, 1)
                dve.wait_ge(rstd_done, 1)
                for b in range(B):
                    dve.tensor_scalar(cn[:, b * QT:(b + 1) * QT, :].rearrange("p q s -> p (q s)"), cT[:, b, :], mean[:, b:b + 1],
                                      rstd[:, b:b + 1], ALU.subtract, ALU.mult).then_inc(c_normed, 1)
                for q in range(4):
                    dve.wait_ge(c_trans, 4 * (q + 1))
                    xs = x[:, q * 4:(q + 1) * 4, :].rearrange("p t c -> p (t c)")
                    dve.tensor_tensor(xs, xs, f_b[q][:, :], ALU.add).then_inc(added, 1)


def program(nc, d, stop_after=None):
    with ExitStack() as stack:
        prog = Program(nc)
        sb, _ = buffers(nc, stack, "g")
        prog.x = sb("x", [P, NT, P])
        prog.xn = sb("xn", [P, NT, P])
        prog.xnT = sb("xnT", [P, NTOK])
        prog.ident = sb("ident", [P, P])
        prog.zeros = sb("zeros", [P, 4 * P])
        prog.inv_p = sb("inv_p", [P, P])
        prog.ones_b = sb("ones_b", [P, P], BF16)
        prog.tri = sb("tri", [P, P], BF16)
        prog.route_consts = sb("route_consts", [P, 80])
        prog.phase(load_phase, d)
        prog.phase(norm_phase, "n1")
        prog.phase(attention_phase, d)
        if stop_after == "attention":
            return prog.phase(store_phase, d)
        prog.phase(norm_phase, "n2")
        prog.phase(experts_phase, d, "f1")
        if stop_after == "ffn1":
            return prog.phase(store_phase, d)
        prog.phase(norm_phase, "n3")
        prog.phase(mamba_phase, d)
        if stop_after == "mamba":
            return prog.phase(store_phase, d)
        prog.phase(norm_phase, "n4")
        prog.phase(experts_phase, d, "f2")
        prog.phase(store_phase, d)


def store_phase(prog, d):
    (stored,) = prog.semaphores("st", "stored")
    with prog.nc.Block() as block:

        @block.sync
        def _(sp):
            for q in range(4):
                tiles = slice(q * 4, q * 4 + 4)
                sp.dma_start(d["out"].rearrange("(t p) c -> p t c", p=P)[:, tiles, :], prog.x[:, tiles, :]).then_inc(stored, 16)
            sp.wait_ge(stored, 64)


def layout(inputs):
    import numpy as np

    def a(name):
        return np.asarray(inputs[name])

    out = {"x": a("L0_attn_a_x").reshape(NTOK, P)}
    out["Wq"] = a("L0_attn_a_Wq")
    out["WkT"] = np.ascontiguousarray(a("L0_attn_a_Wk").T)
    out["WvT"] = np.ascontiguousarray(a("L0_attn_a_Wv").T)
    out["W_down"] = a("L0_attn_a_W_down_kv")
    out["W_up_k"] = a("L0_attn_a_W_up_k")
    out["W_up_v"] = a("L0_attn_a_W_up_v")
    out["Wo"] = a("L0_attn_a_Wo")
    out["gate_wT"] = np.ascontiguousarray(a("L0_ffn_gate_w").T)
    out["gate_b"] = a("L0_ffn_gate_b").reshape(1, E_N)
    w1 = a("L0_ffn_w1").transpose(0, 2, 1)
    w2 = a("L0_ffn_w2").transpose(0, 2, 1).reshape(E_N, HC, P, P).transpose(0, 2, 1, 3).reshape(E_N, P, HC * P)
    b1 = a("L0_ffn_b1").reshape(E_N, HC, P).transpose(0, 2, 1)
    b2 = a("L0_ffn_b2").reshape(E_N, P, 1)
    out["experts"] = np.ascontiguousarray(np.concatenate([w1, w2, b1, b2], axis=2).reshape(E_N * P, HID + HC * P + HC + 1))
    def halves(m):
        return np.ascontiguousarray(m.reshape(DC, P, -1).transpose(1, 0, 2))

    out["in_projT"] = np.ascontiguousarray(a("L0_attn_b_in_proj_w").T)
    out["conv_w"] = halves(a("L0_attn_b_conv_w").reshape(DI, 4))
    out["conv_b"] = halves(a("L0_attn_b_conv_b")).reshape(P, DC)
    out["x_projT"] = halves(a("L0_attn_b_x_proj_w").T)
    out["dt_projT"] = np.ascontiguousarray(a("L0_attn_b_dt_proj_w").T)
    out["dt_b"] = halves(a("L0_attn_b_dt_proj_b")).reshape(P, DC)
    out["A_log"] = halves(a("L0_attn_b_A_log"))
    out["D"] = halves(a("L0_attn_b_D")).reshape(P, DC)
    out["out_projT"] = halves(a("L0_attn_b_out_proj_w").T)
    out["ffn_w1T"] = np.ascontiguousarray(a("L0_attn_b_ffn_w1").T)
    out["ffn_b1"] = np.ascontiguousarray(a("L0_attn_b_ffn_b1").reshape(HC, P).T)
    out["ffn_w2T"] = np.ascontiguousarray(a("L0_attn_b_ffn_w2").T.reshape(HC, P, P).transpose(1, 0, 2))
    out["ffn_b2"] = a("L0_attn_b_ffn_b2").reshape(P, 1)
    pick = (np.arange(96)[:, None] % 32 == np.arange(32)[None, :])[:, :, None]
    out["c_pick"] = np.ascontiguousarray(np.broadcast_to(pick, (96, 32, P))).astype(np.uint16) * np.uint16(BF16_ONE)
    p, s = np.arange(P), np.arange(S)
    q = s.reshape(QT, P)
    distance = np.abs(q.T[:, :, None].astype(np.float32) - s[None, None, :].astype(np.float32))
    out["c_decay"] = np.exp(np.float32(-0.01 * 0.01) * distance).astype(np.float32)
    out["c_ident"] = np.eye(P, dtype=np.float32)
    out["c_headmask"] = (p[:, None] // HD == np.arange(HEADS)[None, :]).astype(np.float32)
    out["c_tri"] = (p[:, None] < p[None, :]).astype(np.uint16) * np.uint16(BF16_ONE)
    route = np.zeros((P, 80), np.float32)
    route[:, R_LESS:R_LESS + E_N] = np.arange(E_N) - E_N
    route[:, R_THRESH:R_THRESH + NT] = np.arange(NT) * P
    route[:, R_TILE:R_TILE + SLOT_TILES] = np.arange(SLOT_TILES)
    route[:, R_PART] = p
    route[:, R_ONES:] = 1.0
    out["c_route"] = route
    return out


def scratch(nc, d):
    d["sorted_x"] = nc.dram_tensor("sorted_x", (SLOT_TILES * P, P), F32, kind="Internal").ap()
    d["sorted_y"] = nc.dram_tensor("sorted_y", (SLOT_TILES * P, P), F32, kind="Internal").ap()
    return d


def kernel(**inputs):
    import concourse.bacc as bacc
    from concourse.bass_utils import run_bass_kernel_spmd

    nc = bacc.Bacc("TRN2", target_bir_lowering=False, num_devices=1)
    arrays = layout(inputs)
    d = {name: nc.dram_tensor(name, a.shape, mybir.dt.from_np(a.dtype), kind="ExternalInput").ap() for name, a in arrays.items()}
    d["out"] = nc.dram_tensor("out", (NTOK, P), F32, kind="ExternalOutput").ap()
    program(nc, scratch(nc, d))
    result = run_bass_kernel_spmd(nc, [arrays], core_ids=[0])
    return result.results[0]["out"].reshape(B, S, P)
```

```python
from contextlib import ExitStack

import concourse.bass as bass
from concourse import mybir

F32 = mybir.dt.float32
BF16 = mybir.dt.bfloat16
U32 = mybir.dt.uint32
BF16_ONE = 0x3F80
ALU = mybir.AluOpType
ACT = mybir.ActivationFunctionType
AX = mybir.AxisListType

P = 128
B, S = 8, 256
NTOK = B * S
NT = NTOK // P
QT = S // P
HEADS, HD = 16, 8
GROUPS, GH = 4, 4
CLAMP = 10000.0
EPS = 1e-5
BANK = 512
E_N, HID = 8, 512
HC = HID // P
XW = P + 1
EW = 2 * HID + HID // P + P
SLOT_TILES = 24
DI, NS, DTR = 256, 16, 64
DC = DI // P


class Program:

    def __init__(self, nc):
        self.nc, self.held = nc, []

    def phase(self, build, *args):
        build(self, *args)
        self.nc.clear_and_free_semaphores(self.held)
        self.nc.all_engine_barrier()
        self.held = []

    def sem(self, name):
        self.held.append(self.nc.alloc_semaphore(name))
        return self.held[-1]

    def semaphores(self, prefix, names):
        return [self.sem(f"{prefix}_{n}") for n in names.split()]


def buffers(nc, stack, prefix):
    def sb(name, shape, dtype=F32):
        return stack.enter_context(nc.sbuf_tensor(f"{prefix}_{name}", shape, dtype))

    def bank(name, dtype=F32):
        return stack.enter_context(nc.psum_tensor(f"{prefix}_{name}", [P, BANK], dtype))

    return sb, bank


def load_phase(prog, d):
    nc = prog.nc
    (loaded, filled, numbered) = prog.semaphores("ld", "loaded filled numbered")
    with nc.Block() as block:

        @block.sync
        def _(sp):
            for q in range(4):
                tiles = slice(q * 4, q * 4 + 4)
                sp.dma_start(prog.x[:, tiles, :], d["x"].rearrange("(t p) c -> p t c", p=P)[:, tiles, :]).then_inc(loaded, 16)
            sp.dma_start(prog.ident[:, :], d["c_ident"]).then_inc(loaded, 16)
            sp.dma_start(prog.route_consts[:, :], d["c_route"]).then_inc(loaded, 16)
            sp.dma_start(prog.tri[:, :], d["c_tri"].bitcast(BF16)).then_inc(loaded, 16)
            sp.wait_ge(loaded, 16 * 7)

        @block.gpsimd
        def _(pool):
            pool.memset(prog.ones_b[:, :], 1.0).then_inc(filled, 1)
            pool.memset(prog.inv_p[:, :], 1.0 / P).then_inc(filled, 1)
            pool.wait_ge(loaded, 16 * 7)
            pool.tensor_copy(prog.xn[:, :, P], prog.route_consts[:, R_TOKEN:R_TOKEN + NT]).then_inc(numbered, 1)


def norm_phase(prog, tag):
    nc = prog.nc
    x, xn, xnT = prog.x, prog.xn, prog.xnT
    (stats_done, moments_done, std_done, rstd_step, normed, transposed, evac_a, evac_v) = prog.semaphores(
        tag, "stats_done moments_done std_done rstd_step normed transposed evac_a evac_v")
    with ExitStack() as stack:
        sb, bank = buffers(nc, stack, tag)
        stats = sb("stats", [P, NT, 6])
        mom = sb("mom", [P, NT, 2])
        var = sb("var", [P, NT])
        std = sb("std", [P, NT])
        r = sb("r", [P, NT])
        r2 = sb("r2", [P, NT])
        r3 = sb("r3", [P, NT])
        tb = [bank(f"tb{i}") for i in range(4)]
        block = stack.enter_context(nc.Block())

        @block.vector
        def _(dve):
            for t in range(NT):
                dve.bn_stats(stats[:, t, :], x[:, t, :]).then_inc(stats_done, 1)
            for t in range(NT):
                dve.wait_ge(stats_done, t + 1)
                dve.bn_aggr(mom[:, t, :], stats[:, t, :]).then_inc(moments_done, 1)
            dve.wait_ge(moments_done, NT)
            dve.tensor_scalar(var[:, :], mom[:, :, 1], EPS, None, ALU.add).then_inc(moments_done, 1)
            dve.wait_ge(std_done, 1)
            dve.reciprocal(r[:, :], std[:, :]).then_inc(rstd_step, 1)
            dve.wait_ge(rstd_step, 1)
            dve.tensor_tensor(r2[:, :], r[:, :], r[:, :], ALU.mult).then_inc(rstd_step, 1)
            dve.wait_ge(rstd_step, 2)
            dve.tensor_tensor(r3[:, :], r2[:, :], var[:, :], ALU.mult).then_inc(rstd_step, 1)
            dve.wait_ge(rstd_step, 3)
            dve.tensor_scalar(r2[:, :], r3[:, :], -0.5, 1.5, ALU.mult, ALU.add).then_inc(rstd_step, 1)
            dve.wait_ge(rstd_step, 4)
            dve.tensor_tensor(r3[:, :], r2[:, :], r[:, :], ALU.mult).then_inc(rstd_step, 1)
            dve.wait_ge(rstd_step, 5)
            for t in range(NT):
                dve.tensor_scalar(xn[:, t, 0:P], x[:, t, :], mom[:, t, 0:1], r3[:, t:t + 1],
                                  ALU.subtract, ALU.mult).then_inc(normed, 1)
            for q in (1, 3):
                dve.wait_ge(transposed, 4 * (q + 1))
                dve.tensor_copy(xnT[:, q * BANK:(q + 1) * BANK], tb[q][:, :]).then_inc(evac_v, 1)

        @block.tensor
        def _(pe):
            for t in range(NT):
                pe.wait_ge(normed, t + 1)
                pe.transpose(tb[t // 4][:, (t % 4) * P:(t % 4 + 1) * P], xn[:, t, 0:P], prog.ident[:, :]).then_inc(transposed, 1)

        @block.scalar
        def _(act):
            act.wait_ge(moments_done, NT + 1)
            act.activation(std[:, :], var[:, :], ACT.Sqrt).then_inc(std_done, 1)
            for q in (0, 2):
                act.wait_ge(transposed, 4 * (q + 1))
                act.activation(xnT[:, q * BANK:(q + 1) * BANK], tb[q][:, :], ACT.Copy).then_inc(evac_a, 1)


def wait(engine, semaphore, value):
    if not isinstance(value, int) or value > 0:
        engine.wait_ge(semaphore, value)


def attention_phase(prog, d):
    nc = prog.nc
    x, xnT, ident = prog.x, prog.xnT, prog.ident
    SCALE = 1.0 / (128.0 ** 0.5 + 1e-08)
    H = HEADS
    ROWS = 9 * HD
    with ExitStack() as stack:
        sb, bank = buffers(nc, stack, "at")
        wq = sb("wq", [P, P])
        wkvT = sb("wkvT", [P, P])
        wvT = sb("wvT", [P, P])
        wdown = sb("wdown", [P, 32])
        wup = sb("wup", [32, 2, P])
        wo = sb("wo", [P, P])
        decay = sb("decay", [P, QT, S])
        downT = sb("downT", [32, P])
        wkv_eff = sb("wkv_eff", [P, 2, P])
        whole = [sb(f"whole{i}", [P, BANK]) for i in range(4)]
        rest = [sb(f"rest{i}", [P, BANK]) for i in range(4)]
        parts = [[sb(f"part{a}{i}", [P, NTOK], BF16) for i in range(3)] for a in "qk"]
        stack_q = [sb(f"stack_q{i}", [ROWS, HEADS, S], BF16) for i in range(2)]
        stack_k = [sb(f"stack_k{i}", [ROWS, HEADS, S], BF16) for i in range(2)]
        v = sb("v", [P, NT, P])
        vaug = sb("vaug", [P, QT, HEADS, 32])
        sc = [sb(f"sc{i}", [P, BANK]) for i in range(4)]
        sd = [sb(f"sd{i}", [P, BANK]) for i in range(4)]
        rowmax = sb("rowmax", [P, HEADS, QT])
        negmax = sb("negmax", [P, HEADS, QT])
        pr = [sb(f"pr{i}", [P, BANK]) for i in range(4)]
        prT = [sb(f"prT{i}", [P, BANK]) for i in range(8)]
        oT = sb("oT", [P, S])
        rden = sb("rden", [P, QT, GH])
        on = sb("on", [P, QT, P])
        onT = sb("onT", [P, S])
        spare = sb("spare", [P, SLOT_TILES, XW])
        score_b = [bank(f"score{i}") for i in range(2)]
        trans_b = [bank(f"trans{i}") for i in range(2)]
        out_b = [bank(f"out{i}") for i in range(2)]
        quad_b = bank("quad")
        misc_b = bank("misc")
        proj_b = [*score_b, *trans_b]

        (wloaded, wsum, eff_step, eff_evac, vones, projected_in, evac_a, evac_v, high_done, rest_done, middle_done,
         low_done, written, spare_ready) = prog.semaphores(
            "atw", "wloaded wsum eff_step eff_evac vones projected_in evac_a evac_v high_done rest_done middle_done low_done written spare_ready")
        with nc.Block() as block:
            FILLS = 2 * NTOK // BANK + NT // 4

            @block.sync
            def _(sp):
                for dst, src in ((wkvT[:, :], d["WkT"]), (wvT[:, :], d["WvT"]), (wdown[:, :], d["W_down"]),
                                 (wup[:, 0, :], d["W_up_k"]), (wup[:, 1, :], d["W_up_v"]), (wq[:, :], d["Wq"]), (wo[:, :], d["Wo"]),
                                 (decay[:, :, :], d["c_decay"])):
                    sp.dma_start(dst, src).then_inc(wloaded, 16)
                for f in range(8):
                    for i, (done, level) in enumerate(((high_done, f + 1), (middle_done, f + 1), (low_done, f + 1))):
                        sp.wait_ge(done, level)
                        b = f // 2 * 2
                        sp.dma_start(d["parts"][f % 2, b:b + 2, i * P:(i + 1) * P, :].rearrange("b p s -> p b s"),
                                     parts[f % 2][i][:, (f // 2) * BANK:(f // 2 + 1) * BANK].rearrange("p (b s) -> p b s", b=2),
                                     ).then_inc(written, 16)
                sp.wait_ge(written, 16 * 24)

            @block.gpsimd
            def _(pool):
                pool.memset(spare[:, :, 0:P], 0.0).then_inc(spare_ready, 1)
                pool.tensor_copy(spare[:, :, P], prog.route_consts[:, R_SPARE:R_SPARE + SLOT_TILES]).then_inc(spare_ready, 1)
                pool.memset(vaug[:, :, :, :], 0.0).then_inc(vones, 1)
                pool.wait_ge(vones, 1)
                pool.memset(vaug[:, :, :, HD:HD + 1], 1.0).then_inc(vones, 1)
                for f in range(8):
                    pool.wait_ge(middle_done, f + 1)
                    _, middle, low = parts[f % 2]
                    cols = slice((f // 2) * BANK, (f // 2 + 1) * BANK)
                    pool.tensor_tensor(low[:, cols], rest[f % 4][:, :], middle[:, cols], ALU.subtract).then_inc(low_done, 1)

            @block.vector
            def _(dve):
                dve.wait_ge(wloaded, 16 * 8)
                dve.tensor_tensor(wkvT[:, :], wkvT[:, :], wvT[:, :], ALU.add).then_inc(wsum, 1)
                dve.wait_ge(eff_step, 1)
                dve.tensor_copy(downT[:, :], misc_b[0:32, 0:P]).then_inc(eff_evac, 1)
                dve.wait_ge(eff_step, 2)
                dve.tensor_copy(wkv_eff[:, :, :], quad_b[:, 0:2 * P].rearrange("p (a c) -> p a c", a=2)).then_inc(eff_evac, 1)

                def split(f):
                    cols = slice((f // 2) * BANK, (f // 2 + 1) * BANK)
                    high, middle, _ = parts[f % 2]
                    dve.wait_ge(evac_v if f % 2 else evac_a, f // 2 + 1)
                    dve.tensor_copy(high[:, cols], whole[f % 4][:, :]).then_inc(high_done, 1)
                    dve.wait_ge(high_done, f + 1)
                    wait(dve, low_done, f - 3)
                    dve.tensor_tensor(rest[f % 4][:, :], whole[f % 4][:, :], high[:, cols], ALU.subtract).then_inc(rest_done, 1)
                    dve.wait_ge(rest_done, f + 1)
                    dve.tensor_copy(middle[:, cols], rest[f % 4][:, :]).then_inc(middle_done, 1)

                for f in range(1, FILLS, 2):
                    dve.wait_ge(projected_in, f + 1)
                    if f < 8:
                        dst = whole[f % 4][:, :]
                        wait(dve, rest_done, f - 3)
                    else:
                        dst = v[:, (f - 8) * 4:(f - 7) * 4, :].rearrange("p t c -> p (t c)")
                    dve.tensor_copy(dst, proj_b[f % 4][:, :]).then_inc(evac_v, 1)
                    if f < 8:
                        split(f - 1)
                        split(f)

            @block.tensor
            def _(pe):
                pe.wait_ge(wsum, 1)
                pe.matmul(misc_b[0:32, 0:P], wdown[:, :], wkvT[:, :], start=True, stop=True).then_inc(eff_step, 1)
                pe.wait_ge(eff_evac, 1)
                pe.matmul(quad_b[:, 0:2 * P], downT[:, :], wup[:, :, :].rearrange("p a c -> p (a c)"),
                          start=True, stop=True).then_inc(eff_step, 1)
                pe.wait_ge(eff_evac, 2)
                for f in range(FILLS):
                    if f >= 4:
                        pe.wait_ge(evac_v if f % 2 else evac_a, (f - 4) // 2 + 1)
                    if f < 8:
                        w = wkv_eff[:, 0, :] if f % 2 else wq[:, :]
                        pe.matmul(proj_b[f % 4][:, :], w, xnT[:, (f // 2) * BANK:(f // 2 + 1) * BANK],
                                  start=True, stop=True).then_inc(projected_in, 1)
                    else:
                        for t in range(4):
                            tok = ((f - 8) * 4 + t) * P
                            last = pe.matmul(proj_b[f % 4][:, t * P:(t + 1) * P], xnT[:, tok:tok + P], wkv_eff[:, 1, :],
                                             start=True, stop=True)
                        last.then_inc(projected_in, 1)

            @block.scalar
            def _(act):
                for f in range(0, FILLS, 2):
                    act.wait_ge(projected_in, f + 1)
                    if f < 8:
                        wait(act, rest_done, f - 3)
                        act.activation(whole[f % 4][:, :], proj_b[f % 4][:, :], ACT.Copy, scale=SCALE).then_inc(evac_a, 1)
                    else:
                        act.activation(v[:, (f - 8) * 4:(f - 7) * 4, :].rearrange("p t c -> p (t c)"), proj_b[f % 4][:, :],
                                       ACT.Copy).then_inc(evac_a, 1)

        (stacked, spare_written, vaug_ready, scored, clipped, decayed, negated, exped, ptrans, pt_ready, attended, ot_ready,
         ot_trans, rden_ready, normed, on_trans, ont_ready, projected, added) = prog.semaphores(
            "at", "stacked spare_written vaug_ready scored clipped decayed negated exped ptrans pt_ready attended ot_ready "
                  "ot_trans rden_ready normed on_trans ont_ready projected added")
        block = stack.enter_context(nc.Block())
        LAST_STEP = 16

        def sequences(engine, steps):
            steps(0, range(H), lambda n: n >= 0, 0)
            with engine.Fori(1, B - 1, 2) as b:
                for half in (1, 0):
                    steps(b + 1 - half, range(H), lambda n: True, half)
            steps(B - 1, range(H), lambda n: True, (B - 1) % 2)
            steps(B, range(LAST_STEP), lambda n: n < 0, 0)

        NSTACK = 4

        @block.sync
        def _(sp):
            def stack_up(b, half):
                wait(sp, scored, b * H - H)
                wait(sp, stacked, b * NSTACK * 16)
                q_parts, k_parts = (d["parts"][a, bass.ds(b, 1), :, :].rearrange("b (r h) s -> (b r) (h s)", h=H) for a in (0, 1))
                for i in range(3):
                    sp.dma_start(stack_q[half][i * 3 * HD:(i + 1) * 3 * HD, :, :].rearrange("p h s -> p (h s)"),
                                 q_parts[i * HD:(i + 1) * HD, :].unsqueeze(0).to_broadcast([3, HD, H * S])).then_inc(stacked, 16)
                sp.dma_start(stack_k[half][:, :, :].rearrange("p h s -> p (h s)"),
                             k_parts.unsqueeze(0).to_broadcast([3, 3 * HD, H * S])).then_inc(stacked, 16)

            stack_up(0, 0)
            stack_up(1, 1)
            with sp.Fori(2, B - 1, 2) as b:
                for half in (0, 1):
                    stack_up(b + half, half)
            for tag in ("f1", "f2"):
                sp.dma_start(d["sorted_x_" + tag].rearrange("(j p) c -> p j c", p=P), spare[:, :, :]).then_inc(spare_written, 16)
            sp.wait_ge(spare_written, 32)

        @block.tensor
        def _(pe):
            def steps(b, numbers, live, half):
                for s in numbers:
                    if live(s):
                        if s == 0:
                            wait(pe, stacked, (b + 1) * NSTACK * 16)
                        wait(pe, clipped, b * H + s - 1)
                        for q in range(QT):
                            last = pe.matmul(score_b[s % 2][:, q * S:(q + 1) * S], stack_q[half][:, s, q * P:(q + 1) * P],
                                             stack_k[half][:, s, :], start=True, stop=True)
                        last.then_inc(scored, 1)
                    n = s - 4
                    if live(n):
                        wait(pe, exped, (b * H + n + 1) * QT)
                        wait(pe, pt_ready, b * H + n - 1)
                        for k in range(QT):
                            for q in range(QT):
                                last = pe.transpose(trans_b[n % 2][:, k * S + q * P:k * S + (q + 1) * P],
                                                    pr[n % 4][:, q * S + k * P:q * S + (k + 1) * P], ident[:, :])
                        last.then_inc(ptrans, 1)
                    g, at = (s - 9) // GH, (s - 9) % GH == 0
                    if at and live(g):
                        wait(pe, pt_ready, b * H + (g + 1) * GH)
                        wait(pe, vaug_ready, b * GROUPS + g + 1)
                        wait(pe, ot_ready, b * GROUPS + g - 1)
                        for k in range(QT):
                            for j in range(GH):
                                h = (g * GH + j) % H
                                last = pe.matmul(out_b[g % 2][32 * j:32 * j + 32, 0:S], vaug[:, k, h, :],
                                                 prT[h % 8][:, k * S:(k + 1) * S], start=(k == 0), stop=(k == QT - 1))
                        last.then_inc(attended, 1)
                    g, at = (s - 12) // GH, (s - 12) % GH == 0
                    if at and live(g):
                        wait(pe, ot_ready, b * GROUPS + g + 1)
                        wait(pe, normed, b * GROUPS + g)
                        for q in range(QT):
                            last = pe.transpose(quad_b[:, q * P:(q + 1) * P], oT[:, q * P:(q + 1) * P], ident[:, :])
                        last.then_inc(ot_trans, 1)
                    if s == 12 and live(-1):
                        wait(pe, normed, b * GROUPS)
                        for q in range(QT):
                            last = pe.transpose(misc_b[:, q * P:(q + 1) * P], on[:, q, :], ident[:, :])
                        last.then_inc(on_trans, 1)
                    if s == 15 and live(-1):
                        wait(pe, ont_ready, b)
                        for q in range(QT):
                            last = pe.matmul(misc_b[:, q * P:(q + 1) * P], onT[:, q * P:(q + 1) * P], wo[:, :],
                                             start=True, stop=True)
                        last.then_inc(projected, 1)

            sequences(pe, steps)

        @block.vector
        def _(dve):
            def steps(b, numbers, live, half):
                for s in numbers:
                    if live(s):
                        wait(dve, scored, b * H + s + 1)
                        dve.tensor_scalar(sc[s % 4][:, :], score_b[s % 2][:, :], -CLAMP, CLAMP, ALU.max, ALU.min).then_inc(clipped, 1)
                    n = s - 1
                    if live(n):
                        wait(dve, clipped, b * H + n + 1)
                        wait(dve, exped, (b * H + n - 3) * QT)
                    n = s - 2
                    if live(n):
                        wait(dve, decayed, (b * H + n + 1) * QT)
                        dve.tensor_scalar(negmax[:, n % H, :], rowmax[:, n % H, :], -1.0, None, ALU.mult).then_inc(negated, 1)
                    n = s - 1
                    if live(n):
                        for q in range(QT):
                            dve.tensor_tensor_reduce(
                                out=sd[n % 4][:, q * S:(q + 1) * S], in0=sc[n % 4][:, q * S:(q + 1) * S], in1=decay[:, q, :],
                                scale=1.0, scalar=-3.0e38, op0=ALU.mult, op1=ALU.max,
                                accum_out=rowmax[:, n % H, q:q + 1]).then_inc(decayed, 1)
                    g, at = (s - 14) // GH, (s - 14) % GH == 0
                    if at and live(g):
                        wait(dve, ot_trans, b * GROUPS + g + 1)
                        if g >= 0:
                            wait(dve, on_trans, b)
                        heads = quad_b[:, 0:QT * P].rearrange("p (q j c) -> p q j c", q=QT, j=GH)
                        dve.reciprocal(rden[:, :, :], heads[:, :, :, HD]).then_inc(rden_ready, 1)
                        wait(dve, rden_ready, b * GROUPS + g + 1)
                        for q in range(QT):
                            last = dve.tensor_tensor(on[:, q, (g % GROUPS) * 32:(g % GROUPS + 1) * 32].rearrange("p (j c) -> p j c", j=GH),
                                                     heads[:, q, :, 0:HD],
                                                     rden[:, q, :].unsqueeze(2).to_broadcast([P, GH, HD]), ALU.mult)
                        last.then_inc(normed, 1)
                    if s == 15 and live(-1):
                        wait(dve, projected, b)
                        xs = x[:, bass.ds(b * QT - QT, QT), :]
                        dve.tensor_tensor(xs, misc_b[:, 0:QT * P].rearrange("p (q c) -> p q c", q=QT), xs, ALU.add).then_inc(added, 1)

            sequences(dve, steps)

        @block.gpsimd
        def _(pool):
            def sequence(b, first):
                for g in range(GROUPS):
                    if not first:
                        pool.wait_ge(attended, b * GROUPS - GROUPS + g + 1)
                    pool.tensor_copy(vaug[:, :, g * GH:(g + 1) * GH, 0:HD],
                                     v[:, bass.ds(b * QT, QT), g * 32:(g + 1) * 32].rearrange("p q (j c) -> p q j c", j=GH),
                                     ).then_inc(vaug_ready, 1)

            sequence(0, True)
            with pool.Fori(1, B) as b:
                sequence(b, False)

        @block.scalar
        def _(act):
            def steps(b, numbers, live, half):
                for s in numbers:
                    if live(s):
                        wait(act, ptrans, b * H + s - 3)
                        wait(act, negated, b * H + s + 1)
                        for q in range(QT):
                            act.activation(pr[s % 4][:, q * S:(q + 1) * S], sd[s % 4][:, q * S:(q + 1) * S], ACT.Exp,
                                           bias=negmax[:, s, q:q + 1]).then_inc(exped, 1)
                    n = s - 2
                    if live(n):
                        wait(act, ptrans, b * H + n + 1)
                        wait(act, attended, b * GROUPS + n // GH - 1)
                        act.activation(prT[n % 8][:, :], trans_b[n % 2][:, :], ACT.Copy).then_inc(pt_ready, 1)
                    g, at = (s - 8) // GH, (s - 8) % GH == 0
                    if at and live(g):
                        wait(act, attended, b * GROUPS + g + 1)
                        wait(act, ot_trans, b * GROUPS + g)
                        act.activation(oT[:, :], out_b[g % 2][:, 0:S], ACT.Copy).then_inc(ot_ready, 1)
                    if s == 11 and live(-1):
                        wait(act, on_trans, b)
                        act.activation(onT[:, :], misc_b[:, 0:S], ACT.Copy).then_inc(ont_ready, 1)

            sequences(act, steps)


R_LESS, R_THRESH, R_TILE, R_ONES, R_TOKEN, R_SPARE, R_END = 0, 8, 24, 48, 64, 80, 104


def experts_phase(prog, d, tag):
    nc = prog.nc
    x, xn, xnT, ident, rc = prog.x, prog.xn, prog.xnT, prog.ident, prog.route_consts
    U = 8
    B1, B2 = 2 * HID, 2 * HID + HC
    with ExitStack() as stack:
        sb, bank = buffers(nc, stack, tag)
        gw = sb("gw", [P, E_N])
        gb = sb("gb", [P, E_N])
        logits = sb("logits", [P, NT, E_N])
        best = sb("best", [P, NT])
        work = sb("work", [P, NT, E_N])
        first = sb("first", [P, NT])
        onehot = sb("onehot", [P, NT, E_N], BF16)
        upto = sb("upto", [P, E_N, NT])
        over = sb("over", [P, E_N, NT])
        tiles = sb("tiles", [P, E_N])
        tile_end = sb("tile_end", [P, E_N])
        tile_start = sb("tile_start", [P, E_N])
        slot_f = sb("slot_f", [P, NT])
        slot = sb("slot", [P, NT], U32)
        before = sb("before", [P, SLOT_TILES, E_N])
        owner_f = sb("owner_f", [P, SLOT_TILES])
        owner = sb("owner", [P, SLOT_TILES], U32)
        sorted_sb = sb("sorted_sb", [P, SLOT_TILES, XW])
        sortedT = sb("sortedT", [P, SLOT_TILES * P])
        token = sb("token", [P, SLOT_TILES], U32)
        y_sorted = sb("y_sorted", [P, SLOT_TILES, P])
        y_tok = sb("y_tok", [P, NT, P])
        W = [sb(f"W{u}", [P, EW]) for u in range(U)]
        hT = [sb(f"hT{u}", [P, HC, P]) for u in range(4)]
        banks = [bank(f"b{i}") for i in range(8)]
        logit_b, rank_b = banks[4], banks[5]

        (loaded, logits_done, onehot_done, counted, slots_done, owners_done, chain, scattered, transposed, evac_a, evac_v,
         tokens_done, hidden_done, relu_a, relu_v, out_done, y_ready, y_scattered, added) = prog.semaphores(
            tag, "loaded logits_done onehot_done counted slots_done owners_done chain scattered transposed evac_a evac_v "
                 "tokens_done hidden_done relu_a relu_v out_done y_ready y_scattered added")
        GROUPS_T = SLOT_TILES // 4
        PASSES = SLOT_TILES // U
        QUARTER = NT // 4
        sorted_loaded = [prog.sem(f"{tag}_sorted_loaded{q}") for q in range(GROUPS_T)]
        fetched = [prog.sem(f"{tag}_fetched{u}") for u in range(U)]
        y_loaded = [prog.sem(f"{tag}_y_loaded{q}") for q in range(4)]
        sorted_x = d["sorted_x_" + tag]
        with nc.Block() as block:

            def passes(engine, steps):
                steps(0, range(U), lambda n: n >= 0)
                with engine.Fori(1, PASSES) as i:
                    steps(i, range(U), lambda n: True)
                steps(PASSES, range(1), lambda n: n < 0)

            @block.sync
            def _(sp):
                def fetch(i, u, first):
                    if not first:
                        sp.wait_ge(y_ready, i * U + (u - U + 1))
                    e = sp.value_load(owner[0:1, bass.ds(i * U + u, 1)], min_val=0, max_val=E_N - 1)
                    sp.dma_start(W[u][:, :], d["experts"][bass.ds(e * P, P), :]).then_inc(fetched[u], 16)

                sp.dma_start(gw[:, :], d["gate_wT"]).then_inc(loaded, 16)
                sp.dma_start(gb[:, :], d["gate_b"].to_broadcast([P, E_N])).then_inc(loaded, 16)
                sp.wait_ge(owners_done, 1)
                for u in range(U):
                    fetch(0, u, True)
                sp.wait_ge(scattered, 16 * NT)
                for q in range(GROUPS_T):
                    sp.dma_start(sorted_sb[:, q * 4:q * 4 + 4, :],
                                 sorted_x.rearrange("(j p) c -> p j c", p=P)[:, q * 4:q * 4 + 4, :]).then_inc(sorted_loaded[q], 16)
                with sp.Fori(1, PASSES) as i:
                    for u in range(U):
                        fetch(i, u, False)
                sp.wait_ge(y_scattered, 16 * SLOT_TILES)
                for q in range(4):
                    tiles = slice(q * QUARTER, (q + 1) * QUARTER)
                    sp.dma_start(y_tok[:, tiles, :],
                                 d["y_tok"][0:NTOK, :].rearrange("(t p) c -> p t c", p=P)[:, tiles, :]).then_inc(y_loaded[q], 16)

            @block.tensor
            def _(pe):
                pe.wait_ge(loaded, 32)
                for t in range(NT):
                    last = pe.matmul(logit_b[:, t * E_N:(t + 1) * E_N], xnT[:, t * P:(t + 1) * P], gw[:, :], start=True, stop=True)
                last.then_inc(logits_done, 1)
                pe.wait_ge(onehot_done, 1)
                oh = onehot[:, :, :].rearrange("p t e -> p (t e)")
                pe.matmul(rank_b[:, 0:NT * E_N], prog.tri[:, :], oh, start=True, stop=True)
                pe.matmul(rank_b[:, NT * E_N:2 * NT * E_N], prog.ones_b[:, :], oh, start=True, stop=True).then_inc(counted, 1)
                for q in range(GROUPS_T):
                    if q >= 4:
                        pe.wait_ge(evac_v if q % 2 else evac_a, (q - 4) // 2 + 1)
                    pe.wait_ge(sorted_loaded[q], 16)
                    for t in range(4):
                        last = pe.transpose(banks[q % 4][:, t * P:(t + 1) * P], sorted_sb[:, q * 4 + t, 0:P], ident[:, :])
                    last.then_inc(transposed, 1)
                pe.wait_ge(evac_a, GROUPS_T // 2)
                pe.wait_ge(evac_v, GROUPS_T // 2)

                def steps(i, numbers, live):
                    for s in numbers:
                        if live(s):
                            pe.wait_ge(fetched[s], (i + 1) * 16)
                            wait(pe, relu_a, i * U + s - 1)
                            wait(pe, relu_v, i * U + s - 1)
                            for c in range(HC):
                                last = pe.matmul(banks[(s % 2) * 2 + c // 2][:, (c % 2) * P:(c % 2 + 1) * P],
                                                 W[s][:, c * P:(c + 1) * P], sortedT[:, bass.ds((i * U + s) * P, P)],
                                                 start=True, stop=True)
                            last.then_inc(hidden_done, 1)
                        n = s - 1
                        if live(n):
                            u = n % U
                            wait(pe, relu_a, i * U + n + 1)
                            wait(pe, relu_v, i * U + n + 1)
                            wait(pe, y_ready, i * U + n - 1)
                            for c in range(HC):
                                last = pe.matmul(banks[4 + u % 2][:, 0:P], hT[u % 4][:, c, :], W[u][:, HID + c * P:HID + (c + 1) * P],
                                                 start=(c == 0), stop=(c == HC - 1))
                            last.then_inc(out_done, 1)

                passes(pe, steps)

            @block.vector
            def _(dve):
                links = [0]

                def link(instruction):
                    links[0] += 1
                    instruction.then_inc(chain, 1)
                    dve.wait_ge(chain, links[0])

                def over_e(a):
                    return a.unsqueeze(2).to_broadcast([P, a.shape[1], E_N])

                def over_t(a, n=NT):
                    return a.unsqueeze(1).to_broadcast([P, n, E_N])

                less = over_t(rc[:, R_LESS:R_LESS + E_N])
                dve.wait_ge(loaded, 32)
                dve.wait_ge(logits_done, 1)
                link(dve.tensor_tensor(logits[:, :, :], logit_b[:, 0:NT * E_N].rearrange("p (t e) -> p t e", e=E_N),
                                       over_t(gb[:, :]), ALU.add))
                link(dve.tensor_reduce(best[:, :], logits[:, :, :], AX.X, ALU.max))
                link(dve.tensor_tensor(work[:, :, :], logits[:, :, :], over_e(best[:, :]), ALU.is_equal))
                link(dve.tensor_tensor(work[:, :, :], work[:, :, :], less, ALU.mult))
                link(dve.tensor_reduce(first[:, :], work[:, :, :], AX.X, ALU.min))
                dve.tensor_tensor(onehot[:, :, :], less, over_e(first[:, :]), ALU.is_equal).then_inc(onehot_done, 1)
                dve.wait_ge(onehot_done, 1)
                dve.wait_ge(counted, 1)
                lower = rank_b[:, 0:NT * E_N].rearrange("p (t e) -> p t e", e=E_N)
                total = rank_b[:, NT * E_N:2 * NT * E_N].rearrange("p (t e) -> p t e", e=E_N)
                for e in range(E_N):
                    last = dve.tensor_tensor_scan(upto[:, e, :], rc[:, R_ONES:R_ONES + NT], total[:, :, e], 0.0, ALU.mult, ALU.add)
                link(last)
                link(dve.tensor_tensor(over[:, :, :], upto[:, :, NT - 1:NT].to_broadcast([P, E_N, NT]),
                                       rc[:, R_THRESH:R_THRESH + NT].unsqueeze(1).to_broadcast([P, E_N, NT]), ALU.is_gt))
                link(dve.tensor_reduce(tiles[:, :], over[:, :, :], AX.X, ALU.add))
                link(dve.tensor_tensor_scan(tile_end[:, :], rc[:, R_ONES:R_ONES + E_N], tiles[:, :], 0.0, ALU.mult, ALU.add))
                link(dve.tensor_tensor(tile_start[:, :], tile_end[:, :], tiles[:, :], ALU.subtract))
                link(dve.tensor_tensor(work[:, :, :], upto[:, :, :].rearrange("p e t -> p t e"), total, ALU.subtract))
                link(dve.scalar_tensor_tensor(work[:, :, :], over_t(tile_start[:, :]), float(P), work[:, :, :], ALU.mult, ALU.add))
                link(dve.tensor_tensor(work[:, :, :], work[:, :, :], lower, ALU.add))
                link(dve.tensor_tensor(work[:, :, :], work[:, :, :], onehot[:, :, :], ALU.mult))
                link(dve.tensor_reduce(slot_f[:, :], work[:, :, :], AX.X, ALU.add))
                dve.tensor_copy(slot[:, :], slot_f[:, :]).then_inc(slots_done, 1)
                link(dve.tensor_tensor(before[:, :, :], over_t(tile_end[:, :], SLOT_TILES),
                                       over_e(rc[:, R_TILE:R_TILE + SLOT_TILES]), ALU.is_le))
                link(dve.tensor_reduce(owner_f[:, :], before[:, :, :], AX.X, ALU.add))
                dve.tensor_scalar(owner[:, :], owner_f[:, :], E_N - 1.0, None, ALU.min).then_inc(owners_done, 1)
                for q in range(1, GROUPS_T, 2):
                    dve.wait_ge(transposed, q + 1)
                    dve.tensor_copy(sortedT[:, q * BANK:(q + 1) * BANK], banks[q % 4][:, :]).then_inc(evac_v, 1)
                dve.tensor_copy(token[:, :], sorted_sb[:, :, P]).then_inc(tokens_done, 1)

                def steps(i, numbers, live):
                    for s in numbers:
                        if live(s):
                            wait(dve, out_done, i * U + s - 3)
                            wait(dve, hidden_done, i * U + s + 1)
                            for c in (2, 3):
                                last = dve.tensor_scalar(hT[s % 4][:, c, :], banks[(s % 2) * 2 + 1][:, (c - 2) * P:(c - 1) * P],
                                                         W[s][:, B1 + c:B1 + c + 1], 0.0, ALU.add, ALU.max)
                            last.then_inc(relu_v, 1)
                        n = s - 1
                        if live(n):
                            wait(dve, out_done, i * U + n + 1)
                            dve.tensor_tensor(y_sorted[:, bass.ds(i * U + n, 1), :].rearrange("p j c -> p (j c)"), banks[4 + n % 2][:, 0:P],
                                              W[n % U][:, B2:B2 + P], ALU.add).then_inc(y_ready, 1)

                passes(dve, steps)
                for q in range(4):
                    part = slice(q * QUARTER, (q + 1) * QUARTER)
                    dve.wait_ge(y_loaded[q], 16)
                    dve.tensor_tensor(x[:, part, :], x[:, part, :], y_tok[:, part, :], ALU.add).then_inc(added, 1)

            @block.gpsimd
            def _(pool):
                pool.wait_ge(slots_done, 1)
                for t in range(NT):
                    pool.indirect_dma_start(out=sorted_x, out_offset=bass.IndirectOffsetOnAxis(ap=slot[:, t:t + 1], axis=0),
                                            in_=xn[:, t, :], in_offset=None).then_inc(scattered, 16)
                pool.wait_ge(tokens_done, 1)
                for j in range(SLOT_TILES):
                    pool.wait_ge(y_ready, j + 1)
                    pool.indirect_dma_start(out=d["y_tok"], out_offset=bass.IndirectOffsetOnAxis(ap=token[:, j:j + 1], axis=0),
                                            in_=y_sorted[:, j, :], in_offset=None).then_inc(y_scattered, 16)

            @block.scalar
            def _(act):
                for q in range(0, GROUPS_T, 2):
                    act.wait_ge(transposed, q + 1)
                    act.activation(sortedT[:, q * BANK:(q + 1) * BANK], banks[q % 4][:, :], ACT.Copy).then_inc(evac_a, 1)

                def steps(i, numbers, live):
                    for s in numbers:
                        if live(s):
                            wait(act, out_done, i * U + s - 3)
                            wait(act, hidden_done, i * U + s + 1)
                            for c in (0, 1):
                                last = act.activation(hT[s % 4][:, c, :], banks[(s % 2) * 2][:, c * P:(c + 1) * P], ACT.Relu,
                                                      bias=W[s][:, B1 + c:B1 + c + 1])
                            last.then_inc(relu_a, 1)

                passes(act, steps)


def mamba_phase(prog, d):
    nc = prog.nc
    x, xnT, ident = prog.x, prog.xnT, prog.ident
    G = NTOK // BANK
    GS = BANK // S
    with ExitStack() as stack:
        sb, _ = buffers(nc, stack, "m")
        w_in = sb("w_in", [P, 2 * DI])
        conv_w = sb("conv_w", [P, DC, 4])
        conv_b = sb("conv_b", [P, DC])
        w_x = sb("w_x", [P, DC, DTR + 2 * NS])
        w_dt = sb("w_dt", [DTR, DI])
        b_dt = sb("b_dt", [P, DC])
        a_log = sb("a_log", [P, DC, NS])
        a_exp = sb("a_exp", [P, DC, NS])
        a_neg = sb("a_neg", [P, DC, NS])
        skip = sb("skip", [P, DC])
        w_out = sb("w_out", [P, DC, P])
        f_w1 = sb("f_w1", [P, HID])
        f_b1 = sb("f_b1", [P, HC])
        f_w2 = sb("f_w2", [P, HC, P])
        f_b2 = sb("f_b2", [P, 1])
        pick = sb("pick", [96, 2 * NS, P], BF16)
        u = sb("u", [P, DC, NTOK])
        sres = sb("sres", [P, DC, NTOK])
        delta = sb("delta", [P, DC, NTOK])
        yz = sb("yz", [P, DC, NTOK])
        bc3 = sb("bc3", [96, NTOK], BF16)

        (loaded, xz_done, conv_first, conv_step, conv_done, res_done, u_done) = prog.semaphores(
            "ma", "loaded xz_done conv_first conv_step conv_done res_done u_done")
        with ExitStack() as inner:
            sbi, bank = buffers(nc, inner, "ma")
            xz_b = [[bank(f"xz{i}{c}") for c in range(4)] for i in range(2)]
            acc = [[sbi(f"acc{i}{c}", [P, GS, S]) for c in range(DC)] for i in range(2)]
            block = inner.enter_context(nc.Block())

            @block.sync
            def _(sp):
                for dst, src in ((w_in[:, :], d["in_projT"]), (conv_w[:, :, :], d["conv_w"]), (conv_b[:, :], d["conv_b"]),
                                 (w_x[:, :, :], d["x_projT"]), (w_dt[:, :], d["dt_projT"]), (b_dt[:, :], d["dt_b"]),
                                 (a_log[:, :, :], d["A_log"]), (skip[:, :], d["D"]), (w_out[:, :, :], d["out_projT"]),
                                 (f_w1[:, :], d["ffn_w1T"]), (f_b1[:, :], d["ffn_b1"]), (f_w2[:, :, :], d["ffn_w2T"]),
                                 (f_b2[:, :], d["ffn_b2"]), (pick[:, :, :], d["c_pick"].bitcast(BF16))):
                    sp.dma_start(dst, src).then_inc(loaded, 16)

            @block.tensor
            def _(pe):
                pe.wait_ge(loaded, 16 * 14)
                for g in range(G):
                    for c in range(4):
                        if g >= 2:
                            if c < DC:
                                pe.wait_ge(conv_done, (g - 2) * DC + c + 1)
                            else:
                                pe.wait_ge(res_done, (g - 2) * DC + c - DC + 1)
                        pe.matmul(xz_b[g % 2][c][:, :], w_in[:, c * P:(c + 1) * P], xnT[:, g * BANK:(g + 1) * BANK],
                                  start=True, stop=True).then_inc(xz_done, 1)

            @block.scalar
            def _(act):
                act.wait_ge(loaded, 16 * 14)
                for g in range(G):
                    for c in range(DC):
                        act.wait_ge(xz_done, g * 4 + c + 1)
                        wait(act, u_done, (g - 2) * DC + c + 1)
                        act.activation(acc[g % 2][c][:, :, :].rearrange("p a s -> p (a s)"), xz_b[g % 2][c][:, :], ACT.Identity,
                                       bias=conv_b[:, c:c + 1], scale=conv_w[:, c, 3:4]).then_inc(conv_first, 1)
                    for c in range(DC):
                        act.wait_ge(xz_done, g * 4 + DC + c + 1)
                        act.activation(sres[:, c, g * BANK:(g + 1) * BANK], xz_b[g % 2][DC + c][:, :], ACT.Silu).then_inc(res_done, 1)
                    for c in range(DC):
                        act.wait_ge(conv_done, g * DC + c + 1)
                        act.activation(u[:, c, g * BANK:(g + 1) * BANK], acc[g % 2][c][:, :, :].rearrange("p a s -> p (a s)"),
                                       ACT.Silu).then_inc(u_done, 1)

            @block.vector
            def _(dve):
                for g in range(G):
                    for k in (2, 1, 0):
                        back = 3 - k
                        for c in range(DC):
                            if k == 2:
                                dve.wait_ge(conv_first, g * DC + c + 1)
                            else:
                                dve.wait_ge(conv_step, (g * 2 + 1 - k) * DC + c + 1)
                            src = xz_b[g % 2][c][:, :].rearrange("p (a s) -> p a s", a=GS)[:, :, 0:S - back]
                            to = acc[g % 2][c][:, :, back:S]
                            step = dve.scalar_tensor_tensor(to, src, conv_w[:, c, k:k + 1], to, ALU.mult, ALU.add)
                            if k == 0:
                                step.then_inc(conv_done, 1)
                            else:
                                step.then_inc(conv_step, 1)

        (xdbl_done, dt_copied, bc_copied, split_step, z_done, zb_done, abs_done, exp_done, log_done, sum_done, ones_done,
         rest_done, delta_done, a_done, a_negated) = prog.semaphores(
            "mb", "xdbl_done dt_copied bc_copied split_step z_done zb_done abs_done exp_done log_done sum_done ones_done "
                  "rest_done delta_done a_done a_negated")
        with ExitStack() as inner:
            sbi, bank = buffers(nc, inner, "mb")
            xd_b = [bank(f"xd{i}") for i in range(2)]
            z_b = [bank(f"z{i}") for i in range(4)]
            dtT = [sbi(f"dtT{i}", [DTR, BANK]) for i in range(2)]
            bc = sbi("bc", [32, BANK])
            rest1 = sbi("rest1", [32, BANK])
            rest2 = sbi("rest2", [32, BANK])
            middle = sbi("middle", [32, BANK], BF16)
            zb = [sbi(f"zb{i}", [P, BANK]) for i in range(4)]
            za = [sbi(f"za{i}", [P, BANK]) for i in range(4)]
            ze = [sbi(f"ze{i}", [P, BANK]) for i in range(4)]
            zl = [sbi(f"zl{i}", [P, BANK]) for i in range(4)]
            z1 = [sbi(f"z1{i}", [P, BANK]) for i in range(4)]
            block = inner.enter_context(nc.Block())
            NU = G * DC

            @block.tensor
            def _(pe):
                def delta_in(g):
                    for c in range(DC):
                        k = g * DC + c
                        pe.wait_ge(dt_copied, g + 1)
                        wait(pe, zb_done, k - 3)
                        pe.matmul(z_b[k % 4][:, :], w_dt[:, c * P:(c + 1) * P], dtT[g % 2][:, :], start=True, stop=True).then_inc(z_done, 1)

                for g in range(G):
                    wait(pe, dt_copied, g - 1)
                    wait(pe, bc_copied, g - 1)
                    for c in range(DC):
                        last = pe.matmul(xd_b[g % 2][0:DTR + 2 * NS, :], w_x[:, c, :], u[:, c, g * BANK:(g + 1) * BANK],
                                         start=(c == 0), stop=(c == DC - 1))
                    last.then_inc(xdbl_done, 1)
                    if g:
                        delta_in(g - 1)
                delta_in(G - 1)

            @block.scalar
            def _(act):
                act.activation(a_exp[:, :, :], a_log[:, :, :], ACT.Exp).then_inc(a_done, 1)
                for g in range(G + 1):
                    if g < G:
                        act.wait_ge(xdbl_done, g + 1)
                        wait(act, z_done, (g - 1) * DC)
                        act.activation(dtT[g % 2][:, :], xd_b[g % 2][0:DTR, :], ACT.Copy).then_inc(dt_copied, 1)
                    if g == 0:
                        continue
                    for k in range((g - 1) * DC, g * DC):
                        act.wait_ge(zb_done, k + 1)
                        wait(act, exp_done, k - 3)
                        act.activation(za[k % 4][:, :], zb[k % 4][:, :], ACT.Abs).then_inc(abs_done, 1)
                    for k in range((g - 1) * DC, g * DC):
                        act.wait_ge(abs_done, k + 1)
                        wait(act, rest_done, k - 3)
                        act.activation(ze[k % 4][:, :], za[k % 4][:, :], ACT.Exp, scale=-1.0).then_inc(exp_done, 1)
                    for k in range((g - 1) * DC, g * DC):
                        act.wait_ge(exp_done, k + 1)
                        wait(act, sum_done, k - 3)
                        act.activation(zl[k % 4][:, :], ze[k % 4][:, :], ACT.Ln, bias=1.0).then_inc(log_done, 1)

            @block.vector
            def _(dve):
                dve.wait_ge(a_done, 1)
                dve.tensor_scalar(a_neg[:, :, :], a_exp[:, :, :], -1.0, None, ALU.mult).then_inc(a_negated, 1)
                steps = [0]

                def split(instruction):
                    steps[0] += 1
                    instruction.then_inc(split_step, 1)
                    dve.wait_ge(split_step, steps[0])

                for g in range(G + 1):
                    if g < G:
                        cols = slice(g * BANK, (g + 1) * BANK)
                        dve.wait_ge(xdbl_done, g + 1)
                        dve.tensor_copy(bc[:, :], xd_b[g % 2][DTR:DTR + 2 * NS, :]).then_inc(bc_copied, 1)
                        dve.wait_ge(bc_copied, g + 1)
                        split(dve.tensor_copy(bc3[0:32, cols], bc[:, :]))
                        split(dve.tensor_tensor(rest1[:, :], bc[:, :], bc3[0:32, cols], ALU.subtract))
                        split(dve.tensor_copy(middle[:, :], rest1[:, :]))
                        split(dve.tensor_copy(bc3[32:64, cols], middle[:, :]))
                        split(dve.tensor_tensor(rest2[:, :], rest1[:, :], middle[:, :], ALU.subtract))
                        split(dve.tensor_copy(bc3[64:96, cols], rest2[:, :]))
                    if g == 0:
                        continue
                    mine = range((g - 1) * DC, g * DC)
                    for k in mine:
                        dve.wait_ge(z_done, k + 1)
                        wait(dve, abs_done, k - 3)
                        dve.tensor_scalar(zb[k % 4][:, :], z_b[k % 4][:, :], b_dt[:, k % DC:k % DC + 1], None, ALU.add).then_inc(zb_done, 1)
                    for k in mine:
                        dve.wait_ge(exp_done, k + 1)
                        dve.tensor_scalar(z1[k % 4][:, :], ze[k % 4][:, :], 1.0, -1.0, ALU.add, ALU.add).then_inc(ones_done, 1)
                    for k in mine:
                        dve.wait_ge(ones_done, k + 1)
                        wait(dve, delta_done, k - 3)
                        dve.tensor_tensor(z1[k % 4][:, :], ze[k % 4][:, :], z1[k % 4][:, :], ALU.subtract).then_inc(rest_done, 1)
                    for k in mine:
                        dve.wait_ge(log_done, k + 1)
                        dve.scalar_tensor_tensor(zl[k % 4][:, :], zb[k % 4][:, :], 0.0, zl[k % 4][:, :], ALU.max, ALU.add).then_inc(sum_done, 1)
                    for k in mine:
                        dve.wait_ge(sum_done, k + 1)
                        dve.wait_ge(rest_done, k + 1)
                        c, q = k % DC, k // DC
                        dve.tensor_tensor(delta[:, c, q * BANK:(q + 1) * BANK], zl[k % 4][:, :], z1[k % 4][:, :], ALU.add).then_inc(delta_done, 1)

        (dA_zeroed, b_done, c_done, b_copied, dA_done, du_done, dBu_done, h_done, hc_done, y_done, y_skip, y_evac) = prog.semaphores(
            "mc", "dA_zeroed b_done c_done b_copied dA_done du_done dBu_done h_done hc_done y_done y_skip y_evac")
        with ExitStack() as inner:
            sbi, bank = buffers(nc, inner, "mc")
            y_b = [bank(f"y{c}") for c in range(DC)]
            b_b = [bank(f"b{i}") for i in range(2)]
            c_b = [bank(f"c{i}") for i in range(2)]
            dA_b = [bank(f"dA{i}") for i in range(2)]
            du = [sbi(f"du{c}", [P, BANK]) for c in range(DC)]
            b_s = [sbi(f"bs{i}", [P, BANK]) for i in range(4)]
            dBu = [sbi(f"dBu{i}", [P, BANK]) for i in range(4)]
            h = [sbi(f"h{i}", [P, BANK]) for i in range(4)]
            hc = [sbi(f"hc{i}", [P, BANK]) for i in range(8)]
            ysum = [sbi(f"ysum{c}", [P, BANK]) for c in range(DC)]
            NUNITS = DC * NS
            LAG = 6
            delta_cur = [sbi(f"delta_cur{c}", [P, GS, S]) for c in range(DC)]
            delta_loaded = [prog.sem(f"mc_delta_loaded{c}") for c in range(DC)]
            block = inner.enter_context(nc.Block())

            def cols(g):
                return bass.ds(g * BANK, BANK)

            def passes(engine, steps):
                steps(0, range(NUNITS), lambda n: n >= 0)
                with engine.Fori(1, G) as g:
                    steps(g, range(NUNITS), lambda n: True)
                steps(G, range(LAG + 2), lambda n: n < 0)

            @block.tensor
            def _(pe):
                def steps(g, numbers, live):
                    for s in numbers:
                        n, c = s // DC, s % DC
                        if live(s) and c == 0:
                            wait(pe, b_copied, g * NS + n - 1)
                            pe.matmul(b_b[n % 2][:, :], pick[:, n, :], bc3[:, cols(g)], start=True, stop=True).then_inc(b_done, 1)
                            wait(pe, hc_done, (g * NS + n - 1) * DC)
                            pe.matmul(c_b[n % 2][:, :], pick[:, NS + n, :], bc3[:, cols(g)], start=True, stop=True).then_inc(c_done, 1)
                        k = s - LAG
                        if live(k):
                            n, c = (k % NUNITS) // DC, k % DC
                            wait(pe, hc_done, g * NUNITS + k + 1)
                            if n == 0:
                                wait(pe, y_evac, g * DC)
                            last = pe.matmul(y_b[c][:, :], ident[:, :], hc[k % 8][:, :], start=(n == 0), stop=(n == NS - 1))
                            last.then_inc(y_done, 1)

                passes(pe, steps)

            @block.scalar
            def _(act):
                act.wait_ge(dA_zeroed, 2)

                def steps(g, numbers, live):
                    for s in numbers:
                        n, c = s // DC, s % DC
                        if not live(s):
                            continue
                        if c == 0:
                            wait(act, b_done, g * NS + n + 1)
                            wait(act, dBu_done, (g * NS + n - 3) * DC)
                            act.activation(b_s[n % 4][:, :], b_b[n % 2][:, :], ACT.Copy).then_inc(b_copied, 1)
                        wait(act, h_done, g * NUNITS + s - 1)
                        wait(act, delta_loaded[c], (g + 1) * 16)
                        act.activation(dA_b[s % 2][:, :].rearrange("p (a s) -> p a s", a=GS)[:, :, 1:S],
                                       delta_cur[c][:, :, 1:S], ACT.Exp,
                                       scale=a_neg[:, c, n:n + 1]).then_inc(dA_done, 1)

                passes(act, steps)

            @block.sync
            def _(sp):
                def one_pass(g):
                    for c in range(DC):
                        wait(sp, dA_done, g * NUNITS - (DC - 1 - c))
                        sp.dma_start(delta_cur[c][:, :, :].rearrange("p a s -> p (a s)"), delta[:, c, cols(g)]).then_inc(delta_loaded[c], 16)

                one_pass(0)
                with sp.Fori(1, G) as g:
                    one_pass(g)

            @block.gpsimd
            def _(pool):
                def one_pass(g):
                    wait(pool, dBu_done, g * NUNITS)
                    for c in range(DC):
                        pool.tensor_tensor(du[c][:, :], delta[:, c, cols(g)], u[:, c, cols(g)], ALU.mult).then_inc(du_done, 1)
                    for s in range(NUNITS):
                        n, c = s // DC, s % DC
                        wait(pool, du_done, (g + 1) * DC)
                        wait(pool, h_done, g * NUNITS + s - 3)
                        wait(pool, b_copied, g * NS + n + 1)
                        pool.tensor_tensor(dBu[s % 4][:, :], du[c][:, :], b_s[n % 4][:, :], ALU.mult).then_inc(dBu_done, 1)

                one_pass(0)
                with pool.Fori(1, G) as g:
                    one_pass(g)

            @block.vector
            def _(dve):
                for i in range(2):
                    dve.memset(dA_b[i][:, :], 0.0).then_inc(dA_zeroed, 1)

                def steps(g, numbers, live):
                    for s in numbers:
                        if live(s):
                            wait(dve, dA_done, g * NUNITS + s + 1)
                            wait(dve, dBu_done, g * NUNITS + s + 1)
                            wait(dve, hc_done, g * NUNITS + s - 3)
                            dve.tensor_tensor_scan(h[s % 4][:, :], dA_b[s % 2][:, :], dBu[s % 4][:, :], 0.0, ALU.mult, ALU.add).then_inc(h_done, 1)
                        k = s - 1
                        if live(k):
                            n = (k % NUNITS) // DC
                            wait(dve, h_done, g * NUNITS + k + 1)
                            wait(dve, c_done, g * NS + k // DC + 1)
                            wait(dve, y_done, g * NUNITS + k - 7)
                            dve.tensor_tensor(hc[k % 8][:, :], h[k % 4][:, :], c_b[n % 2][:, :], ALU.mult).then_inc(hc_done, 1)
                        if s == LAG + 1 and live(-1):
                            for c in range(DC):
                                wait(dve, y_done, g * NUNITS - DC + c + 1)
                                dve.scalar_tensor_tensor(ysum[c][:, :], u[:, c, cols(g - 1)], skip[:, c:c + 1], y_b[c][:, :],
                                                         ALU.mult, ALU.add).then_inc(y_evac, 1)
                            for c in range(DC):
                                wait(dve, y_evac, (g - 1) * DC + c + 1)
                                dve.tensor_tensor(yz[:, c, cols(g - 1)], ysum[c][:, :], sres[:, c, cols(g - 1)], ALU.mult).then_inc(y_skip, 1)

                passes(dve, steps)

        (m_done, m_copied, f1_done, gelu_done, f2_done, c_summed, stat_done, moments, mean_done, mean_copied, dev_step, var_done,
         var_copied, std_done, rstd_done, c_normed, c_trans, added) = prog.semaphores(
            "md", "m_done m_copied f1_done gelu_done f2_done c_summed stat_done moments mean_done mean_copied dev_step var_done "
                  "var_copied std_done rstd_done c_normed c_trans added")
        with ExitStack() as inner:
            sbi, bank = buffers(nc, inner, "md")
            m_b = [bank(f"m{i}") for i in range(2)]
            f_b = [bank(f"f{i}") for i in range(4)]
            o_b = bank("o")
            s_b = bank("s")
            mT = [sbi(f"mT{i}", [P, BANK]) for i in range(2)]
            gl = [[sbi(f"gl{i}{c}", [P, BANK]) for c in range(HC)] for i in range(2)]
            cT = sbi("cT", [P, B, S])
            cn = sbi("cn", [P, NT, P])
            stats = sbi("stats", [P, B, 6])
            mom = sbi("mom", [P, B, 2])
            mean = sbi("mean", [P, B])
            dev = sbi("dev", [P, B])
            dev2 = sbi("dev2", [P, B])
            part_var = sbi("part_var", [P, B])
            var = sbi("var", [P, B])
            std = sbi("std", [P, B])
            rstd = sbi("rstd", [P, B])
            block = inner.enter_context(nc.Block())

            @block.tensor
            def _(pe):
                def out_proj(g):
                    wait(pe, m_copied, g - 1)
                    for c in range(DC):
                        last = pe.matmul(m_b[g % 2][:, :], w_out[:, c, :], yz[:, c, g * BANK:(g + 1) * BANK],
                                         start=(c == 0), stop=(c == DC - 1))
                    last.then_inc(m_done, 1)

                out_proj(0)
                for g in range(G):
                    pe.wait_ge(m_copied, g + 1)
                    for c in range(HC):
                        wait(pe, gelu_done, (g - 1) * HC + c + 1)
                        pe.matmul(f_b[c][:, :], f_w1[:, c * P:(c + 1) * P], mT[g % 2][:, :], start=True, stop=True).then_inc(f1_done, 1)
                    if g + 1 < G:
                        out_proj(g + 1)
                    wait(pe, c_summed, g)
                    for c in range(HC):
                        pe.wait_ge(gelu_done, g * HC + c + 1)
                        last = pe.matmul(o_b[:, :], f_w2[:, c, :], gl[g % 2][c][:, :], start=(c == 0), stop=(c == HC - 1))
                    last.then_inc(f2_done, 1)
                pe.wait_ge(moments, B)
                pe.matmul(s_b[:, 0:B], prog.inv_p[:, :], mom[:, :, 0], start=True, stop=True).then_inc(mean_done, 1)
                pe.wait_ge(dev_step, 3)
                pe.wait_ge(mean_copied, 1)
                pe.matmul(s_b[:, B:2 * B], prog.inv_p[:, :], part_var[:, :], start=True, stop=True).then_inc(var_done, 1)
                for t in range(NT):
                    pe.wait_ge(c_normed, t // QT + 1)
                    pe.transpose(f_b[t // 4][:, (t % 4) * P:(t % 4 + 1) * P], cn[:, t, :], ident[:, :]).then_inc(c_trans, 1)

            @block.scalar
            def _(act):
                for g in range(G):
                    act.wait_ge(m_done, g + 1)
                    wait(act, f1_done, (g - 1) * HC)
                    wait(act, c_summed, g - 1)
                    act.activation(mT[g % 2][:, :], m_b[g % 2][:, :], ACT.Copy).then_inc(m_copied, 1)
                    for c in range(HC):
                        act.wait_ge(f1_done, g * HC + c + 1)
                        wait(act, f2_done, g - 1)
                        act.activation(gl[g % 2][c][:, :], f_b[c][:, :], ACT.Gelu, bias=f_b1[:, c:c + 1]).then_inc(gelu_done, 1)
                act.wait_ge(var_copied, 1)
                act.activation(std[:, :], var[:, :], ACT.Sqrt).then_inc(std_done, 1)

            @block.vector
            def _(dve):
                for g in range(G):
                    dve.wait_ge(f2_done, g + 1)
                    dve.wait_ge(m_copied, g + 1)
                    dve.scalar_tensor_tensor(cT[:, g * GS:(g + 1) * GS, :].rearrange("p a s -> p (a s)"), o_b[:, :], f_b2[:, 0:1],
                                             mT[g % 2][:, :], ALU.add, ALU.add).then_inc(c_summed, 1)
                    dve.wait_ge(c_summed, g + 1)
                    for b in range(g * GS, (g + 1) * GS):
                        dve.bn_stats(stats[:, b, :], cT[:, b, :]).then_inc(stat_done, 1)
                    for b in range(g * GS, (g + 1) * GS):
                        dve.wait_ge(stat_done, b + 1)
                        dve.bn_aggr(mom[:, b, :], stats[:, b, :]).then_inc(moments, 1)
                dve.wait_ge(mean_done, 1)
                dve.tensor_copy(mean[:, :], s_b[:, 0:B]).then_inc(mean_copied, 1)
                dve.wait_ge(mean_copied, 1)
                dve.tensor_tensor(dev[:, :], mom[:, :, 0], mean[:, :], ALU.subtract).then_inc(dev_step, 1)
                dve.wait_ge(dev_step, 1)
                dve.tensor_tensor(dev2[:, :], dev[:, :], dev[:, :], ALU.mult).then_inc(dev_step, 1)
                dve.wait_ge(dev_step, 2)
                dve.tensor_tensor(part_var[:, :], dev2[:, :], mom[:, :, 1], ALU.add).then_inc(dev_step, 1)
                dve.wait_ge(var_done, 1)
                dve.tensor_scalar(var[:, :], s_b[:, B:2 * B], EPS, None, ALU.add).then_inc(var_copied, 1)
                dve.wait_ge(std_done, 1)
                dve.reciprocal(rstd[:, :], std[:, :]).then_inc(rstd_done, 1)
                dve.wait_ge(rstd_done, 1)
                for b in range(B):
                    dve.tensor_scalar(cn[:, b * QT:(b + 1) * QT, :].rearrange("p q s -> p (q s)"), cT[:, b, :], mean[:, b:b + 1],
                                      rstd[:, b:b + 1], ALU.subtract, ALU.mult).then_inc(c_normed, 1)
                for q in range(4):
                    dve.wait_ge(c_trans, 4 * (q + 1))
                    xs = x[:, q * 4:(q + 1) * 4, :].rearrange("p t c -> p (t c)")
                    dve.tensor_tensor(xs, xs, f_b[q][:, :], ALU.add).then_inc(added, 1)


def program(nc, d, stop_after=None):
    with ExitStack() as stack:
        prog = Program(nc)
        sb, _ = buffers(nc, stack, "g")
        prog.x = sb("x", [P, NT, P])
        prog.xn = sb("xn", [P, NT, XW])
        prog.xnT = sb("xnT", [P, NTOK])
        prog.ident = sb("ident", [P, P])
        prog.inv_p = sb("inv_p", [P, P])
        prog.ones_b = sb("ones_b", [P, P], BF16)
        prog.tri = sb("tri", [P, P], BF16)
        prog.route_consts = sb("route_consts", [P, R_END])
        prog.phase(load_phase, d)
        prog.phase(norm_phase, "n1")
        prog.phase(attention_phase, d)
        if stop_after == "attention":
            return prog.phase(store_phase, d)
        prog.phase(norm_phase, "n2")
        prog.phase(experts_phase, d, "f1")
        if stop_after == "ffn1":
            return prog.phase(store_phase, d)
        prog.phase(norm_phase, "n3")
        prog.phase(mamba_phase, d)
        if stop_after == "mamba":
            return prog.phase(store_phase, d)
        prog.phase(norm_phase, "n4")
        prog.phase(experts_phase, d, "f2")
        prog.phase(store_phase, d)


def store_phase(prog, d):
    (stored,) = prog.semaphores("st", "stored")
    with prog.nc.Block() as block:

        @block.sync
        def _(sp):
            for q in range(4):
                tiles = slice(q * 4, q * 4 + 4)
                sp.dma_start(d["out"].rearrange("(t p) c -> p t c", p=P)[:, tiles, :], prog.x[:, tiles, :]).then_inc(stored, 16)
            sp.wait_ge(stored, 64)


def layout(inputs):
    import numpy as np

    def a(name):
        return np.asarray(inputs[name])

    out = {"x": a("L0_attn_a_x").reshape(NTOK, P)}
    by_head_last = np.arange(P).reshape(HEADS, HD).T.reshape(P)
    out["Wq"] = np.ascontiguousarray(a("L0_attn_a_Wq")[:, by_head_last])
    out["WkT"] = np.ascontiguousarray(a("L0_attn_a_Wk").T)
    out["WvT"] = np.ascontiguousarray(a("L0_attn_a_Wv").T)
    out["W_down"] = a("L0_attn_a_W_down_kv")
    out["W_up_k"] = np.ascontiguousarray(a("L0_attn_a_W_up_k")[:, by_head_last])
    out["W_up_v"] = a("L0_attn_a_W_up_v")
    out["Wo"] = a("L0_attn_a_Wo")
    out["gate_wT"] = np.ascontiguousarray(a("L0_ffn_gate_w").T)
    out["gate_b"] = a("L0_ffn_gate_b").reshape(1, E_N)
    w1 = a("L0_ffn_w1").transpose(0, 2, 1)
    w2 = a("L0_ffn_w2").transpose(0, 2, 1).reshape(E_N, HC, P, P).transpose(0, 2, 1, 3).reshape(E_N, P, HC * P)
    b1 = a("L0_ffn_b1").reshape(E_N, HC, P).transpose(0, 2, 1)
    b2 = np.broadcast_to(a("L0_ffn_b2").reshape(E_N, 1, P), (E_N, P, P))
    out["experts"] = np.ascontiguousarray(np.concatenate([w1, w2, b1, b2], axis=2).reshape(E_N * P, EW))
    def halves(m):
        return np.ascontiguousarray(m.reshape(DC, P, -1).transpose(1, 0, 2))

    out["in_projT"] = np.ascontiguousarray(a("L0_attn_b_in_proj_w").T)
    out["conv_w"] = halves(a("L0_attn_b_conv_w").reshape(DI, 4))
    out["conv_b"] = halves(a("L0_attn_b_conv_b")).reshape(P, DC)
    out["x_projT"] = halves(a("L0_attn_b_x_proj_w").T)
    out["dt_projT"] = np.ascontiguousarray(a("L0_attn_b_dt_proj_w").T)
    out["dt_b"] = halves(a("L0_attn_b_dt_proj_b")).reshape(P, DC)
    out["A_log"] = halves(a("L0_attn_b_A_log"))
    out["D"] = halves(a("L0_attn_b_D")).reshape(P, DC)
    out["out_projT"] = halves(a("L0_attn_b_out_proj_w").T)
    out["ffn_w1T"] = np.ascontiguousarray(a("L0_attn_b_ffn_w1").T)
    out["ffn_b1"] = np.ascontiguousarray(a("L0_attn_b_ffn_b1").reshape(HC, P).T)
    out["ffn_w2T"] = np.ascontiguousarray(a("L0_attn_b_ffn_w2").T.reshape(HC, P, P).transpose(1, 0, 2))
    out["ffn_b2"] = a("L0_attn_b_ffn_b2").reshape(P, 1)
    pick = (np.arange(96)[:, None] % 32 == np.arange(32)[None, :])[:, :, None]
    out["c_pick"] = np.ascontiguousarray(np.broadcast_to(pick, (96, 32, P))).astype(np.uint16) * np.uint16(BF16_ONE)
    p, s = np.arange(P), np.arange(S)
    q = s.reshape(QT, P)
    distance = np.abs(q.T[:, :, None].astype(np.float32) - s[None, None, :].astype(np.float32))
    out["c_decay"] = np.exp(np.float32(-0.01 * 0.01) * distance).astype(np.float32)
    out["c_ident"] = np.eye(P, dtype=np.float32)
    out["c_tri"] = (p[:, None] < p[None, :]).astype(np.uint16) * np.uint16(BF16_ONE)
    route = np.zeros((P, R_END), np.float32)
    route[:, R_LESS:R_LESS + E_N] = np.arange(E_N) - E_N
    route[:, R_THRESH:R_THRESH + NT] = np.arange(NT) * P
    route[:, R_TILE:R_TILE + SLOT_TILES] = np.arange(SLOT_TILES)
    route[:, R_ONES:R_ONES + NT] = 1.0
    route[:, R_TOKEN:R_TOKEN + NT] = np.arange(NT) * P + p[:, None]
    route[:, R_SPARE:R_SPARE + SLOT_TILES] = NTOK + np.arange(SLOT_TILES) * P + p[:, None]
    out["c_route"] = route
    return out


def scratch(nc, d):
    for tag in ("f1", "f2"):
        d["sorted_x_" + tag] = nc.dram_tensor("sorted_x_" + tag, (SLOT_TILES * P, XW), F32, kind="Internal").ap()
    d["y_tok"] = nc.dram_tensor("y_tok", (NTOK + SLOT_TILES * P, P), F32, kind="Internal").ap()
    d["parts"] = nc.dram_tensor("parts", (2, B, 3 * P, S), BF16, kind="Internal").ap()
    return d


def kernel(**inputs):
    import concourse.bacc as bacc
    from concourse.bass_utils import run_bass_kernel_spmd

    nc = bacc.Bacc("TRN2", target_bir_lowering=False, num_devices=1)
    arrays = layout(inputs)
    d = {name: nc.dram_tensor(name, a.shape, mybir.dt.from_np(a.dtype), kind="ExternalInput").ap() for name, a in arrays.items()}
    d["out"] = nc.dram_tensor("out", (NTOK, P), F32, kind="ExternalOutput").ap()
    program(nc, scratch(nc, d))
    result = run_bass_kernel_spmd(nc, [arrays], core_ids=[0])
    return result.results[0]["out"].reshape(B, S, P)
```

```python
from contextlib import ExitStack

import concourse.bass as bass
from concourse import mybir

F32 = mybir.dt.float32
BF16 = mybir.dt.bfloat16
U32 = mybir.dt.uint32
BF16_ONE = 0x3F80
ALU = mybir.AluOpType
ACT = mybir.ActivationFunctionType
AX = mybir.AxisListType

P = 128
B, S = 8, 256
NTOK = B * S
NT = NTOK // P
QT = S // P
HEADS, HD = 16, 8
GROUPS, GH = 4, 4
CLAMP = 10000.0
EPS = 1e-5
BANK = 512
E_N, HID = 8, 512
HC = HID // P
XW = P + 1
EW = 2 * HID + HID // P + P
SLOT_TILES = 24
DI, NS, DTR = 256, 16, 64
DC = DI // P


class Program:

    def __init__(self, nc):
        self.nc, self.held = nc, []

    def phase(self, build, *args):
        build(self, *args)
        self.nc.clear_and_free_semaphores(self.held)
        self.nc.all_engine_barrier()
        self.held = []

    def sem(self, name):
        self.held.append(self.nc.alloc_semaphore(name))
        return self.held[-1]

    def semaphores(self, prefix, names):
        return [self.sem(f"{prefix}_{n}") for n in names.split()]


def wait(engine, semaphore, value):
    if not isinstance(value, int) or value > 0:
        engine.wait_ge(semaphore, value)


def buffers(nc, stack, prefix):
    def sb(name, shape, dtype=F32):
        return stack.enter_context(nc.sbuf_tensor(f"{prefix}_{name}", shape, dtype))

    def bank(name, dtype=F32):
        return stack.enter_context(nc.psum_tensor(f"{prefix}_{name}", [P, BANK], dtype))

    return sb, bank


def norm_phase(prog, tag, loads, x_loads=(), gate=False):
    nc = prog.nc
    x, xn, xnT, logits = prog.x, prog.xn, prog.xnT, prog.logits
    (stats_done, moments_done, std_done, rstd_step, normed_v, normed_p, transposed, evac, loaded, filled, numbered, logits_in,
     logits_done) = prog.semaphores(
        tag, "stats_done moments_done std_done rstd_step normed_v normed_p transposed evac loaded filled numbered logits_in "
             "logits_done")
    x_loaded = [prog.sem(f"{tag}_x_loaded{q}") for q in range(4)]
    by_pool = [t for t in range(NT) if t % 5 == 3]
    by_dve = [t for t in range(NT) if t not in by_pool]
    with ExitStack() as stack:
        sb, bank = buffers(nc, stack, tag)
        stats = sb("stats", [P, NT, 6])
        mom = sb("mom", [P, NT, 2])
        var = sb("var", [P, NT])
        std = sb("std", [P, NT])
        r = sb("r", [P, NT])
        r2 = sb("r2", [P, NT])
        r3 = sb("r3", [P, NT])
        tb = [bank(f"tb{i}") for i in range(4)]
        logit_b = bank("logit")
        block = stack.enter_context(nc.Block())

        @block.sync
        def _(sp):
            for q, (dst, src) in enumerate(x_loads):
                sp.dma_start(dst, src).then_inc(x_loaded[q], 16)
            for dst, src in loads:
                sp.dma_start(dst, src).then_inc(loaded, 16)
            wait(sp, loaded, 16 * len(loads))

        def normalise(engine, t):
            return engine.tensor_scalar(xn[:, t, 0:P], x[:, t, :], mom[:, t, 0:1], r3[:, t:t + 1], ALU.subtract, ALU.mult)

        @block.vector
        def _(dve):
            for t in range(NT):
                if x_loads and t % 4 == 0:
                    dve.wait_ge(x_loaded[t // 4], 16)
                dve.bn_stats(stats[:, t, :], x[:, t, :]).then_inc(stats_done, 1)
            for t in range(NT):
                dve.wait_ge(stats_done, t + 1)
                dve.bn_aggr(mom[:, t, :], stats[:, t, :]).then_inc(moments_done, 1)
            dve.wait_ge(moments_done, NT)
            dve.tensor_scalar(var[:, :], mom[:, :, 1], EPS, None, ALU.add).then_inc(moments_done, 1)
            dve.wait_ge(std_done, 1)
            dve.reciprocal(r[:, :], std[:, :]).then_inc(rstd_step, 1)
            dve.wait_ge(rstd_step, 1)
            dve.tensor_tensor(r2[:, :], r[:, :], r[:, :], ALU.mult).then_inc(rstd_step, 1)
            dve.wait_ge(rstd_step, 2)
            dve.tensor_tensor(r3[:, :], r2[:, :], var[:, :], ALU.mult).then_inc(rstd_step, 1)
            dve.wait_ge(rstd_step, 3)
            dve.tensor_scalar(r2[:, :], r3[:, :], -0.5, 1.5, ALU.mult, ALU.add).then_inc(rstd_step, 1)
            dve.wait_ge(rstd_step, 4)
            dve.tensor_tensor(r3[:, :], r2[:, :], r[:, :], ALU.mult).then_inc(rstd_step, 1)
            dve.wait_ge(rstd_step, 5)
            for t in by_dve:
                normalise(dve, t).then_inc(normed_v, 1)
            if gate:
                dve.wait_ge(logits_in, 1)
                dve.tensor_tensor(logits[:, :, :], logit_b[:, 0:NT * E_N].rearrange("p (t e) -> p t e", e=E_N),
                                  prog.gate_b[:, :].unsqueeze(1).to_broadcast([P, NT, E_N]), ALU.add).then_inc(logits_done, 1)

        @block.gpsimd
        def _(pool):
            if x_loads:
                pool.memset(prog.ones_b[:, :], 1.0).then_inc(filled, 1)
                pool.memset(prog.inv_p[:, :], 1.0 / P).then_inc(filled, 1)
            pool.wait_ge(rstd_step, 5)
            for t in by_pool:
                normalise(pool, t).then_inc(normed_p, 1)
            if x_loads:
                pool.wait_ge(loaded, 16 * len(loads))
                pool.tensor_copy(xn[:, :, P], prog.route_consts[:, R_TOKEN:R_TOKEN + NT]).then_inc(numbered, 1)

        @block.tensor
        def _(pe):
            if x_loads:
                pe.wait_ge(loaded, 16 * len(loads))
            for q in range(4):
                for t in range(q * 4, q * 4 + 4):
                    if t in by_pool:
                        pe.wait_ge(normed_p, by_pool.index(t) + 1)
                    else:
                        pe.wait_ge(normed_v, by_dve.index(t) + 1)
                    last = pe.transpose(tb[q][:, (t % 4) * P:(t % 4 + 1) * P], xn[:, t, 0:P], prog.ident[:, :])
                last.then_inc(transposed, 1)
            for t in range(NT if gate else 0):
                pe.wait_ge(evac, t // 4 + 1)
                last = pe.matmul(logit_b[:, t * E_N:(t + 1) * E_N], xnT[:, t * P:(t + 1) * P], prog.gate_w[:, :],
                                 start=True, stop=True)
            if gate:
                last.then_inc(logits_in, 1)

        @block.scalar
        def _(act):
            act.wait_ge(moments_done, NT + 1)
            act.activation(std[:, :], var[:, :], ACT.Sqrt).then_inc(std_done, 1)
            for q in range(4):
                act.wait_ge(transposed, q + 1)
                act.activation(xnT[:, q * BANK:(q + 1) * BANK], tb[q][:, :], ACT.Copy).then_inc(evac, 1)


def attention_weights(prog, stack, d):
    sb, _ = buffers(prog.nc, stack, "aw")
    weights = (wq, wkvT, wvT, wdown, wup, wo, decay) = (
        sb("wq", [P, P]), sb("wkvT", [P, P]), sb("wvT", [P, P]), sb("wdown", [P, 32]), sb("wup", [32, 2, P]), sb("wo", [P, P]),
        sb("decay", [P, QT, S]))
    return weights, ((wkvT[:, :], d["WkT"]), (wvT[:, :], d["WvT"]), (wdown[:, :], d["W_down"]), (wup[:, 0, :], d["W_up_k"]),
                     (wup[:, 1, :], d["W_up_v"]), (wq[:, :], d["Wq"]), (wo[:, :], d["Wo"]), (decay[:, :, :], d["c_decay"]))


def attention_phase(prog, d, weights):
    nc = prog.nc
    x, xnT, ident = prog.x, prog.xnT, prog.ident
    SCALE = 1.0 / (128.0 ** 0.5 + 1e-08)
    H = HEADS
    ROWS = 9 * HD
    with ExitStack() as stack:
        sb, bank = buffers(nc, stack, "at")
        wq, wkvT, wvT, wdown, wup, wo, decay = weights
        downT = sb("downT", [32, P])
        wkv_eff = sb("wkv_eff", [P, 2, P])
        whole = [sb(f"whole{i}", [P, BANK]) for i in range(4)]
        rest = [sb(f"rest{i}", [P, BANK]) for i in range(4)]
        parts = [[sb(f"part{a}{i}", [P, NTOK], BF16) for i in range(3)] for a in "qk"]
        stack_q = [sb(f"stack_q{i}", [ROWS, HEADS, S], BF16) for i in range(2)]
        stack_k = [sb(f"stack_k{i}", [ROWS, HEADS, S], BF16) for i in range(2)]
        v = sb("v", [P, NT, P])
        vaug = sb("vaug", [P, QT, HEADS, 32])
        sc = [sb(f"sc{i}", [P, BANK]) for i in range(4)]
        sd = [sb(f"sd{i}", [P, BANK]) for i in range(4)]
        rowmax = sb("rowmax", [P, HEADS, QT])
        negmax = sb("negmax", [P, HEADS, QT])
        minus = sb("minus", [P, QT])
        pr = [sb(f"pr{i}", [P, BANK]) for i in range(4)]
        prT = [sb(f"prT{i}", [P, BANK]) for i in range(8)]
        oT = sb("oT", [P, S])
        rden = sb("rden", [P, QT, GH])
        on = sb("on", [P, QT, P])
        onT = sb("onT", [P, S])
        spare = sb("spare", [P, SLOT_TILES, XW])
        score_b = [bank(f"score{i}") for i in range(2)]
        trans_b = [bank(f"trans{i}") for i in range(2)]
        out_b = [bank(f"out{i}") for i in range(2)]
        quad_b = bank("quad")
        misc_b = bank("misc")
        proj_b = [*score_b, *trans_b]

        (wsum, eff_step, eff_evac, vones, projected_in, evac_a, whole_done, evac_v, high_done, rest_done, middle_done,
         low_done, written_first, written, spare_ready) = prog.semaphores(
            "atw", "wsum eff_step eff_evac vones projected_in evac_a whole_done evac_v high_done rest_done middle_done low_done "
                   "written_first written spare_ready")
        (stacked, spare_written, vaug_ready, scored, clipped, decayed, negated, exped, ptrans, pt_ready, attended, ot_ready,
         ot_trans, rden_ready, normed, on_trans, ont_ready, projected, added) = prog.semaphores(
            "at", "stacked spare_written vaug_ready scored clipped decayed negated exped ptrans pt_ready attended ot_ready "
                  "ot_trans rden_ready normed on_trans ont_ready projected added")
        NSTACK = 4

        def stack_up(sp, b, half):
            wait(sp, scored, b * H - H)
            wait(sp, stacked, b * NSTACK * 16)
            q_parts, k_parts = (d["parts"][a, bass.ds(b, 1), :, :].rearrange("b (r h) s -> (b r) (h s)", h=H) for a in (0, 1))
            for i in range(3):
                sp.dma_start(stack_q[half][i * 3 * HD:(i + 1) * 3 * HD, :, :].rearrange("p h s -> p (h s)"),
                             q_parts[i * HD:(i + 1) * HD, :].unsqueeze(0).to_broadcast([3, HD, H * S])).then_inc(stacked, 16)
            sp.dma_start(stack_k[half][:, :, :].rearrange("p h s -> p (h s)"),
                         k_parts.unsqueeze(0).to_broadcast([3, 3 * HD, H * S])).then_inc(stacked, 16)

        QK = ((0, 0), (0, 1), (1, 0), (1, 1), (0, 2), (1, 2), (0, 3), (1, 3))
        FILLS = len(QK) + NT // 4

        def split_of(f):
            a, quarter = QK[f]
            return (*parts[a], slice(quarter * BANK, (quarter + 1) * BANK))

        FIRST = 4

        def store_parts(sp, f):
            a, quarter = QK[f]
            b = quarter * BANK // S
            cols = slice(quarter * BANK, (quarter + 1) * BANK)
            for i, part_done in enumerate((high_done, middle_done, low_done)):
                sp.wait_ge(part_done, f + 1)
                sp.dma_start(d["parts"][a, b:b + BANK // S, i * P:(i + 1) * P, :].rearrange("b p s -> p b s"),
                             parts[a][i][:, cols].rearrange("p (b s) -> p b s", s=S)
                             ).then_inc(written if quarter else written_first, 16)

        with nc.Block() as block:

            @block.sync
            def _(sp):
                for f in range(FIRST):
                    store_parts(sp, f)
                sp.wait_ge(written_first, 16 * 3 * 2)
                stack_up(sp, 0, 0)

            @block.gpsimd
            def _(pool):
                pool.memset(spare[:, :, 0:P], 0.0).then_inc(spare_ready, 1)
                pool.tensor_copy(spare[:, :, P], prog.route_consts[:, R_SPARE:R_SPARE + SLOT_TILES]).then_inc(spare_ready, 1)
                pool.memset(vaug[:, :, :, :], 0.0).then_inc(vones, 1)
                pool.wait_ge(vones, 1)
                pool.memset(vaug[:, :, :, HD:HD + 1], 1.0).then_inc(vones, 1)
                pool.memset(minus[:, :], -1.0).then_inc(vones, 1)
                for f in range(len(QK)):
                    pool.wait_ge(middle_done, f + 1)
                    _, middle, low, cols = split_of(f)
                    pool.tensor_tensor(low[:, cols], rest[f % 4][:, :], middle[:, cols], ALU.subtract).then_inc(low_done, 1)

            @block.vector
            def _(dve):
                dve.tensor_tensor(wkvT[:, :], wkvT[:, :], wvT[:, :], ALU.add).then_inc(wsum, 1)
                dve.wait_ge(eff_step, 1)
                dve.tensor_copy(downT[:, :], misc_b[0:32, 0:P]).then_inc(eff_evac, 1)
                dve.wait_ge(eff_step, 2)
                dve.tensor_copy(wkv_eff[:, :, :], quad_b[:, 0:2 * P].rearrange("p (a c) -> p a c", a=2)).then_inc(eff_evac, 1)

                for f in range(len(QK)):
                    high, middle, _, cols = split_of(f)
                    dve.wait_ge(high_done, f + 1)
                    dve.wait_ge(whole_done, f + 1)
                    wait(dve, low_done, f - 3)
                    dve.tensor_tensor(rest[f % 4][:, :], whole[f % 4][:, :], high[:, cols], ALU.subtract).then_inc(rest_done, 1)
                    dve.wait_ge(rest_done, f + 1)
                    dve.tensor_copy(middle[:, cols], rest[f % 4][:, :]).then_inc(middle_done, 1)
                for f in range(len(QK) + 1, FILLS, 2):
                    dve.wait_ge(projected_in, f + 1)
                    dve.tensor_copy(v[:, (f - len(QK)) * 4:(f - len(QK) + 1) * 4, :].rearrange("p t c -> p (t c)"), proj_b[f % 4][:, :]).then_inc(evac_v, 1)

            @block.tensor
            def _(pe):
                def fill(f):
                    wait(pe, high_done, min(f - 3, len(QK)))
                    if f < len(QK):
                        a, quarter = QK[f]
                        pe.matmul(proj_b[f % 4][:, :], wkv_eff[:, 0, :] if a else wq[:, :], xnT[:, quarter * BANK:(quarter + 1) * BANK],
                                  start=True, stop=True).then_inc(projected_in, 1)
                        return
                    for t in range(4):
                        tok = ((f - len(QK)) * 4 + t) * P
                        last = pe.matmul(proj_b[f % 4][:, t * P:(t + 1) * P], xnT[:, tok:tok + P], wkv_eff[:, 1, :],
                                         start=True, stop=True)
                    last.then_inc(projected_in, 1)

                fill(0)
                pe.wait_ge(wsum, 1)
                pe.matmul(misc_b[0:32, 0:P], wdown[:, :], wkvT[:, :], start=True, stop=True).then_inc(eff_step, 1)
                fill(1)
                pe.wait_ge(eff_evac, 1)
                pe.matmul(quad_b[:, 0:2 * P], downT[:, :], wup[:, :, :].rearrange("p a c -> p (a c)"),
                          start=True, stop=True).then_inc(eff_step, 1)
                pe.wait_ge(eff_evac, 2)
                for f in range(2, FILLS):
                    fill(f)

            @block.scalar
            def _(act):
                for f, (a, quarter) in enumerate(QK):
                    scale = 1.0 if a else SCALE
                    act.wait_ge(projected_in, f + 1)
                    wait(act, rest_done, f - 3)
                    act.activation(whole[f % 4][:, :], proj_b[f % 4][:, :], ACT.Copy, scale=scale).then_inc(whole_done, 1)
                    high, _, _, cols = split_of(f)
                    act.activation(high[:, cols], proj_b[f % 4][:, :], ACT.Copy, scale=scale).then_inc(high_done, 1)
                for f in range(len(QK), FILLS, 2):
                    act.wait_ge(projected_in, f + 1)
                    act.activation(v[:, (f - len(QK)) * 4:(f - len(QK) + 1) * 4, :].rearrange("p t c -> p (t c)"), proj_b[f % 4][:, :],
                                   ACT.Copy).then_inc(evac_a, 1)

        block = stack.enter_context(nc.Block())
        LAST_STEP = 16

        def sequences(engine, steps):
            steps(0, range(H), lambda n: n >= 0, 0)
            with engine.Fori(1, B - 1, 2) as b:
                for half in (1, 0):
                    steps(b + 1 - half, range(H), lambda n: True, half)
            steps(B - 1, range(H), lambda n: True, (B - 1) % 2)
            steps(B, range(LAST_STEP), lambda n: n < 0, 0)

        @block.sync
        def _(sp):
            stack_up(sp, 1, 1)
            for f in range(FIRST, len(QK)):
                store_parts(sp, f)
            sp.wait_ge(written, 16 * 18)
            with sp.Fori(2, B - 1, 2) as b:
                for half in (0, 1):
                    stack_up(sp, b + half, half)
            for tag in ("f1", "f2"):
                sp.dma_start(d["sorted_x_" + tag].rearrange("(j p) c -> p j c", p=P), spare[:, :, :]).then_inc(spare_written, 16)
            sp.dma_start(d["out"][NTOK:NTOK + SLOT_TILES * P, :].rearrange("(j p) c -> p j c", p=P), spare[:, :, 0:P]).then_inc(spare_written, 16)
            sp.wait_ge(spare_written, 48)

        @block.tensor
        def _(pe):
            def steps(b, numbers, live, half):
                for s in numbers:
                    if live(s):
                        if s == 0:
                            wait(pe, stacked, (b + 1) * NSTACK * 16)
                        wait(pe, clipped, b * H + s - 1)
                        for q in range(QT):
                            last = pe.matmul(score_b[s % 2][:, q * S:(q + 1) * S], stack_q[half][:, s, q * P:(q + 1) * P],
                                             stack_k[half][:, s, :], start=True, stop=True)
                        last.then_inc(scored, 1)
                    n = s - 4
                    if live(n):
                        wait(pe, exped, (b * H + n + 1) * QT)
                        wait(pe, pt_ready, b * H + n - 1)
                        for k in range(QT):
                            for q in range(QT):
                                last = pe.transpose(trans_b[n % 2][:, k * S + q * P:k * S + (q + 1) * P],
                                                    pr[n % 4][:, q * S + k * P:q * S + (k + 1) * P], ident[:, :])
                        last.then_inc(ptrans, 1)
                    g, at = (s - 9) // GH, (s - 9) % GH == 0
                    if at and live(g):
                        wait(pe, pt_ready, b * H + (g + 1) * GH)
                        wait(pe, vaug_ready, b * GROUPS + g + 1)
                        wait(pe, ot_ready, b * GROUPS + g - 1)
                        for k in range(QT):
                            for j in range(GH):
                                h = (g * GH + j) % H
                                last = pe.matmul(out_b[g % 2][32 * j:32 * j + 32, 0:S], vaug[:, k, h, :],
                                                 prT[h % 8][:, k * S:(k + 1) * S], start=(k == 0), stop=(k == QT - 1))
                        last.then_inc(attended, 1)
                    g, at = (s - 12) // GH, (s - 12) % GH == 0
                    if at and live(g):
                        wait(pe, ot_ready, b * GROUPS + g + 1)
                        wait(pe, normed, b * GROUPS + g)
                        for q in range(QT):
                            last = pe.transpose(quad_b[:, q * P:(q + 1) * P], oT[:, q * P:(q + 1) * P], ident[:, :])
                        last.then_inc(ot_trans, 1)
                    if s == 12 and live(-1):
                        wait(pe, normed, b * GROUPS)
                        for q in range(QT):
                            last = pe.transpose(misc_b[:, q * P:(q + 1) * P], on[:, q, :], ident[:, :])
                        last.then_inc(on_trans, 1)
                    if s == 15 and live(-1):
                        wait(pe, ont_ready, b)
                        for q in range(QT):
                            last = pe.matmul(misc_b[:, q * P:(q + 1) * P], onT[:, q * P:(q + 1) * P], wo[:, :],
                                             start=True, stop=True)
                        last.then_inc(projected, 1)

            sequences(pe, steps)

        @block.vector
        def _(dve):
            def steps(b, numbers, live, half):
                for s in numbers:
                    n = s - 1
                    if live(n):
                        wait(dve, clipped, b * H + n + 1)
                        wait(dve, exped, (b * H + n - 3) * QT)
                    if live(s):
                        wait(dve, scored, b * H + s + 1)
                        dve.tensor_scalar(sc[s % 4][:, :], score_b[s % 2][:, :], -CLAMP, CLAMP, ALU.max, ALU.min).then_inc(clipped, 1)
                    if live(n):
                        for q in range(QT):
                            dve.tensor_tensor_reduce(
                                out=sd[n % 4][:, q * S:(q + 1) * S], in0=sc[n % 4][:, q * S:(q + 1) * S], in1=decay[:, q, :],
                                scale=1.0, scalar=-3.0e38, op0=ALU.mult, op1=ALU.max,
                                accum_out=rowmax[:, n % H, q:q + 1]).then_inc(decayed, 1)
                    g, at = (s - 14) // GH, (s - 14) % GH == 0
                    if at and live(g):
                        wait(dve, ot_trans, b * GROUPS + g + 1)
                        if g >= 0:
                            wait(dve, on_trans, b)
                        heads = quad_b[:, 0:QT * P].rearrange("p (q j c) -> p q j c", q=QT, j=GH)
                        dve.reciprocal(rden[:, :, :], heads[:, :, :, HD]).then_inc(rden_ready, 1)
                        wait(dve, rden_ready, b * GROUPS + g + 1)
                        for q in range(QT):
                            last = dve.tensor_tensor(on[:, q, (g % GROUPS) * 32:(g % GROUPS + 1) * 32].rearrange("p (j c) -> p j c", j=GH),
                                                     heads[:, q, :, 0:HD],
                                                     rden[:, q, :].unsqueeze(2).to_broadcast([P, GH, HD]), ALU.mult)
                        last.then_inc(normed, 1)
                    if s == 15 and live(-1):
                        wait(dve, projected, b)
                        xs = x[:, bass.ds(b * QT - QT, QT), :]
                        dve.tensor_tensor(xs, misc_b[:, 0:QT * P].rearrange("p (q c) -> p q c", q=QT), xs, ALU.add).then_inc(added, 1)

            sequences(dve, steps)

        @block.gpsimd
        def _(pool):
            def sequence(b, first):
                for s in range(H):
                    wait(pool, decayed, (b * H + s + 1) * QT)
                    pool.tensor_tensor(negmax[:, s, :], rowmax[:, s, :], minus[:, :], ALU.mult).then_inc(negated, 1)
                    if s % 2 and s < 2 * GROUPS:
                        g = s // 2
                        if not first:
                            pool.wait_ge(attended, b * GROUPS - GROUPS + g + 1)
                        pool.tensor_copy(vaug[:, :, g * GH:(g + 1) * GH, 0:HD],
                                         v[:, bass.ds(b * QT, QT), g * 32:(g + 1) * 32].rearrange("p q (j c) -> p q j c", j=GH),
                                         ).then_inc(vaug_ready, 1)

            sequence(0, True)
            with pool.Fori(1, B) as b:
                sequence(b, False)

        @block.scalar
        def _(act):
            def steps(b, numbers, live, half):
                for s in numbers:
                    if live(s):
                        wait(act, ptrans, b * H + s - 3)
                        wait(act, negated, b * H + s + 1)
                        for q in range(QT):
                            act.activation(pr[s % 4][:, q * S:(q + 1) * S], sd[s % 4][:, q * S:(q + 1) * S], ACT.Exp,
                                           bias=negmax[:, s, q:q + 1]).then_inc(exped, 1)
                    n = s - 2
                    if live(n):
                        wait(act, ptrans, b * H + n + 1)
                        wait(act, attended, b * GROUPS + n // GH - 1)
                        act.activation(prT[n % 8][:, :], trans_b[n % 2][:, :], ACT.Copy).then_inc(pt_ready, 1)
                    g, at = (s - 8) // GH, (s - 8) % GH == 0
                    if at and live(g):
                        wait(act, attended, b * GROUPS + g + 1)
                        wait(act, ot_trans, b * GROUPS + g)
                        act.activation(oT[:, :], out_b[g % 2][:, 0:S], ACT.Copy).then_inc(ot_ready, 1)
                    if s == 11 and live(-1):
                        wait(act, on_trans, b)
                        act.activation(onT[:, :], misc_b[:, 0:S], ACT.Copy).then_inc(ont_ready, 1)

            sequences(act, steps)


R_LESS, R_THRESH, R_TILE, R_ONES, R_TOKEN, R_SPARE, R_END = 0, 8, 24, 48, 64, 80, 104


def experts_phase(prog, d, tag, out=None):
    nc = prog.nc
    x, xn, ident, rc = prog.x, prog.xn, prog.ident, prog.route_consts
    U = 8
    B1, B2 = 2 * HID, 2 * HID + HC
    with ExitStack() as stack:
        sb, bank = buffers(nc, stack, tag)
        logits = prog.logits
        best = sb("best", [P, NT])
        work = sb("work", [P, NT, E_N])
        first = sb("first", [P, NT])
        onehot = sb("onehot", [P, NT, E_N], BF16)
        upto = sb("upto", [P, E_N, NT])
        over = sb("over", [P, E_N, NT])
        tiles = sb("tiles", [P, E_N])
        tile_end = sb("tile_end", [P, E_N])
        tile_start = sb("tile_start", [P, E_N])
        slot_f = sb("slot_f", [P, NT])
        slot = sb("slot", [P, NT], U32)
        before = sb("before", [P, SLOT_TILES, E_N])
        owner_f = sb("owner_f", [P, SLOT_TILES])
        owner = sb("owner", [P, SLOT_TILES], U32)
        sorted_sb = sb("sorted_sb", [P, SLOT_TILES, XW])
        sortedT = sb("sortedT", [P, SLOT_TILES * P])
        token = sb("token", [P, SLOT_TILES], U32)
        y_sorted = sb("y_sorted", [P, SLOT_TILES, P])
        y_tok = sb("y_tok", [P, NT, P])
        W = [sb(f"W{u}", [P, EW]) for u in range(U)]
        hT = [sb(f"hT{u}", [P, HC, P]) for u in range(4)]
        banks = [bank(f"b{i}") for i in range(8)]
        rank_b = banks[4]

        (onehot_done, counted, slots_done, owners_done, chain, scattered, transposed, evac_a, evac_v,
         tokens_done, hidden_done, relu_a, relu_v, out_done, y_ready, y_scattered, added, stored) = prog.semaphores(
            tag, "onehot_done counted slots_done owners_done chain scattered transposed evac_a evac_v "
                 "tokens_done hidden_done relu_a relu_v out_done y_ready y_scattered added stored")
        GROUPS_T = SLOT_TILES // 4
        PASSES = SLOT_TILES // U
        QUARTER = NT // 4
        sorted_loaded = [prog.sem(f"{tag}_sorted_loaded{q}") for q in range(GROUPS_T)]
        fetched = [prog.sem(f"{tag}_fetched{u}") for u in range(U)]
        y_loaded = [prog.sem(f"{tag}_y_loaded{q}") for q in range(4)]
        sorted_x = d["sorted_x_" + tag]
        with nc.Block() as block:

            def passes(engine, steps):
                steps(0, range(U), lambda n: n >= 0)
                with engine.Fori(1, PASSES) as i:
                    steps(i, range(U), lambda n: True)
                steps(PASSES, range(1), lambda n: n < 0)

            @block.sync
            def _(sp):
                def fetch(i, u, first):
                    if not first:
                        sp.wait_ge(y_ready, i * U + (u - U + 1))
                    e = sp.value_load(owner[0:1, bass.ds(i * U + u, 1)], min_val=0, max_val=E_N - 1)
                    sp.dma_start(W[u][:, :], d["experts"][bass.ds(e * P, P), :]).then_inc(fetched[u], 16)

                if out is not None:
                    sp.dma_start(out[0:NTOK, :].rearrange("(t p) c -> p t c", p=P), x[:, :, :]).then_inc(stored, 16)
                sp.wait_ge(owners_done, 1)
                for u in range(U):
                    fetch(0, u, True)
                sp.wait_ge(scattered, 16 * NT)
                for q in range(GROUPS_T):
                    sp.dma_start(sorted_sb[:, q * 4:q * 4 + 4, :],
                                 sorted_x.rearrange("(j p) c -> p j c", p=P)[:, q * 4:q * 4 + 4, :]).then_inc(sorted_loaded[q], 16)
                with sp.Fori(1, PASSES) as i:
                    for u in range(U):
                        fetch(i, u, False)
                sp.wait_ge(y_scattered, 16 * SLOT_TILES)
                for q in range(4 if out is None else 0):
                    tiles = slice(q * QUARTER, (q + 1) * QUARTER)
                    sp.dma_start(y_tok[:, tiles, :],
                                 d["y_tok"][0:NTOK, :].rearrange("(t p) c -> p t c", p=P)[:, tiles, :]).then_inc(y_loaded[q], 16)

            @block.tensor
            def _(pe):
                pe.wait_ge(onehot_done, 1)
                oh = onehot[:, :, :].rearrange("p t e -> p (t e)")
                pe.matmul(rank_b[:, 0:NT * E_N], prog.tri[:, :], oh, start=True, stop=True)
                pe.matmul(rank_b[:, NT * E_N:2 * NT * E_N], prog.ones_b[:, :], oh, start=True, stop=True).then_inc(counted, 1)
                for q in range(GROUPS_T):
                    if q >= 4:
                        pe.wait_ge(evac_v if q % 2 else evac_a, (q - 4) // 2 + 1)
                    pe.wait_ge(sorted_loaded[q], 16)
                    for t in range(4):
                        last = pe.transpose(banks[q % 4][:, t * P:(t + 1) * P], sorted_sb[:, q * 4 + t, 0:P], ident[:, :])
                    last.then_inc(transposed, 1)
                pe.wait_ge(evac_a, GROUPS_T // 2)
                pe.wait_ge(evac_v, GROUPS_T // 2)

                def steps(i, numbers, live):
                    for s in numbers:
                        if live(s):
                            pe.wait_ge(fetched[s], (i + 1) * 16)
                            wait(pe, relu_a, i * U + s - 1)
                            wait(pe, relu_v, i * U + s - 1)
                            for c in range(HC):
                                last = pe.matmul(banks[(s % 2) * 2 + c // 2][:, (c % 2) * P:(c % 2 + 1) * P],
                                                 W[s][:, c * P:(c + 1) * P], sortedT[:, bass.ds((i * U + s) * P, P)],
                                                 start=True, stop=True)
                            last.then_inc(hidden_done, 1)
                        n = s - 1
                        if live(n):
                            u = n % U
                            wait(pe, relu_a, i * U + n + 1)
                            wait(pe, relu_v, i * U + n + 1)
                            wait(pe, y_ready, i * U + n - 1)
                            for c in range(HC):
                                last = pe.matmul(banks[4 + u % 2][:, 0:P], hT[u % 4][:, c, :], W[u][:, HID + c * P:HID + (c + 1) * P],
                                                 start=(c == 0), stop=(c == HC - 1))
                            last.then_inc(out_done, 1)

                passes(pe, steps)

            @block.vector
            def _(dve):
                links = [0]

                def link(instruction):
                    links[0] += 1
                    instruction.then_inc(chain, 1)
                    dve.wait_ge(chain, links[0])

                def over_e(a):
                    return a.unsqueeze(2).to_broadcast([P, a.shape[1], E_N])

                def over_t(a, n=NT):
                    return a.unsqueeze(1).to_broadcast([P, n, E_N])

                less = over_t(rc[:, R_LESS:R_LESS + E_N])
                link(dve.tensor_reduce(best[:, :], logits[:, :, :], AX.X, ALU.max))
                link(dve.tensor_tensor(work[:, :, :], logits[:, :, :], over_e(best[:, :]), ALU.is_equal))
                link(dve.tensor_tensor(work[:, :, :], work[:, :, :], less, ALU.mult))
                link(dve.tensor_reduce(first[:, :], work[:, :, :], AX.X, ALU.min))
                dve.tensor_tensor(onehot[:, :, :], less, over_e(first[:, :]), ALU.is_equal).then_inc(onehot_done, 1)
                dve.wait_ge(onehot_done, 1)
                dve.wait_ge(counted, 1)
                lower = rank_b[:, 0:NT * E_N].rearrange("p (t e) -> p t e", e=E_N)
                total = rank_b[:, NT * E_N:2 * NT * E_N].rearrange("p (t e) -> p t e", e=E_N)
                for e in range(E_N):
                    last = dve.tensor_tensor_scan(upto[:, e, :], rc[:, R_ONES:R_ONES + NT], total[:, :, e], 0.0, ALU.mult, ALU.add)
                link(last)
                link(dve.tensor_tensor(over[:, :, :], upto[:, :, NT - 1:NT].to_broadcast([P, E_N, NT]),
                                       rc[:, R_THRESH:R_THRESH + NT].unsqueeze(1).to_broadcast([P, E_N, NT]), ALU.is_gt))
                link(dve.tensor_reduce(tiles[:, :], over[:, :, :], AX.X, ALU.add))
                link(dve.tensor_tensor_scan(tile_end[:, :], rc[:, R_ONES:R_ONES + E_N], tiles[:, :], 0.0, ALU.mult, ALU.add))
                link(dve.tensor_tensor(tile_start[:, :], tile_end[:, :], tiles[:, :], ALU.subtract))
                link(dve.tensor_tensor(work[:, :, :], upto[:, :, :].rearrange("p e t -> p t e"), total, ALU.subtract))
                link(dve.scalar_tensor_tensor(work[:, :, :], over_t(tile_start[:, :]), float(P), work[:, :, :], ALU.mult, ALU.add))
                link(dve.tensor_tensor(work[:, :, :], work[:, :, :], lower, ALU.add))
                link(dve.tensor_tensor(work[:, :, :], work[:, :, :], onehot[:, :, :], ALU.mult))
                link(dve.tensor_reduce(slot_f[:, :], work[:, :, :], AX.X, ALU.add))
                dve.tensor_copy(slot[:, :], slot_f[:, :]).then_inc(slots_done, 1)
                link(dve.tensor_tensor(before[:, :, :], over_t(tile_end[:, :], SLOT_TILES),
                                       over_e(rc[:, R_TILE:R_TILE + SLOT_TILES]), ALU.is_le))
                link(dve.tensor_reduce(owner_f[:, :], before[:, :, :], AX.X, ALU.add))
                dve.tensor_scalar(owner[:, :], owner_f[:, :], E_N - 1.0, None, ALU.min).then_inc(owners_done, 1)
                for q in range(1, GROUPS_T, 2):
                    dve.wait_ge(transposed, q + 1)
                    dve.tensor_copy(sortedT[:, q * BANK:(q + 1) * BANK], banks[q % 4][:, :]).then_inc(evac_v, 1)
                dve.tensor_copy(token[:, :], sorted_sb[:, :, P]).then_inc(tokens_done, 1)

                def steps(i, numbers, live):
                    for s in numbers:
                        if live(s):
                            wait(dve, out_done, i * U + s - 3)
                            wait(dve, hidden_done, i * U + s + 1)
                            for c in (2, 3):
                                last = dve.tensor_scalar(hT[s % 4][:, c, :], banks[(s % 2) * 2 + 1][:, (c - 2) * P:(c - 1) * P],
                                                         W[s][:, B1 + c:B1 + c + 1], 0.0, ALU.add, ALU.max)
                            last.then_inc(relu_v, 1)
                        n = s - 1
                        if live(n):
                            wait(dve, out_done, i * U + n + 1)
                            dve.tensor_tensor(y_sorted[:, bass.ds(i * U + n, 1), :].rearrange("p j c -> p (j c)"), banks[4 + n % 2][:, 0:P],
                                              W[n % U][:, B2:B2 + P], ALU.add).then_inc(y_ready, 1)

                passes(dve, steps)
                for q in range(4 if out is None else 0):
                    part = slice(q * QUARTER, (q + 1) * QUARTER)
                    dve.wait_ge(y_loaded[q], 16)
                    dve.tensor_tensor(x[:, part, :], x[:, part, :], y_tok[:, part, :], ALU.add).then_inc(added, 1)

            @block.gpsimd
            def _(pool):
                pool.wait_ge(slots_done, 1)
                for t in range(NT):
                    pool.indirect_dma_start(out=sorted_x, out_offset=bass.IndirectOffsetOnAxis(ap=slot[:, t:t + 1], axis=0),
                                            in_=xn[:, t, :], in_offset=None).then_inc(scattered, 16)
                pool.wait_ge(tokens_done, 1)
                if out is not None:
                    pool.wait_ge(stored, 16)
                for j in range(SLOT_TILES):
                    pool.wait_ge(y_ready, j + 1)
                    pool.indirect_dma_start(out=d["y_tok"] if out is None else out,
                                            out_offset=bass.IndirectOffsetOnAxis(ap=token[:, j:j + 1], axis=0),
                                            in_=y_sorted[:, j, :], in_offset=None,
                                            compute_op=ALU.bypass if out is None else ALU.add).then_inc(y_scattered, 16)

            @block.scalar
            def _(act):
                for q in range(0, GROUPS_T, 2):
                    act.wait_ge(transposed, q + 1)
                    act.activation(sortedT[:, q * BANK:(q + 1) * BANK], banks[q % 4][:, :], ACT.Copy).then_inc(evac_a, 1)

                def steps(i, numbers, live):
                    for s in numbers:
                        if live(s):
                            wait(act, out_done, i * U + s - 3)
                            wait(act, hidden_done, i * U + s + 1)
                            for c in (0, 1):
                                last = act.activation(hT[s % 4][:, c, :], banks[(s % 2) * 2][:, c * P:(c + 1) * P], ACT.Relu,
                                                      bias=W[s][:, B1 + c:B1 + c + 1])
                            last.then_inc(relu_a, 1)

                passes(act, steps)


def mamba_weights(prog, stack, d):
    sb, _ = buffers(prog.nc, stack, "mw")
    weights = (w_in, conv_w, conv_b, w_x, w_dt, b_dt, a_log, skip, w_out, f_w1, f_b1, f_w2, f_b2, pick) = (
        sb("w_in", [P, 2 * DI]), sb("conv_w", [P, DC, 4]), sb("conv_b", [P, DC]), sb("w_x", [P, DC, DTR + 2 * NS]),
        sb("w_dt", [DTR, DI]), sb("b_dt", [P, DC]), sb("a_log", [P, DC, NS]), sb("skip", [P, DC]), sb("w_out", [P, DC, P]),
        sb("f_w1", [P, HID]), sb("f_b1", [P, HC]), sb("f_w2", [P, HC, P]), sb("f_b2", [P, 1]),
        sb("pick", [96, 2 * NS, P], BF16))
    return weights, ((w_in[:, :], d["in_projT"]), (conv_w[:, :, :], d["conv_w"]), (conv_b[:, :], d["conv_b"]),
                     (w_x[:, :, :], d["x_projT"]), (w_dt[:, :], d["dt_projT"]), (b_dt[:, :], d["dt_b"]),
                     (a_log[:, :, :], d["A_log"]), (skip[:, :], d["D"]), (w_out[:, :, :], d["out_projT"]),
                     (f_w1[:, :], d["ffn_w1T"]), (f_b1[:, :], d["ffn_b1"]), (f_w2[:, :, :], d["ffn_w2T"]),
                     (f_b2[:, :], d["ffn_b2"]), (pick[:, :, :], d["c_pick"].bitcast(BF16)))


def mamba_phase(prog, d, weights):
    nc = prog.nc
    x, xnT, ident = prog.x, prog.xnT, prog.ident
    G = NTOK // BANK
    GS = BANK // S
    with ExitStack() as stack:
        sb, _ = buffers(nc, stack, "m")
        a_exp = sb("a_exp", [P, DC, NS])
        a_neg = sb("a_neg", [P, DC, NS])
        w_in, conv_w, conv_b, w_x, w_dt, b_dt, a_log, skip, w_out, f_w1, f_b1, f_w2, f_b2, pick = weights
        u = sb("u", [P, DC, NTOK])
        sres = sb("sres", [P, DC, NTOK])
        delta = sb("delta", [P, DC, NTOK])
        du = sb("du", [P, DC, NTOK])
        skip_diag = sb("skip_diag", [P, DC, P])
        yz = sb("yz", [P, DC, NTOK])
        bc3 = sb("bc3", [96, NTOK], BF16)

        (xm_done, res_in, conv_first, conv_step, conv_done, res_done, u_done, xdbl_done, dbl_copied, split_step, z_done,
         abs_done, relu_done, exp_done, log_done, ones_done, rest_done, sum_done, delta_done, du_done, a_done, a_negated,
         diag_done) = prog.semaphores(
            "ma", "xm_done res_in conv_first conv_step conv_done res_done u_done xdbl_done dbl_copied split_step z_done "
                  "abs_done relu_done exp_done log_done ones_done rest_done sum_done delta_done du_done a_done a_negated "
                  "diag_done")
        with ExitStack() as inner:
            sbi, bank = buffers(nc, inner, "ma")
            xm_b = [[bank(f"xm{i}{c}") for c in range(DC)] for i in range(2)]
            res_b = bank("res")
            xd_b = bank("xd")
            z_b = [bank(f"z{i}") for i in range(DC)]
            acc = [[sbi(f"acc{i}{c}", [P, GS, S]) for c in range(DC)] for i in range(2)]
            dbl = [sbi(f"dbl{g}", [DTR + 2 * NS, BANK]) for g in range(G)]
            rest1 = sbi("rest1", [32, BANK])
            rest2 = sbi("rest2", [32, BANK])
            middle = sbi("middle", [32, BANK], BF16)
            e_z = sbi("e_z", [P, DC, NTOK])
            relu_z = yz
            NU = G * DC
            BY_POOL = 3
            block = inner.enter_context(nc.Block())

            def of(buffer, k):
                return buffer[:, k % DC, (k // DC) * BANK:(k // DC + 1) * BANK]

            def exp_units(step):
                return range(0 if step == G + 1 else (step - 3) * DC, (step - 2) * DC) if step > G else ()

            @block.tensor
            def _(pe):
                for step in range(G + 3):
                    g = step
                    if g < G:
                        tokens = xnT[:, g * BANK:(g + 1) * BANK]
                        for c in range(DC):
                            wait(pe, conv_done, (g - 2) * DC + c + 1)
                            pe.matmul(xm_b[g % 2][c][:, :], w_in[:, c * P:(c + 1) * P], tokens, start=True, stop=True).then_inc(xm_done, 1)
                            wait(pe, res_done, g * DC + c)
                            pe.matmul(res_b[:, :], w_in[:, DI + c * P:DI + (c + 1) * P], tokens, start=True, stop=True).then_inc(res_in, 1)
                    g = step - 2
                    if 0 <= g < G:
                        wait(pe, dbl_copied, g)
                        pe.wait_ge(u_done, (g + 1) * DC)
                        for c in range(DC):
                            last = pe.matmul(xd_b[0:DTR + 2 * NS, :], w_x[:, c, :], of(u, g * DC + c),
                                             start=(c == 0), stop=(c == DC - 1))
                        last.then_inc(xdbl_done, 1)
                    g = step - 3
                    if g >= 0:
                        pe.wait_ge(dbl_copied, g + 1)
                        for k in range(g * DC, (g + 1) * DC):
                            wait(pe, abs_done, k - DC + 1)
                            wait(pe, relu_done, k - DC + 1)
                            pe.matmul(z_b[k % DC][:, :], w_dt[:, (k % DC) * P:(k % DC + 1) * P], dbl[g][0:DTR, :],
                                      start=True, stop=True).then_inc(z_done, 1)

            @block.scalar
            def _(act):
                for step in range(G + 3):
                    g = step
                    if g < G:
                        for c in range(DC):
                            act.wait_ge(xm_done, g * DC + c + 1)
                            wait(act, u_done, (g - 2) * DC + c + 1)
                            act.activation(acc[g % 2][c][:, :, :].rearrange("p a s -> p (a s)"), xm_b[g % 2][c][:, :], ACT.Identity,
                                           bias=conv_b[:, c:c + 1], scale=conv_w[:, c, 3:4]).then_inc(conv_first, 1)
                            act.wait_ge(res_in, g * DC + c + 1)
                            act.activation(of(sres, g * DC + c), res_b[:, :], ACT.Silu).then_inc(res_done, 1)
                    g = step - 1
                    if 0 <= g < G:
                        for k in range(g * DC, (g + 1) * DC):
                            act.wait_ge(conv_done, k + 1)
                            act.activation(of(u, k), acc[g % 2][k % DC][:, :, :].rearrange("p a s -> p (a s)"), ACT.Silu).then_inc(u_done, 1)
                    g = step - 2
                    if 0 <= g < G:
                        act.wait_ge(xdbl_done, g + 1)
                        act.activation(dbl[g][:, :], xd_b[0:DTR + 2 * NS, :], ACT.Copy).then_inc(dbl_copied, 1)
                    g = step - 3
                    if g >= 0:
                        for k in range(g * DC, (g + 1) * DC):
                            act.wait_ge(z_done, k + 1)
                            act.activation(of(e_z, k), z_b[k % DC][:, :], ACT.Abs, bias=b_dt[:, k % DC:k % DC + 1]).then_inc(abs_done, 1)
                            act.activation(of(relu_z, k), z_b[k % DC][:, :], ACT.Relu, bias=b_dt[:, k % DC:k % DC + 1]).then_inc(relu_done, 1)
                    for k in exp_units(step):
                        act.wait_ge(abs_done, k + 1)
                        act.activation(of(e_z, k), of(e_z, k), ACT.Exp, scale=-1.0).then_inc(exp_done, 1)
                act.activation(a_exp[:, :, :], a_log[:, :, :], ACT.Exp).then_inc(a_done, 1)
                for k in range(NU):
                    act.wait_ge(exp_done, k + 1)
                    act.activation(of(delta, k), of(e_z, k), ACT.Ln, bias=1.0).then_inc(log_done, 1)

            @block.vector
            def _(dve):
                steps = [0]

                def split(instruction):
                    steps[0] += 1
                    instruction.then_inc(split_step, 1)
                    dve.wait_ge(split_step, steps[0])

                for c in range(DC):
                    dve.tensor_scalar(skip_diag[:, c, :], ident[:, :], skip[:, c:c + 1], None, ALU.mult).then_inc(diag_done, 1)
                for step in range(G + 3):
                    g = step
                    if g < G:
                        for k in (2, 1, 0):
                            back = 3 - k
                            for c in range(DC):
                                if k == 2:
                                    dve.wait_ge(conv_first, g * DC + c + 1)
                                else:
                                    dve.wait_ge(conv_step, (g * 2 + 1 - k) * DC + c + 1)
                                src = xm_b[g % 2][c][:, :].rearrange("p (a s) -> p a s", a=GS)[:, :, 0:S - back]
                                to = acc[g % 2][c][:, :, back:S]
                                tap = dve.scalar_tensor_tensor(to, src, conv_w[:, c, k:k + 1], to, ALU.mult, ALU.add)
                                if k == 0:
                                    tap.then_inc(conv_done, 1)
                                else:
                                    tap.then_inc(conv_step, 1)
                    g = step - 2
                    if 0 <= g < G:
                        cols = slice(g * BANK, (g + 1) * BANK)
                        both = dbl[g][DTR:DTR + 2 * NS, :]
                        dve.wait_ge(dbl_copied, g + 1)
                        split(dve.tensor_copy(bc3[0:32, cols], both))
                        split(dve.tensor_tensor(rest1[:, :], both, bc3[0:32, cols], ALU.subtract))
                        split(dve.tensor_copy(middle[:, :], rest1[:, :]))
                        split(dve.tensor_copy(bc3[32:64, cols], middle[:, :]))
                        split(dve.tensor_tensor(rest2[:, :], rest1[:, :], middle[:, :], ALU.subtract))
                        split(dve.tensor_copy(bc3[64:96, cols], rest2[:, :]))
                    for k in exp_units(step):
                        dve.wait_ge(exp_done, k + 1)
                        dve.tensor_scalar(of(du, k), of(e_z, k), 1.0, -1.0, ALU.add, ALU.add).then_inc(ones_done, 1)
                    for k in exp_units(step):
                        dve.wait_ge(ones_done, k + 1)
                        dve.tensor_tensor(of(du, k), of(e_z, k), of(du, k), ALU.subtract).then_inc(rest_done, 1)
                dve.wait_ge(a_done, 1)
                dve.tensor_scalar(a_neg[:, :, :], a_exp[:, :, :], -1.0, None, ALU.mult).then_inc(a_negated, 1)
                for k in range(NU):
                    dve.wait_ge(log_done, k + 1)
                    dve.wait_ge(sum_done, k + 1)
                    dve.tensor_tensor(of(delta, k), of(delta, k), of(relu_z, k), ALU.add).then_inc(delta_done, 1)
                for k in range(BY_POOL, NU):
                    dve.wait_ge(delta_done, k + 1)
                    dve.tensor_tensor(of(du, k), of(delta, k), of(u, k), ALU.mult).then_inc(du_done, 1)

            @block.gpsimd
            def _(pool):
                for k in range(NU):
                    pool.wait_ge(relu_done, k + 1)
                    pool.wait_ge(rest_done, k + 1)
                    pool.tensor_tensor(of(relu_z, k), of(relu_z, k), of(du, k), ALU.add).then_inc(sum_done, 1)
                for k in range(BY_POOL):
                    pool.wait_ge(delta_done, k + 1)
                    pool.tensor_tensor(of(du, k), of(delta, k), of(u, k), ALU.mult).then_inc(du_done, 1)

        (dA_zeroed, b_done, c_done, b_copied, dA_done, dBu_done, h_done, hc_done, y_done, y_evac) = prog.semaphores(
            "mc", "dA_zeroed b_done c_done b_copied dA_done dBu_done h_done hc_done y_done y_evac")
        with ExitStack() as inner:
            sbi, bank = buffers(nc, inner, "mc")
            y_b = [bank(f"y{c}") for c in range(DC)]
            b_b = [bank(f"b{i}") for i in range(2)]
            c_b = [bank(f"c{i}") for i in range(2)]
            dA_b = [bank(f"dA{i}") for i in range(2)]
            b_s = [sbi(f"bs{i}", [P, BANK]) for i in range(4)]
            dBu = [sbi(f"dBu{i}", [P, BANK]) for i in range(4)]
            h = [sbi(f"h{i}", [P, BANK]) for i in range(4)]
            hc = [sbi(f"hc{i}", [P, BANK]) for i in range(8)]
            NUNITS = DC * NS
            AHEAD = 2
            LAG = 7
            delta_cur = [sbi(f"delta_cur{c}", [P, GS, S]) for c in range(DC)]
            delta_tail = [sbi(f"delta_tail{c}", [P, GS, S]) for c in range(DC)]
            delta_loaded = [prog.sem(f"mc_delta_loaded{c}") for c in range(DC)]
            tail_loaded = [prog.sem(f"mc_tail_loaded{c}") for c in range(DC)]
            block = inner.enter_context(nc.Block())

            def cols(g):
                return bass.ds(g * BANK, BANK)

            def passes(engine, steps):
                steps(0, range(NUNITS), lambda n: n >= 0)
                with engine.Fori(1, G) as g:
                    steps(g, range(NUNITS), lambda n: True)
                steps(G, range(LAG), lambda n: n < 0)

            @block.tensor
            def _(pe):
                def steps(g, numbers, live):
                    for s in numbers:
                        n, c = s // DC, s % DC
                        if live(s) and c == 0:
                            wait(pe, b_copied, g * NS + n - 1)
                            pe.matmul(b_b[n % 2][:, :], pick[:, n, :], bc3[:, cols(g)], start=True, stop=True).then_inc(b_done, 1)
                        if live(s - AHEAD) and c == 0:
                            m = n - AHEAD // DC
                            wait(pe, hc_done, (g * NS + m - 1) * DC)
                            at = cols(g if m >= 0 else g - 1)
                            pe.matmul(c_b[m % 2][:, :], pick[:, NS + m % NS, :], bc3[:, at], start=True, stop=True).then_inc(c_done, 1)
                        k = s - LAG
                        if live(k):
                            n, c = (k % NUNITS) // DC, k % DC
                            wait(pe, hc_done, g * NUNITS + k + 1)
                            if n == 0:
                                wait(pe, y_evac, (g - 1) * DC + c + 1)
                                pe.matmul(y_b[c][:, :], skip_diag[:, c, :], u[:, c, cols(g)], start=True, stop=False)
                            last = pe.matmul(y_b[c][:, :], ident[:, :], hc[k % 8][:, :], start=False, stop=(n == NS - 1))
                            last.then_inc(y_done, 1)

                passes(pe, steps)

            @block.scalar
            def _(act):
                act.wait_ge(dA_zeroed, 2)

                def steps(g, numbers, live):
                    for s in numbers:
                        n, c = s // DC, s % DC
                        if live(s) and c == 0:
                            wait(act, b_done, g * NS + n + 1)
                            wait(act, dBu_done, (g * NS + n - 3) * DC)
                            act.activation(b_s[n % 4][:, :], b_b[n % 2][:, :], ACT.Copy).then_inc(b_copied, 1)
                        k = s - AHEAD
                        if live(k):
                            wait(act, h_done, g * NUNITS + k - 1)
                            m = (k % NUNITS) // DC
                            source, loaded = (delta_tail, tail_loaded) if m == NS - 1 else (delta_cur, delta_loaded)
                            wait(act, loaded[c], (g + (k >= 0)) * 16)
                            act.activation(dA_b[k % 2][:, :].rearrange("p (a s) -> p a s", a=GS)[:, :, 1:S],
                                           source[c][:, :, 1:S], ACT.Exp,
                                           scale=a_neg[:, c, m:m + 1]).then_inc(dA_done, 1)

                passes(act, steps)

            @block.sync
            def _(sp):
                def one_pass(g):
                    for to, loaded, left in ((delta_cur, delta_loaded, DC), (delta_tail, tail_loaded, 0)):
                        for c in range(DC):
                            wait(sp, dA_done, g * NUNITS - left - (DC - 1 - c))
                            sp.dma_start(to[c][:, :, :].rearrange("p a s -> p (a s)"), delta[:, c, cols(g)]).then_inc(loaded[c], 16)

                one_pass(0)
                with sp.Fori(1, G) as g:
                    one_pass(g)

            @block.gpsimd
            def _(pool):
                def units(g, i):
                    for s in range(UNROLL):
                        n, c = s // DC, s % DC
                        done = i * UNROLL + g * NUNITS + s
                        wait(pool, h_done, done - 3)
                        wait(pool, b_copied, i * (UNROLL // DC) + g * NS + n + 1)
                        pool.tensor_tensor(dBu[s % 4][:, :], du[:, c, g * BANK:(g + 1) * BANK], b_s[n % 4][:, :],
                                           ALU.mult).then_inc(dBu_done, 1)

                UNROLL = 4 * DC
                units(0, 0)
                for g in range(G):
                    with pool.Fori(0 if g else 1, NUNITS // UNROLL) as i:
                        units(g, i)

            @block.vector
            def _(dve):
                for i in range(2):
                    dve.memset(dA_b[i][:, :], 0.0).then_inc(dA_zeroed, 1)

                def steps(g, numbers, live):
                    for s in numbers:
                        if live(s):
                            wait(dve, dA_done, g * NUNITS + s + 1)
                            wait(dve, dBu_done, g * NUNITS + s + 1)
                            wait(dve, hc_done, g * NUNITS + s - 3)
                            dve.tensor_tensor_scan(h[s % 4][:, :], dA_b[s % 2][:, :], dBu[s % 4][:, :], 0.0, ALU.mult, ALU.add).then_inc(h_done, 1)
                        k = s - 1
                        if live(k):
                            n = (k % NUNITS) // DC
                            wait(dve, h_done, g * NUNITS + k + 1)
                            wait(dve, c_done, g * NS + k // DC + 1)
                            wait(dve, y_done, g * NUNITS + k - 7)
                            dve.tensor_tensor(hc[k % 8][:, :], h[k % 4][:, :], c_b[n % 2][:, :], ALU.mult).then_inc(hc_done, 1)
                        if s == 3 and live(-1):
                            for c in range(DC):
                                wait(dve, y_done, g * NUNITS - DC + c + 1)
                                dve.tensor_tensor(yz[:, c, cols(g - 1)], y_b[c][:, :], sres[:, c, cols(g - 1)], ALU.mult).then_inc(y_evac, 1)

                passes(dve, steps)

        (m_done, m_copied, f1_done, gelu_done, f2_done, c_summed, stat_done, moments, mean_done, mean_copied, dev_step, var_done,
         var_copied, std_done, rstd_done, c_normed, c_trans, added) = prog.semaphores(
            "md", "m_done m_copied f1_done gelu_done f2_done c_summed stat_done moments mean_done mean_copied dev_step var_done "
                  "var_copied std_done rstd_done c_normed c_trans added")
        with ExitStack() as inner:
            sbi, bank = buffers(nc, inner, "md")
            m_b = [bank(f"m{i}") for i in range(2)]
            f_b = [bank(f"f{i}") for i in range(4)]
            o_b = bank("o")
            s_b = bank("s")
            mT = [sbi(f"mT{i}", [P, BANK]) for i in range(2)]
            gl = [[sbi(f"gl{i}{c}", [P, BANK]) for c in range(HC)] for i in range(2)]
            cT = sbi("cT", [P, B, S])
            cn = sbi("cn", [P, NT, P])
            stats = sbi("stats", [P, B, 6])
            mom = sbi("mom", [P, B, 2])
            mean = sbi("mean", [P, B])
            dev = sbi("dev", [P, B])
            dev2 = sbi("dev2", [P, B])
            part_var = sbi("part_var", [P, B])
            var = sbi("var", [P, B])
            std = sbi("std", [P, B])
            rstd = sbi("rstd", [P, B])
            block = inner.enter_context(nc.Block())

            @block.tensor
            def _(pe):
                def out_proj(g):
                    wait(pe, m_copied, g - 1)
                    for c in range(DC):
                        last = pe.matmul(m_b[g % 2][:, :], w_out[:, c, :], yz[:, c, g * BANK:(g + 1) * BANK],
                                         start=(c == 0), stop=(c == DC - 1))
                    last.then_inc(m_done, 1)

                out_proj(0)
                for g in range(G):
                    pe.wait_ge(m_copied, g + 1)
                    for c in range(HC):
                        wait(pe, gelu_done, (g - 1) * HC + c + 1)
                        pe.matmul(f_b[c][:, :], f_w1[:, c * P:(c + 1) * P], mT[g % 2][:, :], start=True, stop=True).then_inc(f1_done, 1)
                    if g + 1 < G:
                        out_proj(g + 1)
                    wait(pe, c_summed, g)
                    for c in range(HC):
                        pe.wait_ge(gelu_done, g * HC + c + 1)
                        last = pe.matmul(o_b[:, :], f_w2[:, c, :], gl[g % 2][c][:, :], start=(c == 0), stop=(c == HC - 1))
                    last.then_inc(f2_done, 1)
                pe.wait_ge(moments, B)
                pe.matmul(s_b[:, 0:B], prog.inv_p[:, :], mom[:, :, 0], start=True, stop=True).then_inc(mean_done, 1)
                pe.wait_ge(dev_step, 3)
                pe.wait_ge(mean_copied, 1)
                pe.matmul(s_b[:, B:2 * B], prog.inv_p[:, :], part_var[:, :], start=True, stop=True).then_inc(var_done, 1)
                for t in range(NT):
                    pe.wait_ge(c_normed, t // QT + 1)
                    pe.transpose(f_b[t // 4][:, (t % 4) * P:(t % 4 + 1) * P], cn[:, t, :], ident[:, :]).then_inc(c_trans, 1)

            @block.scalar
            def _(act):
                for g in range(G):
                    act.wait_ge(m_done, g + 1)
                    wait(act, f1_done, (g - 1) * HC)
                    wait(act, c_summed, g - 1)
                    act.activation(mT[g % 2][:, :], m_b[g % 2][:, :], ACT.Copy).then_inc(m_copied, 1)
                    for c in range(HC):
                        act.wait_ge(f1_done, g * HC + c + 1)
                        wait(act, f2_done, g - 1)
                        act.activation(gl[g % 2][c][:, :], f_b[c][:, :], ACT.Gelu, bias=f_b1[:, c:c + 1]).then_inc(gelu_done, 1)
                act.wait_ge(var_copied, 1)
                act.activation(std[:, :], var[:, :], ACT.Sqrt).then_inc(std_done, 1)

            @block.vector
            def _(dve):
                for g in range(G):
                    dve.wait_ge(f2_done, g + 1)
                    dve.wait_ge(m_copied, g + 1)
                    dve.scalar_tensor_tensor(cT[:, g * GS:(g + 1) * GS, :].rearrange("p a s -> p (a s)"), o_b[:, :], f_b2[:, 0:1],
                                             mT[g % 2][:, :], ALU.add, ALU.add).then_inc(c_summed, 1)
                    dve.wait_ge(c_summed, g + 1)
                    for b in range(g * GS, (g + 1) * GS):
                        dve.bn_stats(stats[:, b, :], cT[:, b, :]).then_inc(stat_done, 1)
                    for b in range(g * GS, (g + 1) * GS):
                        dve.wait_ge(stat_done, b + 1)
                        dve.bn_aggr(mom[:, b, :], stats[:, b, :]).then_inc(moments, 1)
                dve.wait_ge(mean_done, 1)
                dve.tensor_copy(mean[:, :], s_b[:, 0:B]).then_inc(mean_copied, 1)
                dve.wait_ge(mean_copied, 1)
                dve.tensor_tensor(dev[:, :], mom[:, :, 0], mean[:, :], ALU.subtract).then_inc(dev_step, 1)
                dve.wait_ge(dev_step, 1)
                dve.tensor_tensor(dev2[:, :], dev[:, :], dev[:, :], ALU.mult).then_inc(dev_step, 1)
                dve.wait_ge(dev_step, 2)
                dve.tensor_tensor(part_var[:, :], dev2[:, :], mom[:, :, 1], ALU.add).then_inc(dev_step, 1)
                dve.wait_ge(var_done, 1)
                dve.tensor_scalar(var[:, :], s_b[:, B:2 * B], EPS, None, ALU.add).then_inc(var_copied, 1)
                dve.wait_ge(std_done, 1)
                dve.reciprocal(rstd[:, :], std[:, :]).then_inc(rstd_done, 1)
                dve.wait_ge(rstd_done, 1)
                for b in range(B):
                    dve.tensor_scalar(cn[:, b * QT:(b + 1) * QT, :].rearrange("p q s -> p (q s)"), cT[:, b, :], mean[:, b:b + 1],
                                      rstd[:, b:b + 1], ALU.subtract, ALU.mult).then_inc(c_normed, 1)
                for q in range(4):
                    dve.wait_ge(c_trans, 4 * (q + 1))
                    xs = x[:, q * 4:(q + 1) * 4, :].rearrange("p t c -> p (t c)")
                    dve.tensor_tensor(xs, xs, f_b[q][:, :], ALU.add).then_inc(added, 1)


def program(nc, d):
    with ExitStack() as stack:
        prog = Program(nc)
        sb, _ = buffers(nc, stack, "g")
        prog.x = sb("x", [P, NT, P])
        prog.xn = sb("xn", [P, NT, XW])
        prog.xnT = sb("xnT", [P, NTOK])
        prog.ident = sb("ident", [P, P])
        prog.inv_p = sb("inv_p", [P, P])
        prog.ones_b = sb("ones_b", [P, P], BF16)
        prog.tri = sb("tri", [P, P], BF16)
        prog.logits = sb("logits", [P, NT, E_N])
        prog.gate_w = sb("gate_w", [P, E_N])
        prog.gate_b = sb("gate_b", [P, E_N])
        prog.route_consts = sb("route_consts", [P, R_END])
        x_loads = [(prog.x[:, q * 4:q * 4 + 4, :], d["x"].rearrange("(t p) c -> p t c", p=P)[:, q * 4:q * 4 + 4, :]) for q in range(4)]
        constants = ((prog.ident[:, :], d["c_ident"]), (prog.route_consts[:, :], d["c_route"]), (prog.tri[:, :], d["c_tri"].bitcast(BF16)))
        gate_loads = ((prog.gate_w[:, :], d["gate_wT"]), (prog.gate_b[:, :], d["gate_b"].to_broadcast([P, E_N])))
        with ExitStack() as held:
            weights, loads = attention_weights(prog, held, d)
            prog.phase(norm_phase, "n1", constants + gate_loads + loads, x_loads)
            prog.phase(attention_phase, d, weights)
        prog.phase(norm_phase, "n2", (), (), True)
        prog.phase(experts_phase, d, "f1")
        with ExitStack() as held:
            weights, loads = mamba_weights(prog, held, d)
            prog.phase(norm_phase, "n3", loads)
            prog.phase(mamba_phase, d, weights)
        prog.phase(norm_phase, "n4", (), (), True)
        prog.phase(experts_phase, d, "f2", d["out"])


def layout(inputs):
    import numpy as np

    def a(name):
        return np.asarray(inputs[name])

    out = {"x": a("L0_attn_a_x").reshape(NTOK, P)}
    by_head_last = np.arange(P).reshape(HEADS, HD).T.reshape(P)
    out["Wq"] = np.ascontiguousarray(a("L0_attn_a_Wq")[:, by_head_last])
    out["WkT"] = np.ascontiguousarray(a("L0_attn_a_Wk").T)
    out["WvT"] = np.ascontiguousarray(a("L0_attn_a_Wv").T)
    out["W_down"] = a("L0_attn_a_W_down_kv")
    out["W_up_k"] = np.ascontiguousarray(a("L0_attn_a_W_up_k")[:, by_head_last])
    out["W_up_v"] = a("L0_attn_a_W_up_v")
    out["Wo"] = a("L0_attn_a_Wo")
    out["gate_wT"] = np.ascontiguousarray(a("L0_ffn_gate_w").T)
    out["gate_b"] = a("L0_ffn_gate_b").reshape(1, E_N)
    w1 = a("L0_ffn_w1").transpose(0, 2, 1)
    w2 = a("L0_ffn_w2").transpose(0, 2, 1).reshape(E_N, HC, P, P).transpose(0, 2, 1, 3).reshape(E_N, P, HC * P)
    b1 = a("L0_ffn_b1").reshape(E_N, HC, P).transpose(0, 2, 1)
    b2 = np.broadcast_to(a("L0_ffn_b2").reshape(E_N, 1, P), (E_N, P, P))
    out["experts"] = np.ascontiguousarray(np.concatenate([w1, w2, b1, b2], axis=2).reshape(E_N * P, EW))

    def halves(m):
        return np.ascontiguousarray(m.reshape(DC, P, -1).transpose(1, 0, 2))

    out["in_projT"] = np.ascontiguousarray(a("L0_attn_b_in_proj_w").T)
    out["conv_w"] = halves(a("L0_attn_b_conv_w").reshape(DI, 4))
    out["conv_b"] = halves(a("L0_attn_b_conv_b")).reshape(P, DC)
    out["x_projT"] = halves(a("L0_attn_b_x_proj_w").T)
    out["dt_projT"] = np.ascontiguousarray(a("L0_attn_b_dt_proj_w").T)
    out["dt_b"] = halves(a("L0_attn_b_dt_proj_b")).reshape(P, DC)
    out["A_log"] = halves(a("L0_attn_b_A_log"))
    out["D"] = halves(a("L0_attn_b_D")).reshape(P, DC)
    out["out_projT"] = halves(a("L0_attn_b_out_proj_w").T)
    out["ffn_w1T"] = np.ascontiguousarray(a("L0_attn_b_ffn_w1").T)
    out["ffn_b1"] = np.ascontiguousarray(a("L0_attn_b_ffn_b1").reshape(HC, P).T)
    out["ffn_w2T"] = np.ascontiguousarray(a("L0_attn_b_ffn_w2").T.reshape(HC, P, P).transpose(1, 0, 2))
    out["ffn_b2"] = a("L0_attn_b_ffn_b2").reshape(P, 1)
    pick = (np.arange(96)[:, None] % 32 == np.arange(32)[None, :])[:, :, None]
    out["c_pick"] = np.ascontiguousarray(np.broadcast_to(pick, (96, 32, P))).astype(np.uint16) * np.uint16(BF16_ONE)
    p, s = np.arange(P), np.arange(S)
    q = s.reshape(QT, P)
    distance = np.abs(q.T[:, :, None].astype(np.float32) - s[None, None, :].astype(np.float32))
    out["c_decay"] = np.exp(np.float32(-0.01 * 0.01) * distance).astype(np.float32)
    out["c_ident"] = np.eye(P, dtype=np.float32)
    out["c_tri"] = (p[:, None] < p[None, :]).astype(np.uint16) * np.uint16(BF16_ONE)
    route = np.zeros((P, R_END), np.float32)
    route[:, R_LESS:R_LESS + E_N] = np.arange(E_N) - E_N
    route[:, R_THRESH:R_THRESH + NT] = np.arange(NT) * P
    route[:, R_TILE:R_TILE + SLOT_TILES] = np.arange(SLOT_TILES)
    route[:, R_ONES:R_ONES + NT] = 1.0
    route[:, R_TOKEN:R_TOKEN + NT] = np.arange(NT) * P + p[:, None]
    route[:, R_SPARE:R_SPARE + SLOT_TILES] = NTOK + np.arange(SLOT_TILES) * P + p[:, None]
    out["c_route"] = route
    return out


def scratch(nc, d):
    for tag in ("f1", "f2"):
        d["sorted_x_" + tag] = nc.dram_tensor("sorted_x_" + tag, (SLOT_TILES * P, XW), F32, kind="Internal").ap()
    d["y_tok"] = nc.dram_tensor("y_tok", (NTOK + SLOT_TILES * P, P), F32, kind="Internal").ap()
    d["parts"] = nc.dram_tensor("parts", (2, B, 3 * P, S), BF16, kind="Internal").ap()
    return d


def kernel(**inputs):
    import concourse.bacc as bacc
    from concourse.bass_utils import run_bass_kernel_spmd

    nc = bacc.Bacc("TRN2", target_bir_lowering=False, num_devices=1)
    arrays = layout(inputs)
    d = {name: nc.dram_tensor(name, a.shape, mybir.dt.from_np(a.dtype), kind="ExternalInput").ap() for name, a in arrays.items()}
    d["out"] = nc.dram_tensor("out", (NTOK + SLOT_TILES * P, P), F32, kind="ExternalOutput").ap()
    program(nc, scratch(nc, d))
    result = run_bass_kernel_spmd(nc, [arrays], core_ids=[0])
    return result.results[0]["out"][0:NTOK].reshape(B, S, P)
```
